# Optimizing a Trainium2 kernel written in Bass

```python
import numpy as np
import jax
import jax.numpy as jnp

def _softmax(x, axis=-1):
    return jax.nn.softmax(x, axis=axis)

def _gelu(x):
    return jax.nn.gelu(x, approximate=True)

def _silu(x):
    return jax.nn.silu(x)

def _sigmoid(x):
    return jax.nn.sigmoid(x)

def _layernorm(x, axis=-1, eps=1e-05):
    m = jnp.mean(x, axis=axis, keepdims=True)
    v = jnp.var(x, axis=axis, keepdims=True)
    return (x - m) / jnp.sqrt(v + eps)

def _scatter_add(tgt, idx, src, axis=0):
    return tgt.at[idx].add(src)

def _segment_sum(src, seg, n):
    return jax.ops.segment_sum(src, seg, n)
kernel_name = 'mk_adaln_d1_jaxref_r8_b30915'

def setup_inputs(seed: int=0):
    np.random.seed(seed)
    _w = jnp.asarray

    def _L0_attn_setup():
        import jax, jax.numpy as jnp
        import numpy as np
        HIDDEN = 256
        N_HEADS = 16
        N_KV = 4
        HEAD_DIM = 128
        SEQ = 256
        BATCH = 2
        THETA = 10000.0

        def rotate_half(x):
            half = x.shape[-1] // 2
            x1, x2 = (x[..., :half], x[..., half:])
            return jnp.concatenate((-x2, x1), axis=-1)

        def rope_cos_sin(seq_len, dim, theta, dtype):
            inv_freq = 1.0 / theta ** (jnp.arange(0, dim, 2, dtype=jnp.float32) / dim)
            t = jnp.arange(seq_len, dtype=jnp.float32)
            freqs = jnp.einsum('i,j->ij', t, inv_freq)
            emb = jnp.concatenate((freqs, freqs), axis=-1)
            return (jnp.cos(emb).astype(dtype), jnp.sin(emb).astype(dtype))
        key = jax.random.key(seed)
        kx, kq, kk, kv, ko = jax.random.split(key, 5)
        s = 0.02
        return {'x': jax.random.normal(kx, (BATCH, SEQ, HIDDEN), dtype=jnp.float32), 'Wq': jax.random.normal(kq, (HIDDEN, N_HEADS * HEAD_DIM), dtype=jnp.float32) * s, 'Wk': jax.random.normal(kk, (HIDDEN, N_KV * HEAD_DIM), dtype=jnp.float32) * s, 'Wv': jax.random.normal(kv, (HIDDEN, N_KV * HEAD_DIM), dtype=jnp.float32) * s, 'Wo': jax.random.normal(ko, (N_HEADS * HEAD_DIM, HIDDEN), dtype=jnp.float32) * s}
    _L0_attn_in = _L0_attn_setup()

    def _L0_ffn_setup():
        import jax, jax.numpy as jnp
        import numpy as np
        TOP_K = 4

        def _silu_and_mul(gu):
            g, u = jnp.split(gu, 2, axis=-1)
            return jax.nn.silu(g) * u
        key = jax.random.key(seed)
        ks = jax.random.split(key, 7)
        H, E, I, Is = (256, 16, 176, 704)
        s = 0.02
        return {'hidden_states': jax.random.normal(ks[0], (4, 128, H), dtype=jnp.float32), 'gate_w': jax.random.normal(ks[1], (E, H), dtype=jnp.float32) * s, 'sgate_w': jax.random.normal(ks[2], (1, H), dtype=jnp.float32) * s, 'w13': jax.random.normal(ks[3], (E, 2 * I, H), dtype=jnp.float32) * s, 'w2': jax.random.normal(ks[4], (E, H, I), dtype=jnp.float32) * s, 'shared_gate_up_w': jax.random.normal(ks[5], (2 * Is, H), dtype=jnp.float32) * s, 'shared_down_w': jax.random.normal(ks[6], (H, Is), dtype=jnp.float32) * s}
    _L0_ffn_in = _L0_ffn_setup()
    _L0_c = _w((lambda *s: np.random.randn(*s).astype(np.float32) * 0.05)(4, 256))
    _L0_wmod = _w((lambda *s: np.random.randn(*s).astype(np.float32) * 0.05)(256, 6 * 256) * 256 ** (-0.5))
    _d = {'L0_attn_x': _L0_attn_in['x'], 'L0_attn_Wq': _L0_attn_in['Wq'], 'L0_attn_Wk': _L0_attn_in['Wk'], 'L0_attn_Wv': _L0_attn_in['Wv'], 'L0_attn_Wo': _L0_attn_in['Wo'], 'L0_ffn_gate_w': _L0_ffn_in['gate_w'], 'L0_ffn_sgate_w': _L0_ffn_in['sgate_w'], 'L0_ffn_w13': _L0_ffn_in['w13'], 'L0_ffn_w2': _L0_ffn_in['w2'], 'L0_ffn_shared_gate_up_w': _L0_ffn_in['shared_gate_up_w'], 'L0_ffn_shared_down_w': _L0_ffn_in['shared_down_w'], 'L0_c': _L0_c, 'L0_wmod': _L0_wmod}
    _x0 = _d['L0_attn_x']
    _d['L0_attn_x'] = jax.random.normal(jax.random.fold_in(jax.random.key(seed), 1), (4, 256, 256), dtype=_x0.dtype)
    del _x0
    return _d

def reference(L0_attn_x, L0_attn_Wq, L0_attn_Wk, L0_attn_Wv, L0_attn_Wo, L0_ffn_gate_w, L0_ffn_sgate_w, L0_ffn_w13, L0_ffn_w2, L0_ffn_shared_gate_up_w, L0_ffn_shared_down_w, L0_c, L0_wmod):

    def _L0_attn_ref(x, Wq, Wk, Wv, Wo):
        import jax, jax.numpy as jnp
        import numpy as np
        HIDDEN = 256
        N_HEADS = 16
        N_KV = 4
        HEAD_DIM = 128
        SEQ = 256
        BATCH = 2
        THETA = 10000.0

        def rotate_half(x):
            half = x.shape[-1] // 2
            x1, x2 = (x[..., :half], x[..., half:])
            return jnp.concatenate((-x2, x1), axis=-1)

        def rope_cos_sin(seq_len, dim, theta, dtype):
            inv_freq = 1.0 / theta ** (jnp.arange(0, dim, 2, dtype=jnp.float32) / dim)
            t = jnp.arange(seq_len, dtype=jnp.float32)
            freqs = jnp.einsum('i,j->ij', t, inv_freq)
            emb = jnp.concatenate((freqs, freqs), axis=-1)
            return (jnp.cos(emb).astype(dtype), jnp.sin(emb).astype(dtype))
        B, S, _ = x.shape
        q = (x @ Wq).reshape(B, S, N_HEADS, HEAD_DIM)
        k = (x @ Wk).reshape(B, S, N_KV, HEAD_DIM)
        v = (x @ Wv).reshape(B, S, N_KV, HEAD_DIM)
        cos, sin = rope_cos_sin(S, HEAD_DIM, THETA, x.dtype)
        cos = cos[None, :, None, :]
        sin = sin[None, :, None, :]
        q = q * cos + rotate_half(q) * sin
        k = k * cos + rotate_half(k) * sin
        repeat = N_HEADS // N_KV
        k = jnp.repeat(k, repeat, axis=2)
        v = jnp.repeat(v, repeat, axis=2)
        q = q.transpose(0, 2, 1, 3)
        k = k.transpose(0, 2, 1, 3)
        v = v.transpose(0, 2, 1, 3)
        scale = HEAD_DIM ** (-0.5)
        scores = jnp.einsum('bhqd,bhkd->bhqk', q, k) * scale
        causal = jnp.triu(jnp.full((S, S), -jnp.inf, dtype=scores.dtype), k=1)
        scores = scores + causal
        probs = jax.nn.softmax(scores, axis=-1)
        out = jnp.einsum('bhqk,bhkd->bhqd', probs, v)
        out = out.transpose(0, 2, 1, 3).reshape(B, S, N_HEADS * HEAD_DIM)
        return out @ Wo

    def _L0_ffn_ref(hidden_states, gate_w, sgate_w, w13, w2, shared_gate_up_w, shared_down_w):
        import jax, jax.numpy as jnp
        import numpy as np
        TOP_K = 4

        def _silu_and_mul(gu):
            g, u = jnp.split(gu, 2, axis=-1)
            return jax.nn.silu(g) * u
        B, S, H = hidden_states.shape
        x = hidden_states.reshape(-1, H)
        E = gate_w.shape[0]
        shared = _silu_and_mul(x @ shared_gate_up_w.T) @ shared_down_w.T
        shared = shared * jax.nn.sigmoid(x @ sgate_w.T)
        router_logits = x @ gate_w.T
        routing_weights = jax.nn.softmax(router_logits.astype(jnp.float32), axis=-1)
        topk_w, topk_ids = jax.lax.top_k(routing_weights, TOP_K)

        def body(acc, ew):
            w13_e, w2_e, e = ew
            coef = jnp.sum(jnp.where(topk_ids == e, topk_w, 0.0), axis=-1)
            h = _silu_and_mul(x @ w13_e.T)
            acc = acc + (h @ w2_e.T).astype(jnp.float32) * coef[:, None]
            return (acc, None)
        init = jnp.zeros((x.shape[0], H), dtype=jnp.float32)
        sparse_out, _ = jax.lax.scan(body, init, (w13, w2, jnp.arange(E)))
        out = shared + sparse_out.astype(x.dtype)
        return out.reshape(B, S, H)
    x = L0_attn_x
    mod = (_silu(L0_c) @ L0_wmod).reshape(L0_c.shape[0], 6, 1, -1)
    sa, ca, ga, sb, cb, gb = (mod[:, 0], mod[:, 1], mod[:, 2], mod[:, 3], mod[:, 4], mod[:, 5])
    ga = (2 * (ga >= 0) - 1) * jnp.maximum(jnp.abs(ga), 0.25)
    gb = (2 * (gb >= 0) - 1) * jnp.maximum(jnp.abs(gb), 0.25)
    h = _layernorm(x, axis=-1) * (1 + ca) + sa
    x = x + ga * _L0_attn_ref(h, L0_attn_Wq, L0_attn_Wk, L0_attn_Wv, L0_attn_Wo)
    h = _layernorm(x, axis=-1) * (1 + cb) + sb
    x = x + gb * _L0_ffn_ref(h, L0_ffn_gate_w, L0_ffn_sgate_w, L0_ffn_w13, L0_ffn_w2, L0_ffn_shared_gate_up_w, L0_ffn_shared_down_w)
    return x

_drawn_inputs = setup_inputs


def setup_inputs(seed=0):
    import zlib

    import numpy as np

    out = dict(_drawn_inputs(seed))
    spreads = {}
    factors = {'L0_attn_Wq': 8.0,
     'L0_attn_Wk': 8.0,
     'L0_attn_Wv': 5.137,
     'L0_attn_Wo': 5.072,
     'L0_ffn_gate_w': 8.0,
     'L0_ffn_sgate_w': 8.0,
     'L0_ffn_w13': 8.0,
     'L0_ffn_w2': 8.0,
     'L0_ffn_shared_gate_up_w': 8.0,
     'L0_ffn_shared_down_w': 8.0,
     'L0_c': 4.967,
     'L0_wmod': 4.958}
    for name, (base, spread) in spreads.items():
        noise = np.random.default_rng([zlib.crc32(name.encode()), seed]).standard_normal(out[name].shape)
        drawn = base * np.exp(spread * noise) if base else spread * noise
        out[name] = jnp.asarray(drawn.astype(out[name].dtype))
    for name, factor in factors.items():
        out[name] = (out[name] * factor).astype(out[name].dtype)
    return out
```

```python
from contextlib import ExitStack

import concourse.bass as bass
from concourse import mybir

F32 = mybir.dt.float32
F32R = mybir.dt.float32r
BF16 = mybir.dt.bfloat16
ACT = mybir.ActivationFunctionType
ALU = mybir.AluOpType
AX_X = mybir.AxisListType.X

P = 128
BATCH, SEQ, HID = 4, 256, 256
KC = HID // P
NT = SEQ // P
HEADS, KV, HD = 16, 4, 128
UNITS = HEADS // 2
EXPERTS, INNER, SHARED, TOP_K = 16, 176, 704, 4
CHUNKS = -(-(EXPERTS * INNER + SHARED) // P)
GATES = EXPERTS + 1
GW = 32
EPS = 1e-5
MASKED = -3.0e38
SENTINEL = -5.0
HALF = BATCH * SEQ // 2
RAW = 4
SPLITS = 10
LOOKAHEAD = 3


def build(nc, x_d, wq_d, wk_d, wv_d, wo_d, gate_d, up_d, down_d, c_d, wmod_d,
          cos_d, sin_d, ident_d, causal_d, select_d, out_d):
    with ExitStack() as ctx:
        def sb(name, shape, dt):
            return ctx.enter_context(nc.sbuf_tensor(name, shape, dt))

        def sem(name):
            return ctx.enter_context(nc.semaphore(name))

        wq = sb("wq", [P, 2, KC, HEADS * HD], F32R)
        wk = sb("wk", [P, 2, KC, KV * HD], F32R)
        wv = sb("wv", [P, 2, KC, KV * HD], F32R)
        wo = sb("wo", [P, 2, HEADS, HID], F32R)
        hT = sb("hT", [P, 2, KC, BATCH * SEQ], F32R)
        xs = sb("xs", [P, BATCH, NT, HID], F32)
        gates = sb("gates", [P, BATCH, 2, HID], F32)
        raw = sb("raw", [P, RAW, 1024], F32)
        h_stat = sb("h_stat", [P, 2, KC, SEQ], F32R)
        v = sb("v", [P, 2, NT, KV * HD], F32R)
        qT = sb("qT", [P, 2, 2, 2, SEQ], F32R)
        kT = sb("kT", [P, 2, 2, SEQ], F32R)
        pT = sb("pT", [P, 2, 2 * SEQ + 2 * P], F32R)
        oT = sb("oT", [P, 2, 2, SEQ], F32R)
        work = sb("work", [P, 3584], F32)
        prob = work[:, 0:1536].rearrange("p (r n) -> p r n", r=2)
        rot = work[:, 1536:2560].rearrange("p (r h n) -> p r h n", r=2, h=2)
        qcos = work[:, 2560:3584].rearrange("p (r h n) -> p r h n", r=2, h=2)
        wmod = work[:, 0:KC * 6 * HID].rearrange("p (c n) -> p c n", c=KC)
        kwork = sb("kwork", [P, 1024], F32)
        krot = kwork[:, 0:256]
        kcos = kwork[:, 256:512]
        c_wide = kwork[:, :].rearrange("p (c b n) -> p c b n", c=KC, b=BATCH)
        z = sb("z", [P, NT, HID], F32)
        hbuf = sb("hbuf", [P, KC, SEQ], F32)
        ybuf = sb("ybuf", [P, NT, HID], F32)
        cosT = sb("cosT", [P, SEQ], F32)
        sinT = sb("sinT", [P, SEQ], F32)
        ident = sb("ident", [P, P], F32)
        ident_bf = sb("ident_bf", [P, P], BF16)
        causal = sb("causal", [P, P], BF16)
        select = sb("select", [3 * GW, CHUNKS * P], BF16)
        coefT = sb("coefT", [3 * GW, BATCH * SEQ], BF16)
        gw = sb("gw", [P, 2, KC, GW], F32R)
        gw_raw = sb("gw_raw", [P, KC, GW], F32)
        cT = sb("cT", [P, KC, BATCH], F32)
        ce = sb("ce", [P, 3, KC, BATCH], F32)
        modc = sb("modc", [P, 4, KC, BATCH], F32)
        stats = sb("stats", [P, NT, 6], F32)
        mv = sb("mv", [P, NT, 2], F32)
        ve = sb("ve", [P, NT], F32)
        neg_half = sb("neg_half", [P, NT], F32)
        rstd = sb("rstd", [P, NT], F32)
        nmax = sb("nmax", [P, 2, 2, 2], F32)
        sums = sb("sums", [P, 2, 2, 2], F32)
        rsum = sb("rsum", [P, 2, 2, 3], F32)
        lt = sb("lt", [P, SEQ], F32)
        rmax = sb("rmax", [P, NT], F32)
        rexp = sb("rexp", [P, NT, EXPERTS], F32)
        rtot = sb("rtot", [P, 2, NT], F32)
        sg = sb("sg", [P, 2, NT, 1], F32)
        probs20 = sb("probs20", [P, NT, EXPERTS + 4], F32)
        top8 = sb("top8", [P, NT, 8], F32)
        left20 = sb("left20", [P, NT, EXPERTS + 4], F32)
        coef = sb("coef", [P, NT, GATES], F32)
        rest = sb("rest", [P, 2, NT, GATES], F32)
        piece = sb("piece", [P, 2, NT, GATES], BF16)
        pieces = sb("pieces", [P, NT, 3, GW], F32)

        flat = wq[:, 0, :, :].rearrange("p c n -> p (c n)")
        flat2 = wq[:, 1, :, :].rearrange("p c n -> p (c n)")
        w_gu = flat[:, 0:2048].rearrange("p (r s c g n) -> p r s c g n", r=2, s=2, c=KC, g=2)
        w_dn = flat[:, 2048:3072].rearrange("p (r s n) -> p r s n", r=2, s=2)
        actT = flat2[:, 0:2048].rearrange("p (r s n) -> p r s n", r=2, s=2)
        silu = work[:, 0:1024].rearrange("p (r n) -> p r n", r=2)
        prod = work[:, 1024:2048].rearrange("p (r n) -> p r n", r=2)
        scaled = work[:, 2048:3072].rearrange("p (r n) -> p r n", r=2)

        bank = [ctx.enter_context(nc.psum_tensor(f"bank{i}", [P, 512], F32)) for i in range(8)]
        q_ps = bank[0][:, :].rearrange("p (h n) -> p h n", h=2)
        misc = bank[1]
        s0_ps = bank[2][:, 0:256].rearrange("p (h n) -> p h n", h=2)
        s1_ps = bank[3][:, :].rearrange("p (h n) -> p h n", h=2)
        p0_ps = bank[4][:, :].rearrange("p (h n) -> p h n", h=2)
        p1_ps = bank[5][:, 0:256].rearrange("p (h n) -> p h n", h=2)
        o_ps = bank[6][:, :].rearrange("p (h n) -> p h n", h=2)
        y_ps = bank[7][:, :].rearrange("p (t n) -> p t n", t=NT)
        mod_ps = bank[2][:, 0:32].rearrange("p (j k b) -> p j k b", j=4, k=KC)
        gate_ps = [bank[4 + b] for b in range(BATCH)]
        y2_ps = [bank[4 + b][:, :].rearrange("p (t n) -> p t n", t=NT) for b in range(BATCH)]
        g_ps, u_ps, c_ps = bank[0], bank[2], bank[3]

        in_c, in_mod, in_x, in_rope, in_const, in_gw = (sem(n) for n in (
            "in_c", "in_mod", "in_x", "in_rope", "in_const", "in_gw"))
        raw_in = [sem(f"raw_in{i}") for i in range(RAW)]
        c_step, mod_cols, mod_rows, cols_out, rows_out, gates_step = (sem(n) for n in (
            "c_step", "mod_cols", "mod_rows", "cols_out", "rows_out", "gates_step"))
        consts, half_ok = sem("consts"), sem("half_ok")
        hi_split, lo_even, lo_odd, gw_split = (sem(n) for n in ("hi_split", "lo_even", "lo_odd", "gw_split"))
        ln_step, rstd_ok, z_ok, zT_ok, h_ok, h_hi, h_lo, h_stat_ok = (sem(n) for n in (
            "ln_step", "rstd_ok", "z_ok", "zT_ok", "h_ok", "h_hi", "h_lo", "h_stat_ok"))
        q_ok, q_rot, q_cos, q_sin, q_add, q_hi, q_lo = (sem(n) for n in (
            "q_ok", "q_rot", "q_cos", "q_sin", "q_add", "q_hi", "q_lo"))
        k_ok, k_rot, k_cos, k_sin, k_add, k_hi, k_lo = (sem(n) for n in (
            "k_ok", "k_rot", "k_cos", "k_sin", "k_add", "k_hi", "k_lo"))
        v_ok, v_hi, v_lo = (sem(n) for n in ("v_ok", "v_hi", "v_lo"))
        s_ok, max_ok, exp_ok, rsum_ok, norm_ok = (sem(n) for n in ("s_ok", "max_ok", "exp_ok", "rsum_ok", "norm_ok"))
        pT_ok, pT_hi, pT_lo, o_ok, o_hi, o_lo = (sem(n) for n in ("pT_ok", "pT_hi", "pT_lo", "o_ok", "o_hi", "o_lo"))
        d_ok, y_read, x1_ok = (sem(n) for n in ("d_ok", "y_read", "x1_ok"))
        lt_ok, lt_out, l_ok, rmax_ok, rexp_ok, r_step, pieces_ok, cT_ok, coefs_ok = (sem(n) for n in (
            "lt_ok", "lt_out", "l_ok", "rmax_ok", "rexp_ok", "r_step", "pieces_ok", "cT_ok", "coefs_ok"))
        w_in = [sem(f"w_in{i}") for i in range(2)]
        w_hi, w_lo, zeroed = (sem(n) for n in ("w_hi", "w_lo", "zeroed"))
        g_ok, u_ok, c_ok, silu_ok, prod_ok, scaled_ok, a_hi, a_lo, down_ok = (sem(n) for n in (
            "g_ok", "u_ok", "c_ok", "silu_ok", "prod_ok", "scaled_ok", "a_hi", "a_lo", "down_ok"))
        yg_ok, x2_ok, out_ok = (sem(n) for n in ("yg_ok", "x2_ok", "out_ok"))

        wq_v = wq_d.rearrange("(c p) n -> p c n", p=P)
        wk_v = wk_d.rearrange("(c p) n -> p c n", p=P)
        wv_v = wv_d.rearrange("(c p) n -> p c n", p=P)
        wo_v = wo_d.rearrange("(h p) n -> p h n", p=P)
        x_v = x_d.rearrange("b (t p) n -> p b t n", p=P)
        out_v = out_d.rearrange("b (t p) n -> p b t n", p=P)

        def piece_of(w, w_v, cols):
            return w_v[:, :, cols], w[:, :, :, cols], KC

        q4 = [piece_of(wq, wq_v, slice(g * 512, (g + 1) * 512)) for g in range(KV)]
        all_k = slice(0, KV * HD)
        splits = [piece_of(wk, wk_v, all_k), q4[0], piece_of(wv, wv_v, all_k), q4[1], q4[2], q4[3]]
        splits += [(wo_v[:, 4 * r:4 * r + 4, :], wo[:, :, 4 * r:4 * r + 4, :], 4) for r in range(4)]
        K_SPLIT, V_SPLIT = 0, 2
        Q_SPLIT = [1, 3, 4, 5]
        O_SPLIT = [6, 7, 8, 9]

        def raw_piece(i):
            return raw[:, i % RAW, :].rearrange("p (c n) -> p c n", c=splits[i][2])

        PASSES = ((1, 0), (0, 1), (0, 0))

        block = ctx.enter_context(nc.Block())

        @block.sync
        def _(sp):
            sp.dma_start(cT[:, :, :], c_d.rearrange("p (c b) -> p c b", c=KC)).then_inc(in_c, 16)
            sp.dma_start(wmod, wmod_d.rearrange("(c p) n -> p c n", p=P)).then_inc(in_mod, 16)
            sp.dma_start(xs[:, :, :, :], x_v).then_inc(in_x, 16)
            for i in range(2):
                sp.dma_start(raw_piece(i), splits[i][0]).then_inc(raw_in[i], 16)
            sp.dma_start(ident[:, :], ident_d).then_inc(in_const, 16)
            sp.dma_start(cosT[:, :], cos_d).then_inc(in_rope, 16)
            sp.dma_start(sinT[:, :], sin_d).then_inc(in_rope, 16)
            sp.dma_start(causal[:, :], causal_d).then_inc(in_const, 16)
            for i in range(2, RAW):
                sp.dma_start(raw_piece(i), splits[i][0]).then_inc(raw_in[i], 16)
            sp.dma_start(gw_raw[:, :, :], gate_d.rearrange("(c p) n -> p c n", p=P)).then_inc(in_gw, 16)
            sp.dma_start(select[:, :], select_d).then_inc(in_const, 16)
            for i in range(RAW, SPLITS):
                sp.wait_ge(hi_split, i - RAW + 1)
                if (i - RAW) % 2 == 0:
                    sp.wait_ge(lo_even, (i - RAW) // 2 + 1)
                else:
                    sp.wait_ge(lo_odd, (i - RAW) // 2 + 1)
                sp.dma_start(raw_piece(i), splits[i][0]).then_inc(raw_in[i % RAW], 16)

            def load_chunk(c, slot):
                sp.dma_start(raw[:, slot, 0:512], up_d[bass.ds(c, 1), :, :].rearrange("a p n -> p (a n)")).then_inc(w_in[slot], 16)
                sp.dma_start(raw[:, slot, 512:768], down_d[bass.ds(c, 1), :, :].rearrange("a p n -> p (a n)")).then_inc(w_in[slot], 16)

            sp.wait_ge(hi_split, SPLITS)
            sp.wait_ge(lo_even, SPLITS // 2)
            sp.wait_ge(lo_odd, SPLITS // 2)
            load_chunk(0, 0)
            load_chunk(1, 1)
            with sp.Fori(1, CHUNKS // 2) as i:
                for slot in range(2):
                    sp.wait_ge(w_hi, 2 * i - 1 + slot)
                    sp.wait_ge(w_lo, 2 * i - 1 + slot)
                    load_chunk(2 * i + slot, slot)
            for b in range(BATCH):
                sp.wait_ge(x2_ok, b + 1)
                sp.dma_start(out_v[:, b], xs[:, b]).then_inc(out_ok, 16)
            sp.wait_ge(out_ok, 16 * BATCH)

        @block.tensor
        def _(pe):
            def norm_transposes(l):
                pe.wait_ge(z_ok, l + 1)
                zT = misc[:, :].rearrange("p (c n) -> p c n", c=KC)
                for c in range(KC):
                    for t in range(NT):
                        last = nc.tensor.transpose(zT[:, c, t * P:(t + 1) * P], z[:, t, c * P:(c + 1) * P], ident[:, :])
                last.then_inc(zT_ok, 1)

            def project_q(b, p):
                u = UNITS * b + p
                if not (isinstance(b, int) and b == 0 and p == 0):
                    pe.wait_ge(q_cos, u)
                n = 0
                for j in range(2):
                    for c in range(KC):
                        for ws, xsel in PASSES:
                            mm = nc.tensor.matmul(q_ps[:, j, :], wq[:, ws, c, (2 * p + j) * HD:(2 * p + j + 1) * HD],
                                                  hT[:, xsel, c, bass.ds(b * SEQ, SEQ)],
                                                  start=(n == 0), stop=(n % (3 * KC) == 3 * KC - 1), skip_group_check=True)
                            n += 1
                mm.then_inc(q_ok, 1)

            def project_k(b, g):
                n = 0
                for c in range(KC):
                    for ws, xsel in PASSES:
                        mm = nc.tensor.matmul(misc[:, 0:SEQ], wk[:, ws, c, g * HD:(g + 1) * HD],
                                              hT[:, xsel, c, bass.ds(b * SEQ, SEQ)], start=(n == 0), stop=(n == 3 * KC - 1))
                        n += 1
                mm.then_inc(k_ok, 1)

            def project_v(b, t):
                if t == 0:
                    pe.wait_ge(h_stat_ok, b + 1)
                n = 0
                for c in range(KC):
                    for hs, ws in PASSES:
                        mm = nc.tensor.matmul(misc[:, :], h_stat[:, hs, c, t * P:(t + 1) * P], wv[:, ws, c, :],
                                              start=(n == 0), stop=(n == 3 * KC - 1))
                        n += 1
                mm.then_inc(v_ok, 1)

            def scores(b, p):
                u, g, r = UNITS * b + p, p // 2, p % 2
                pe.wait_ge(q_lo, u + 1)
                if p % 2 == 0:
                    pe.wait_ge(k_lo, KV * b + g + 1)
                if not (isinstance(b, int) and b == 0 and p == 0):
                    pe.wait_ge(exp_ok, u)
                for j in range(2):
                    nc.tensor.matmul(s0_ps[:, j, :], ident_bf[:, :], causal[:, :], start=(j == 0), stop=False, skip_group_check=True)
                    for qs, ks in PASSES:
                        nc.tensor.matmul(s0_ps[:, j, :], qT[:, r, qs, j, 0:P], kT[:, g % 2, ks, 0:P],
                                         start=False, stop=(qs + ks == 0), skip_group_check=True)
                for j in range(2):
                    for n, (qs, ks) in enumerate(PASSES):
                        nc.tensor.matmul(s1_ps[:, j, :], qT[:, r, qs, j, P:SEQ], kT[:, g % 2, ks, :],
                                         start=(j == 0 and n == 0), stop=False, skip_group_check=True)
                    mm = nc.tensor.matmul(s1_ps[:, j, P:SEQ], ident_bf[:, :], causal[:, :], start=False, stop=True, skip_group_check=True)
                mm.then_inc(s_ok, 1)

            def prob_transposes(b, p):
                u, r = UNITS * b + p, p % 2
                pe.wait_ge(norm_ok, u + 1)
                if not (isinstance(b, int) and b == 0 and p == 0):
                    pe.wait_ge(pT_lo, u)
                for j in range(2):
                    for n, dst in enumerate((p0_ps[:, j, 0:P], p0_ps[:, j, P:SEQ], p1_ps[:, j, :])):
                        at = (3 * j + n) * P
                        tr = nc.tensor.transpose(dst, prob[:, r, at:at + P], ident[:, :])
                tr.then_inc(pT_ok, 1)

            def times_v(b, p):
                u, g = UNITS * b + p, p // 2
                if p == 0:
                    pe.wait_ge(v_lo, NT * (b + 1))
                pe.wait_ge(pT_lo, u + 1)
                if not (isinstance(b, int) and b == 0 and p == 0):
                    pe.wait_ge(o_lo, u)
                cols = slice(g * HD, (g + 1) * HD)
                for n, (vs, ps) in enumerate(PASSES):
                    nc.tensor.matmul(o_ps[:, :, :], v[:, vs, 0, cols], pT[:, ps, 0:2 * SEQ], start=(n == 0), stop=False, skip_group_check=True)
                for n, (vs, ps) in enumerate(PASSES):
                    mm = nc.tensor.matmul(o_ps[:, :, P:SEQ], v[:, vs, 1, cols],
                                          pT[:, ps, 2 * SEQ:].rearrange("p (h n) -> p h n", h=2), start=False, stop=(n == 2), skip_group_check=True)
                mm.then_inc(o_ok, 1)

            def project_out(b, p):
                u = UNITS * b + p
                pe.wait_ge(o_lo, u + 1)
                if p == 0 and not (isinstance(b, int) and b == 0):
                    pe.wait_ge(y_read, b)
                if isinstance(b, int) and b == 0 and p % 2 == 0:
                    i = O_SPLIT[p // 2]
                    pe.wait_ge(hi_split, i + 1)
                    pe.wait_ge(lo_even if i % 2 == 0 else lo_odd, i // 2 + 1)
                for j in range(2):
                    for t in range(NT):
                        for n, (os, ws) in enumerate(PASSES):
                            mm = nc.tensor.matmul(y_ps[:, t, :], oT[:, os, j, t * P:(t + 1) * P], wo[:, ws, 2 * p + j, :],
                                                  start=(p == 0 and j == 0 and t == 0 and n == 0),
                                                  stop=(p == UNITS - 1 and j == 1 and n == 2), skip_group_check=True)
                mm.then_inc(d_ok, 1)

            def router_logits(b):
                pe.wait_ge(h_lo, BATCH + b + 1)
                n = 0
                for c in range(KC):
                    for ws, xsel in PASSES:
                        mm = nc.tensor.matmul(misc[0:GW, 0:SEQ], gw[:, ws, c, :], hT[:, xsel, c, bass.ds(b * SEQ, SEQ)],
                                              start=(n == 0), stop=(n == 3 * KC - 1))
                        n += 1
                mm.then_inc(lt_ok, 1)

            def logit_transposes(b):
                pe.wait_ge(lt_out, b + 1)
                for t in range(NT):
                    tr = nc.tensor.transpose(misc[:, t * P:(t + 1) * P], lt[:, t * P:(t + 1) * P], ident[:, :])
                tr.then_inc(l_ok, 1)

            def coef_transposes(b):
                pe.wait_ge(pieces_ok, b + 1)
                for t in range(NT):
                    tr = nc.tensor.transpose(misc[0:3 * GW, t * P:(t + 1) * P], pieces[:, t].rearrange("p a n -> p (a n)"), ident[:, :])
                tr.then_inc(cT_ok, 1)

            pe.wait_ge(in_mod, 16)
            pe.wait_ge(c_step, 4)
            for j, field in enumerate((0, 1, 3, 4)):
                for ko in range(KC):
                    at = field * HID + ko * P
                    for c in range(KC):
                        mm = nc.tensor.matmul(mod_ps[:, j, ko, :], wmod[:, c, at:at + P], ce[:, 2, c, :], start=(c == 0), stop=(c == KC - 1))
            mm.then_inc(mod_cols, 1)
            pe.wait_ge(c_step, 5)
            for b in range(BATCH):
                for j, field in enumerate((2, 5)):
                    for c in range(KC):
                        mm = nc.tensor.matmul(gate_ps[b][:, j * HID:(j + 1) * HID], c_wide[:, c, b, :],
                                              wmod[:, c, field * HID:(field + 1) * HID], start=(c == 0), stop=(c == KC - 1))
                mm.then_inc(mod_rows, 1)
            pe.wait_ge(in_const, 48)
            for l in range(BATCH):
                if l > 0:
                    pe.wait_ge(h_ok, l)
                norm_transposes(l)
            pe.wait_ge(consts, 2)
            pe.wait_ge(h_lo, BATCH)
            pe.wait_ge(hi_split, 2)
            pe.wait_ge(lo_even, 1)
            pe.wait_ge(lo_odd, 1)
            project_k(0, 0)
            pe.wait_ge(rows_out, 4)
            project_q(0, 0)
            project_q(0, 1)
            pe.wait_ge(hi_split, Q_SPLIT[1] + 1)
            pe.wait_ge(lo_odd, Q_SPLIT[1] // 2 + 1)
            pe.wait_ge(k_cos, 1)
            project_k(0, 1)
            project_q(0, 2)
            pe.wait_ge(cols_out, 1)
            scores(0, 0)

            def batch(b, first, last):
                for p in range(UNITS):
                    if p < UNITS - 1:
                        scores(b, p + 1)
                    elif not last:
                        scores(b + 1, 0)
                    prob_transposes(b, p)
                    if p == 0:
                        if first:
                            pe.wait_ge(hi_split, V_SPLIT + 1)
                            pe.wait_ge(lo_even, V_SPLIT // 2 + 1)
                        pe.wait_ge(k_cos, KV * b + 2)
                        if not first:
                            pe.wait_ge(coefs_ok, b)
                        project_v(b, 0)
                    ahead = p + LOOKAHEAD
                    if ahead < UNITS or not last:
                        if first and ahead < UNITS and ahead % 2 == 0:
                            i = Q_SPLIT[ahead // 2]
                            pe.wait_ge(hi_split, i + 1)
                            pe.wait_ge(lo_even if i % 2 == 0 else lo_odd, i // 2 + 1)
                        ab, ap = (b, ahead) if ahead < UNITS else (b + 1, ahead - UNITS)
                        if ap % 2 == 0:
                            if p == 1:
                                pe.wait_ge(v_lo, NT * b + 2)
                            elif first:
                                pe.wait_ge(k_cos, KV * b + 2 + p // 2)
                            else:
                                pe.wait_ge(*{3: (h_ok, BATCH + b), 5: (lt_out, b), 7: (rexp_ok, b)}[p])
                            project_k(ab, ap // 2)
                        project_q(ab, ap)
                    if p == 0:
                        pe.wait_ge(v_lo, NT * b + 1)
                        project_v(b, 1)
                    if p > 0:
                        project_out(b, p - 1)
                    elif not first:
                        project_out(b - 1, UNITS - 1)
                    times_v(b, p)
                    if not first:
                        if p == 2:
                            pe.wait_ge(k_cos, KV * b + 3)
                            norm_transposes(BATCH + b - 1)
                        if p == 4:
                            pe.wait_ge(k_cos, KV * b + 4)
                            router_logits(b - 1)
                        if p == 6:
                            pe.wait_ge(*((lt_out, b) if last else (k_cos, KV * b + 5)))
                            logit_transposes(b - 1)
                        if p == 7:
                            pe.wait_ge(*((rexp_ok, b) if last else (k_cos, KV * b + 6)))
                            coef_transposes(b - 1)

            batch(0, True, False)
            with pe.Fori(1, BATCH - 1) as b:
                batch(b, False, False)
            batch(BATCH - 1, False, True)
            b = BATCH - 1
            project_out(b, UNITS - 1)
            pe.wait_ge(coefs_ok, BATCH)
            norm_transposes(BATCH + b)
            pe.wait_ge(h_ok, 2 * BATCH)
            router_logits(b)
            pe.wait_ge(lt_out, BATCH)
            logit_transposes(b)
            pe.wait_ge(rexp_ok, BATCH)
            coef_transposes(b)

            def step(s, c, slot, half, first):
                toks = slice(half * HALF, (half + 1) * HALF)
                if half == 0:
                    pe.wait_ge(w_hi, c + 1)
                    pe.wait_ge(w_lo, c + 1)
                for i, (ps, used, ready) in enumerate(((g_ps, silu_ok, g_ok), (u_ps, prod_ok, u_ok))):
                    if not first:
                        pe.wait_ge(used, s)
                    n = 0
                    for kc in range(KC):
                        for ws, xsel in PASSES:
                            mm = nc.tensor.matmul(ps[:, :], w_gu[:, slot, ws, kc, i, :], hT[:, xsel, kc, toks],
                                                  start=(n == 0), stop=(n == 3 * KC - 1))
                            n += 1
                    mm.then_inc(ready, 1)
                if not first:
                    pe.wait_ge(scaled_ok, s)
                nc.tensor.matmul(c_ps[:, :], select[:, bass.ds(c * P, P)], coefT[:, toks], start=True, stop=True).then_inc(c_ok, 1)

            def down(s, slot, half):
                pe.wait_ge(a_lo, s + 1)
                for t in range(4):
                    for n, (as_, ws) in enumerate(PASSES):
                        mm = nc.tensor.matmul(y2_ps[2 * half + t // 2][:, t % 2, :], actT[:, half, as_, t * P:(t + 1) * P],
                                              w_dn[:, slot, ws, :], start=False, stop=False, skip_group_check=True)
                mm.then_inc(down_ok, 1)

            def chunk_pair(i, first):
                for slot in range(2):
                    for half in range(2):
                        at = 2 * slot + half
                        step(4 * i + at, 2 * i + slot, slot, half, first and at == 0)
                        if at > 0:
                            down(4 * i + at - 1, (at - 1) // 2, (at - 1) % 2)
                        elif not first:
                            down(4 * i - 1, 1, 1)

            pe.wait_ge(coefs_ok, 1 + BATCH)
            pe.wait_ge(zeroed, 1)
            chunk_pair(0, True)
            with pe.Fori(1, CHUNKS // 2) as i:
                chunk_pair(i, False)
            down(2 * CHUNKS - 1, 1, 1)

        @block.scalar
        def _(act):
            nc.scalar.preload_act_table(ACT.Exp)

            def h_split(l, b):
                act.wait_ge(h_ok, l + 1)
                nc.scalar.activation(hT[:, 0, :, bass.ds(b * SEQ, SEQ)], hbuf[:, :, :], ACT.Copy).then_inc(h_hi, 1)

            def split_hi(i):
                act.wait_ge(raw_in[i % RAW], 16 * (i // RAW + 1))
                nc.scalar.activation(splits[i][1][:, 0], raw_piece(i), ACT.Copy).then_inc(hi_split, 1)

            def rotate_q(b, p):
                u, r = UNITS * b + p, p % 2
                act.wait_ge(q_ok, u + 1)
                if not (isinstance(b, int) and b == 0 and p < 2):
                    act.wait_ge(q_lo, u - 1)
                nc.scalar.activation(rot[0:64, r], q_ps[64:128, :, :], ACT.Copy)
                nc.scalar.activation(rot[64:128, r], q_ps[0:64, :, :], ACT.Copy).then_inc(q_rot, 1)

            def rotate_k(b, g):
                n = KV * b + g
                act.wait_ge(k_ok, n + 1)
                if not (isinstance(b, int) and b == 0 and g == 0):
                    act.wait_ge(k_lo, n)
                nc.scalar.activation(krot[0:64, :], misc[64:128, 0:SEQ], ACT.Copy)
                nc.scalar.activation(krot[64:128, :], misc[0:64, 0:SEQ], ACT.Copy).then_inc(k_rot, 1)

            def exps(b, p):
                u, r = UNITS * b + p, p % 2
                act.wait_ge(max_ok, u + 1)
                if not (isinstance(b, int) and b == 0 and p < 2):
                    act.wait_ge(pT_ok, u - 1)
                    act.wait_ge(rsum_ok, u - 1)
                for j in range(2):
                    at = 3 * j * P
                    nc.scalar.activation(prob[:, r, at:at + P], s0_ps[:, j, :], ACT.Exp, bias=nmax[:, r, 0, j:j + 1],
                                         accum_out=sums[:, r, j, 0:1])
                    e = nc.scalar.activation(prob[:, r, at + P:at + 3 * P], s1_ps[:, j, :], ACT.Exp, bias=nmax[:, r, 1, j:j + 1],
                                             accum_out=sums[:, r, j, 1:2])
                e.then_inc(exp_ok, 1)

            def pT_split(b, p):
                u = UNITS * b + p
                act.wait_ge(pT_ok, u + 1)
                if not (isinstance(b, int) and b == 0 and p == 0):
                    act.wait_ge(o_ok, u)
                nc.scalar.activation(pT[:, 0, 0:2 * SEQ], bank[4][:, :], ACT.Copy).then_inc(pT_hi, 1)
                nc.scalar.activation(pT[:, 0, 2 * SEQ:], bank[5][:, 0:2 * P], ACT.Copy).then_inc(pT_hi, 1)

            def o_split(b, p):
                u = UNITS * b + p
                act.wait_ge(o_ok, u + 1)
                if not (isinstance(b, int) and b == 0 and p == 0):
                    act.wait_ge(d_ok, u)
                nc.scalar.activation(oT[:, 0], o_ps[:, :, :], ACT.Copy).then_inc(o_hi, 1)

            def v_split(b, t):
                act.wait_ge(v_ok, NT * b + t + 1)
                if t == 0 and not (isinstance(b, int) and b == 0):
                    act.wait_ge(o_ok, UNITS * b)
                nc.scalar.activation(v[:, 0, t, :], misc[:, :], ACT.Copy).then_inc(v_hi, 1)

            def router_exps(b):
                act.wait_ge(rmax_ok, b + 1)
                lg = misc[:, 0:NT * P].rearrange("p (t n) -> p t n", t=NT)
                for t in range(NT):
                    nc.scalar.activation(rexp[:, t, :], lg[:, t, 0:EXPERTS], ACT.Exp, bias=rmax[:, t:t + 1], accum_out=rtot[:, 0, t:t + 1])
                nc.scalar.activation(sg[:, 0], lg[:, :, EXPERTS:GATES], ACT.Exp, scale=-1.0).then_inc(rexp_ok, 1)

            act.wait_ge(in_c, 16)
            nc.scalar.activation(ce[:, 0], cT[:, :, :], ACT.Exp, scale=-1.0).then_inc(c_step, 1)
            split_hi(0)
            split_hi(1)
            for b in range(BATCH):
                act.wait_ge(mod_rows, b + 1)
                nc.scalar.activation(gates[:, b].rearrange("p j n -> p (j n)"), gate_ps[b][:, :], ACT.Copy).then_inc(rows_out, 1)
                h_split(b, b)
                if b + 2 < 6:
                    split_hi(b + 2)
            rotate_k(0, 0)
            rotate_q(0, 0)
            rotate_q(0, 1)
            rotate_k(0, 1)
            rotate_q(0, 2)
            exps(0, 0)

            def batch(b, first, last):
                for p in range(UNITS):
                    if not first and p == 3:
                        h_split(BATCH + b - 1, b - 1)
                    if not first and p == 7:
                        router_exps(b - 1)
                    pT_split(b, p)
                    if p == 0:
                        v_split(b, 0)
                    if p < UNITS - 1:
                        exps(b, p + 1)
                    elif not last:
                        exps(b + 1, 0)
                    ahead = p + LOOKAHEAD
                    if ahead < UNITS or not last:
                        ab, ap = (b, ahead) if ahead < UNITS else (b + 1, ahead - UNITS)
                        if ap % 2 == 0:
                            rotate_k(ab, ap // 2)
                        rotate_q(ab, ap)
                    if p == 0:
                        v_split(b, 1)
                    if first and p < 4:
                        split_hi(6 + p)
                    o_split(b, p)

            batch(0, True, False)
            with act.Fori(1, BATCH - 1) as b:
                batch(b, False, False)
            batch(BATCH - 1, False, True)
            h_split(2 * BATCH - 1, BATCH - 1)
            router_exps(BATCH - 1)

            def weights_hi(i, slot, first):
                act.wait_ge(w_in[slot], 32 * i + 32)
                if first:
                    act.wait_ge(q_ok, UNITS * BATCH)
                else:
                    act.wait_ge(down_ok, 4 * i - 2 + 2 * slot)
                nc.scalar.activation(w_gu[:, slot, 0].rearrange("p c g n -> p (c g n)"), raw[:, slot, 0:512], ACT.Copy)
                nc.scalar.activation(w_dn[:, slot, 0], raw[:, slot, 512:768], ACT.Copy).then_inc(w_hi, 1)

            def act_step(s, half, at, first):
                act.wait_ge(g_ok, s + 1)
                if not (first and at < 2):
                    act.wait_ge(prod_ok, s - 1)
                nc.scalar.activation(silu[:, half, :], g_ps[:, :], ACT.Silu).then_inc(silu_ok, 1)
                act.wait_ge(scaled_ok, s + 1)
                if not (first and at < 2):
                    act.wait_ge(down_ok, s - 1)
                nc.scalar.activation(actT[:, half, 0, :], scaled[:, half, :], ACT.Copy).then_inc(a_hi, 1)

            def chunk_pair(i, first, last):
                for slot in range(2):
                    for half in range(2):
                        at = 2 * slot + half
                        act_step(4 * i + at, half, at, first)
                        if at == 2 and not last:
                            weights_hi(i + 1, 0, False)
                        if at == 0 and not first:
                            weights_hi(i, 1, False)

            nc.scalar.preload_act_table(ACT.Silu)
            weights_hi(0, 0, True)
            weights_hi(0, 1, True)
            chunk_pair(0, True, False)
            with act.Fori(1, CHUNKS // 2 - 1) as i:
                chunk_pair(i, False, False)
            chunk_pair(CHUNKS // 2 - 1, False, True)

        @block.vector
        def _(dve):
            def norm_stats(l, b):
                for t in range(NT):
                    i = nc.vector.bn_stats(stats[:, t, :], xs[:, bass.ds(b, 1), t, :].rearrange("p a n -> p (a n)"))
                i.then_inc(ln_step, 1)
                dve.wait_ge(ln_step, 3 * l + 1)
                nc.vector.memset(ve[:, :], EPS)
                for t in range(NT):
                    i = nc.vector.bn_aggr(mv[:, t, :], stats[:, t, :])
                i.then_inc(ln_step, 1)
                dve.wait_ge(ln_step, 3 * l + 2)
                nc.vector.tensor_tensor(ve[:, :], mv[:, :, 1], ve[:, :], ALU.add).then_inc(ln_step, 1)

            def normalize(l, b):
                dve.wait_ge(rstd_ok, l + 1)
                if not (isinstance(l, int) and l == 0):
                    dve.wait_ge(zT_ok, l)
                for t in range(NT):
                    i = nc.vector.tensor_scalar(z[:, t, :], xs[:, bass.ds(b, 1), t, :].rearrange("p a n -> p (a n)"),
                                                mv[:, t, 0:1], rstd[:, t:t + 1], ALU.subtract, ALU.mult)
                i.then_inc(z_ok, 1)

            def modulate(l, b, shift):
                dve.wait_ge(zT_ok, l + 1)
                if not (isinstance(l, int) and l == 0):
                    dve.wait_ge(h_lo, l)
                zT = misc[:, :].rearrange("p (c n) -> p c n", c=KC)
                for c in range(KC):
                    i = nc.vector.tensor_scalar(hbuf[:, c, :], zT[:, c, :], modc[:, shift + 1, c, bass.ds(b, 1)],
                                                modc[:, shift, c, bass.ds(b, 1)], ALU.mult, ALU.add)
                i.then_inc(h_ok, 1)

            def h_rest(l, b):
                dve.wait_ge(h_hi, l + 1)
                at = bass.ds(b * SEQ, SEQ)
                nc.vector.tensor_tensor(hT[:, 1, :, at], hbuf[:, :, :], hT[:, 0, :, at].bitcast(F32), ALU.subtract).then_inc(h_lo, 1)

            def split_lo(i):
                dve.wait_ge(hi_split, i + 1)
                nc.vector.tensor_tensor(splits[i][1][:, 1], raw_piece(i), splits[i][1][:, 0].bitcast(F32), ALU.subtract).then_inc(lo_even, 1)

            def q_times_cos(b, p):
                u, r = UNITS * b + p, p % 2
                dve.wait_ge(q_rot, u + 1)
                if not (isinstance(b, int) and b == 0 and p < 2):
                    dve.wait_ge(q_add, u - 1)
                nc.vector.tensor_tensor(qcos[:, r], q_ps[:, :, :], cosT[:, :].unsqueeze(1).to_broadcast([P, 2, SEQ]), ALU.mult).then_inc(q_cos, 1)

            def k_times_cos(b, g):
                n = KV * b + g
                dve.wait_ge(k_rot, n + 1)
                if not (isinstance(b, int) and b == 0 and g == 0):
                    dve.wait_ge(k_lo, n)
                nc.vector.tensor_tensor(kcos, misc[:, 0:SEQ], cosT[:, :], ALU.mult).then_inc(k_cos, 1)

            def q_split(b, p):
                u, r = UNITS * b + p, p % 2
                dve.wait_ge(q_add, u + 1)
                if not (isinstance(b, int) and b == 0 and p < 2):
                    dve.wait_ge(s_ok, u - 1)
                nc.vector.tensor_copy(qT[:, r, 0], rot[:, r]).then_inc(q_hi, 1)
                dve.wait_ge(q_hi, u + 1)
                nc.vector.tensor_tensor(qT[:, r, 1], rot[:, r], qT[:, r, 0].bitcast(F32), ALU.subtract).then_inc(q_lo, 1)

            def k_split(b, g):
                n, r = KV * b + g, g % 2
                dve.wait_ge(k_add, n + 1)
                if not (isinstance(b, int) and b == 0 and g < 2):
                    dve.wait_ge(s_ok, 2 * n - 2)
                nc.vector.tensor_copy(kT[:, r, 0, :], krot).then_inc(k_hi, 1)
                dve.wait_ge(k_hi, n + 1)
                nc.vector.tensor_tensor(kT[:, r, 1, :], krot, kT[:, r, 0, :].bitcast(F32), ALU.subtract).then_inc(k_lo, 1)

            def maxima(b, p):
                u, r = UNITS * b + p, p % 2
                dve.wait_ge(s_ok, u + 1)
                if not (isinstance(b, int) and b == 0 and p < 2):
                    dve.wait_ge(exp_ok, u - 1)
                nc.vector.tensor_reduce(nmax[:, r, 0, :], s0_ps[:, :, :], AX_X, ALU.max, negate=True)
                nc.vector.tensor_reduce(nmax[:, r, 1, :], s1_ps[:, :, :], AX_X, ALU.max, negate=True).then_inc(max_ok, 1)

            def reciprocals(b, p):
                u, r = UNITS * b + p, p % 2
                dve.wait_ge(exp_ok, u + 1)
                if not (isinstance(b, int) and b == 0 and p < 2):
                    dve.wait_ge(norm_ok, u - 1)
                nc.vector.reciprocal(rsum[:, r, :, 0:1], sums[:, r, :, 0:1])
                nc.vector.reciprocal(rsum[:, r, :, 1:3], sums[:, r, :, 1:2].to_broadcast([P, 2, 2])).then_inc(rsum_ok, 1)

            def pT_rest(b, p):
                u = UNITS * b + p
                for n, (lo, hi, bk) in enumerate(((0, 2 * SEQ, 4), (2 * SEQ, 2 * SEQ + 2 * P, 5))):
                    dve.wait_ge(pT_hi, 2 * u + n + 1)
                    i = nc.vector.tensor_tensor(pT[:, 1, lo:hi], bank[bk][:, 0:hi - lo], pT[:, 0, lo:hi].bitcast(F32), ALU.subtract)
                i.then_inc(pT_lo, 1)

            def o_rest(b, p):
                u = UNITS * b + p
                dve.wait_ge(o_hi, u + 1)
                nc.vector.tensor_tensor(oT[:, 1], o_ps[:, :, :], oT[:, 0].bitcast(F32), ALU.subtract).then_inc(o_lo, 1)

            def v_rest(b, t):
                dve.wait_ge(v_hi, NT * b + t + 1)
                nc.vector.tensor_tensor(v[:, 1, t, :], misc[:, :], v[:, 0, t, :].bitcast(F32), ALU.subtract).then_inc(v_lo, 1)

            def clamp_gates(b):
                g = gates[:, b].rearrange("p j n -> p (j n)")
                sign = hbuf[:, :, :].rearrange("p c n -> p (c n)")
                dve.wait_ge(rows_out, b + 1)
                nc.vector.tensor_scalar(sign, g, 0.0, 2.0, ALU.is_ge, ALU.mult).then_inc(gates_step, 1)
                dve.wait_ge(gates_step, 4 * b + 1)
                nc.vector.tensor_scalar(sign, sign, -1.0, None, ALU.add).then_inc(gates_step, 1)
                dve.wait_ge(gates_step, 4 * b + 2)
                nc.vector.tensor_tensor(g, g, sign, ALU.mult).then_inc(gates_step, 1)
                dve.wait_ge(gates_step, 4 * b + 3)
                nc.vector.scalar_tensor_tensor(g, g, 0.25, sign, ALU.max, ALU.mult).then_inc(gates_step, 1)
                dve.wait_ge(gates_step, 4 * b + 4)

            def gate_y(b):
                dve.wait_ge(d_ok, UNITS * (b + 1))
                if not (isinstance(b, int) and b == 0):
                    dve.wait_ge(x1_ok, b)
                ga = gates[:, bass.ds(b, 1), 0, :].to_broadcast([P, NT, HID])
                nc.vector.tensor_tensor(ybuf[:, :, :], y_ps[:, :, :], ga, ALU.mult).then_inc(y_read, 1)

            def logits_out(b):
                dve.wait_ge(lt_ok, b + 1)
                if not (isinstance(b, int) and b == 0):
                    dve.wait_ge(l_ok, b)
                nc.vector.tensor_copy(lt[0:GW, :], misc[0:GW, 0:SEQ]).then_inc(lt_out, 1)

            def router_max(b):
                dve.wait_ge(l_ok, b + 1)
                lg = misc[:, 0:NT * P].rearrange("p (t n) -> p t n", t=NT)
                nc.vector.tensor_reduce(rmax[:, :], lg[:, :, 0:EXPERTS], AX_X, ALU.max, negate=True).then_inc(rmax_ok, 1)

            ROUTER_STEPS = 11

            def routing(b):
                count = [0]

                def after_it(i):
                    i.then_inc(r_step, 1)
                    count[0] += 1
                    dve.wait_ge(r_step, ROUTER_STEPS * b + count[0])

                dve.wait_ge(rexp_ok, b + 1)
                after_it(nc.vector.reciprocal(rtot[:, 1, :], rtot[:, 0, :]))
                for t in range(NT):
                    i = nc.vector.tensor_scalar(probs20[:, t, 0:EXPERTS], rexp[:, t, :], rtot[:, 1, t:t + 1], None, ALU.mult)
                after_it(i)
                nc.vector.tensor_scalar(sg[:, 1], sg[:, 0], 1.0, None, ALU.add)
                for t in range(NT):
                    i = nc.vector.max(top8[:, t, :], probs20[:, t, 0:EXPERTS])
                after_it(i)
                after_it(nc.vector.memset(top8[:, :, TOP_K:8], SENTINEL))
                nc.vector.reciprocal(coef[:, :, EXPERTS:GATES], sg[:, 1])
                for t in range(NT):
                    i = nc.vector.match_replace(left20[:, t, :], top8[:, t, :], probs20[:, t, :], -1.0)
                after_it(i)
                after_it(nc.vector.scalar_tensor_tensor(coef[:, :, 0:EXPERTS], left20[:, :, 0:EXPERTS], 0.0, probs20[:, :, 0:EXPERTS],
                                                        ALU.is_lt, ALU.mult))
                after_it(nc.vector.tensor_copy(piece[:, 0], coef[:, :, :]))
                if not (isinstance(b, int) and b == 0):
                    dve.wait_ge(cT_ok, b)
                nc.vector.tensor_copy(pieces[:, :, 0, 0:GATES], piece[:, 0])
                after_it(nc.vector.tensor_tensor(rest[:, 0], coef[:, :, :], piece[:, 0], ALU.subtract))
                after_it(nc.vector.tensor_copy(piece[:, 1], rest[:, 0]))
                nc.vector.tensor_copy(pieces[:, :, 1, 0:GATES], piece[:, 1])
                after_it(nc.vector.tensor_tensor(rest[:, 1], rest[:, 0], piece[:, 1], ALU.subtract))
                after_it(nc.vector.tensor_copy(piece[:, 0], rest[:, 1]))
                nc.vector.tensor_copy(pieces[:, :, 2, 0:GATES], piece[:, 0]).then_inc(pieces_ok, 1)

            def coefs_out(b):
                dve.wait_ge(cT_ok, b + 1)
                nc.vector.tensor_copy(coefT[:, bass.ds(b * SEQ, SEQ)], misc[0:3 * GW, 0:SEQ]).then_inc(coefs_ok, 1)

            dve.wait_ge(c_step, 1)
            nc.vector.tensor_scalar(ce[:, 1], ce[:, 0], 1.0, None, ALU.add).then_inc(c_step, 1)
            dve.wait_ge(c_step, 2)
            nc.vector.reciprocal(ce[:, 0], ce[:, 1]).then_inc(c_step, 1)
            dve.wait_ge(c_step, 3)
            nc.vector.tensor_tensor(ce[:, 2], ce[:, 0], cT[:, :, :], ALU.mult).then_inc(c_step, 1)
            dve.wait_ge(c_step, 4)
            nc.vector.tensor_copy(c_wide, ce[:, 2].unsqueeze(3).to_broadcast([P, KC, BATCH, P])).then_inc(c_step, 1)
            nc.vector.memset(pieces[:, :, :, :], 0.0)
            nc.vector.memset(lt[:, :], 0.0).then_inc(consts, 1)
            nc.vector.memset(probs20[:, :, EXPERTS:EXPERTS + 4], SENTINEL).then_inc(coefs_ok, 1)
            dve.wait_ge(in_x, 16)
            norm_stats(0, 0)
            dve.wait_ge(in_const, 48)
            nc.vector.tensor_copy(ident_bf[:, :], ident[:, :]).then_inc(consts, 1)
            normalize(0, 0)
            dve.wait_ge(mod_cols, 1)
            for j in range(4):
                i = nc.vector.tensor_scalar(modc[:, j], mod_ps[:, j], float(j % 2), None, ALU.add)
            i.then_inc(cols_out, 1)
            dve.wait_ge(cols_out, 1)
            for b in range(BATCH):
                if b < BATCH - 1:
                    norm_stats(b + 1, b + 1)
                modulate(b, b, 0)
                if b < BATCH - 1:
                    normalize(b + 1, b + 1)
                if b < 3:
                    split_lo(2 * b)
                h_rest(b, b)
            k_times_cos(0, 0)
            q_times_cos(0, 0)
            k_split(0, 0)
            q_split(0, 0)
            q_times_cos(0, 1)
            dve.wait_ge(in_gw, 16)
            nc.vector.tensor_copy(gw[:, 0], gw_raw[:, :, :]).then_inc(gw_split, 1)
            dve.wait_ge(gw_split, 1)
            nc.vector.tensor_tensor(gw[:, 1], gw_raw[:, :, :], gw[:, 0].bitcast(F32), ALU.subtract)
            k_times_cos(0, 1)
            q_split(0, 1)
            k_split(0, 1)
            maxima(0, 0)
            q_times_cos(0, 2)
            reciprocals(0, 0)

            def batch(b, first, last):
                for p in range(UNITS):
                    if p > 0:
                        o_rest(b, p - 1)
                    elif not first:
                        o_rest(b - 1, UNITS - 1)
                    if not first and p == 2:
                        normalize(BATCH + b - 1, b - 1)
                    if not first and p == 3:
                        modulate(BATCH + b - 1, b - 1, 2)
                    if not first and p == 5:
                        logits_out(b - 1)
                    if not first and p == 7:
                        router_max(b - 1)
                    if p < UNITS - 1:
                        maxima(b, p + 1)
                    elif not last:
                        maxima(b + 1, 0)
                    pT_rest(b, p)
                    if p == 0:
                        v_rest(b, 0)
                    ahead = p + LOOKAHEAD - 1
                    if ahead < UNITS or not last:
                        ab, ap = (b, ahead) if ahead < UNITS else (b + 1, ahead - UNITS)
                        if ap % 2 == 0 and not (first and p == 0):
                            k_split(ab, ap // 2)
                        q_split(ab, ap)
                    if p < UNITS - 1:
                        reciprocals(b, p + 1)
                    elif not last:
                        reciprocals(b + 1, 0)
                    ahead = p + LOOKAHEAD
                    if ahead < UNITS or not last:
                        ab, ap = (b, ahead) if ahead < UNITS else (b + 1, ahead - UNITS)
                        if ap % 2 == 0:
                            k_times_cos(ab, ap // 2)
                        q_times_cos(ab, ap)
                    if p == 0:
                        v_rest(b, 1)
                    if first and p in (0, 2):
                        split_lo(6 + p)
                    if first and p >= 4:
                        clamp_gates(p - 4)
                    if not first and p == 0:
                        gate_y(b - 1)
                    if not first and p == 1:
                        dve.wait_ge(x1_ok, b)
                        norm_stats(BATCH + b - 1, b - 1)
                    if not first and p == 3:
                        h_rest(BATCH + b - 1, b - 1)
                    if not first and p == 7:
                        routing(b - 1)
                        coefs_out(b - 1)

            batch(0, True, False)
            with dve.Fori(1, BATCH - 1) as b:
                batch(b, False, False)
            batch(BATCH - 1, False, True)
            b = BATCH - 1
            o_rest(b, UNITS - 1)
            gate_y(b)
            dve.wait_ge(y_read, BATCH)
            for n in range(BATCH):
                i = nc.vector.memset(bank[4 + n][:, :], 0.0)
            i.then_inc(zeroed, 1)
            dve.wait_ge(x1_ok, BATCH)
            norm_stats(BATCH + b, b)
            normalize(BATCH + b, b)
            modulate(BATCH + b, b, 2)
            h_rest(BATCH + b, b)
            logits_out(b)
            router_max(b)
            routing(b)
            coefs_out(b)

            def dve_step(s, half, at, first):
                dve.wait_ge(silu_ok, s + 1)
                dve.wait_ge(u_ok, s + 1)
                if not (first and at < 2):
                    dve.wait_ge(scaled_ok, s - 1)
                nc.vector.tensor_tensor(prod[:, half, :], u_ps[:, :], silu[:, half, :], ALU.mult).then_inc(prod_ok, 1)
                dve.wait_ge(prod_ok, s + 1)
                dve.wait_ge(c_ok, s + 1)
                if not (first and at < 2):
                    dve.wait_ge(a_lo, s - 1)
                nc.vector.tensor_tensor(scaled[:, half, :], c_ps[:, :], prod[:, half, :], ALU.mult).then_inc(scaled_ok, 1)
                dve.wait_ge(a_hi, s + 1)
                nc.vector.tensor_tensor(actT[:, half, 1, :], scaled[:, half, :], actT[:, half, 0, :].bitcast(F32), ALU.subtract).then_inc(a_lo, 1)

            def chunk_pair(i, first):
                for at in range(4):
                    dve_step(4 * i + at, at % 2, at, first)

            chunk_pair(0, True)
            with dve.Fori(1, CHUNKS // 2) as i:
                chunk_pair(i, False)
            for b in range(BATCH):
                dve.wait_ge(down_ok, 2 * CHUNKS - 1 + b // 2)
                nc.vector.tensor_tensor(z[:, :, :] if b % 2 else ybuf[:, :, :], y2_ps[b],
                                        gates[:, b, 1, :].unsqueeze(1).to_broadcast([P, NT, HID]), ALU.mult).then_inc(yg_ok, 1)
                dve.wait_ge(yg_ok, b + 1)
                nc.vector.tensor_tensor(xs[:, b], z[:, :, :] if b % 2 else ybuf[:, :, :], xs[:, b], ALU.add).then_inc(x2_ok, 1)

        @block.gpsimd
        def _(pool):
            def power(l):
                pool.wait_ge(ln_step, 3 * l + 3)
                if not (isinstance(l, int) and l == 0):
                    pool.wait_ge(z_ok, l)
                nc.gpsimd.tensor_tensor(rstd[:, :], ve[:, :], neg_half[:, :], ALU.pow).then_inc(rstd_ok, 1)

            def split_lo(i):
                pool.wait_ge(hi_split, i + 1)
                nc.gpsimd.tensor_tensor(splits[i][1][:, 1], raw_piece(i), splits[i][1][:, 0].bitcast(F32), ALU.subtract).then_inc(lo_odd, 1)

            def q_rope(b, p):
                u, r = UNITS * b + p, p % 2
                pool.wait_ge(q_rot, u + 1)
                nc.gpsimd.tensor_tensor(rot[:, r], rot[:, r], sinT[:, :].unsqueeze(1).to_broadcast([P, 2, SEQ]), ALU.mult).then_inc(q_sin, 1)
                pool.wait_ge(q_sin, u + 1)
                pool.wait_ge(q_cos, u + 1)
                nc.gpsimd.tensor_tensor(rot[:, r], rot[:, r], qcos[:, r], ALU.add).then_inc(q_add, 1)

            def k_rope(b, g):
                n = KV * b + g
                pool.wait_ge(k_rot, n + 1)
                nc.gpsimd.tensor_tensor(krot, krot, sinT[:, :], ALU.mult).then_inc(k_sin, 1)
                pool.wait_ge(k_sin, n + 1)
                pool.wait_ge(k_cos, n + 1)
                nc.gpsimd.tensor_tensor(krot, krot, kcos, ALU.add).then_inc(k_add, 1)

            def norm_probs(b, p):
                u, r = UNITS * b + p, p % 2
                pool.wait_ge(rsum_ok, u + 1)
                e = prob[:, r, :].rearrange("p (k n) -> p k n", k=6)
                by = rsum[:, r].rearrange("p h k -> p (h k)").unsqueeze(2).to_broadcast([P, 6, P])
                nc.gpsimd.tensor_tensor(e, e, by, ALU.mult).then_inc(norm_ok, 1)

            def add_x(b):
                pool.wait_ge(y_read, b + 1)
                at = xs[:, bass.ds(b, 1)].rearrange("p a t n -> p (a t) n")
                nc.gpsimd.tensor_tensor(at, at, ybuf[:, :, :], ALU.add).then_inc(x1_ok, 1)

            def h_copy(b):
                if isinstance(b, int) and b == 0:
                    pool.wait_ge(h_lo, 1)
                else:
                    pool.wait_ge(v_ok, NT * b)
                for s in range(2):
                    i = nc.gpsimd.tensor_copy(h_stat[:, s], hT[:, s, :, bass.ds(b * SEQ, SEQ)])
                i.then_inc(h_stat_ok, 1)

            nc.gpsimd.memset(neg_half[:, :], -0.5).then_inc(half_ok, 1)
            pool.wait_ge(half_ok, 1)
            power(0)
            for b in range(BATCH):
                if b < BATCH - 1:
                    power(b + 1)
                if b == 0:
                    split_lo(1)
                if b == 2:
                    split_lo(3)
            pool.wait_ge(in_rope, 32)
            k_rope(0, 0)
            q_rope(0, 0)
            h_copy(0)
            q_rope(0, 1)
            k_rope(0, 1)
            norm_probs(0, 0)
            split_lo(5)
            q_rope(0, 2)

            def batch(b, first, last):
                for p in range(UNITS):
                    if not first and p == 1:
                        add_x(b - 1)
                    if p < UNITS - 1:
                        norm_probs(b, p + 1)
                    elif not last:
                        norm_probs(b + 1, 0)
                    if not first and p == 1:
                        power(BATCH + b - 1)
                    ahead = p + LOOKAHEAD
                    if ahead < UNITS or not last:
                        ab, ap = (b, ahead) if ahead < UNITS else (b + 1, ahead - UNITS)
                        if ap % 2 == 0:
                            k_rope(ab, ap // 2)
                        q_rope(ab, ap)
                    if first and p in (1, 3):
                        split_lo(6 + p)
                    if not last and p == 2:
                        h_copy(b + 1)

            batch(0, True, False)
            with pool.Fori(1, BATCH - 1) as b:
                batch(b, False, False)
            batch(BATCH - 1, False, True)
            add_x(BATCH - 1)
            power(2 * BATCH - 1)

            def weights_lo(i, slot, first):
                pool.wait_ge(w_hi, 2 * i + slot + 1)
                nc.gpsimd.tensor_tensor(w_gu[:, slot, 1].rearrange("p c g n -> p (c g n)"), raw[:, slot, 0:512],
                                        w_gu[:, slot, 0].rearrange("p c g n -> p (c g n)").bitcast(F32), ALU.subtract)
                nc.gpsimd.tensor_tensor(w_dn[:, slot, 1], raw[:, slot, 512:768], w_dn[:, slot, 0].bitcast(F32), ALU.subtract).then_inc(w_lo, 1)

            for slot in range(2):
                weights_lo(0, slot, True)
            with pool.Fori(1, CHUNKS // 2) as i:
                for slot in range(2):
                    weights_lo(i, slot, False)


def _constants(np):
    f = np.float32
    inv = f(1.0) / np.power(f(10000.0), np.arange(0, HD, 2, dtype=f) / f(HD)).astype(f)
    ang = np.arange(SEQ, dtype=f)[None, :] * inv[:, None]
    root = f(HD ** -0.25)
    cos = np.concatenate([np.cos(ang), np.cos(ang)]) * root
    sin = np.concatenate([-np.sin(ang), np.sin(ang)]) * root
    causal = np.where(np.arange(P)[None, :] > np.arange(P)[:, None], f(MASKED), f(0))
    select = np.zeros((3 * GW, CHUNKS * P), f)
    for n in range(EXPERTS * INNER + SHARED):
        e = min(n // INNER, EXPERTS)
        select[[e, GW + e, 2 * GW + e], n] = 1
    return cos.astype(f), sin.astype(f), np.eye(P, dtype=f), causal.astype(f), select


def kernel(**inputs):
    import numpy as np
    import ml_dtypes
    import concourse.bacc as bacc
    from concourse.bass_utils import run_bass_kernel_spmd

    i = {k[3:]: np.asarray(a) for k, a in inputs.items()}
    pad = CHUNKS * P - EXPERTS * INNER - SHARED

    def features(w, shared):
        rows = [w.reshape(EXPERTS * INNER, HID), shared, np.zeros((pad, HID), w.dtype)]
        return np.concatenate(rows).reshape(CHUNKS, P, HID)

    def as_stationary(w):
        return w.reshape(CHUNKS, P, KC, P).transpose(0, 3, 2, 1)

    gate = features(i["ffn_w13"][:, :INNER], i["ffn_shared_gate_up_w"][:SHARED])
    up = features(i["ffn_w13"][:, INNER:], i["ffn_shared_gate_up_w"][SHARED:])
    gate_up = np.stack([as_stationary(gate), as_stationary(up)], 3).reshape(CHUNKS, P, 2 * KC * P)
    down = features(i["ffn_w2"].transpose(0, 2, 1), i["ffn_shared_down_w"].T)
    router = np.zeros((HID, GW), np.float32)
    router[:, :EXPERTS] = i["ffn_gate_w"].T
    router[:, EXPERTS] = i["ffn_sgate_w"][0]
    c = i["c"].T.reshape(KC, P, BATCH).transpose(1, 0, 2).reshape(P, KC * BATCH)
    cos, sin, ident, causal, select = _constants(np)
    arrays = {
        "x_dram": i["attn_x"], "wq_dram": i["attn_Wq"], "wk_dram": i["attn_Wk"], "wv_dram": i["attn_Wv"],
        "wo_dram": i["attn_Wo"], "router_dram": router, "gate_up_dram": gate_up, "down_dram": down,
        "c_dram": c, "wmod_dram": i["wmod"], "cos_dram": cos, "sin_dram": sin, "ident_dram": ident,
        "causal_dram": causal.astype(ml_dtypes.bfloat16), "select_dram": select.astype(ml_dtypes.bfloat16),
    }
    arrays = {k: np.ascontiguousarray(a) for k, a in arrays.items()}
    nc = bacc.Bacc("TRN2", target_bir_lowering=False, num_devices=1)
    args = [nc.dram_tensor(k, a.shape, mybir.dt.from_np(a.dtype), kind="ExternalInput").ap() for k, a in arrays.items()]
    out = nc.dram_tensor("out_dram", (BATCH, SEQ, HID), F32, kind="ExternalOutput").ap()
    build(nc, *args, out)
    r = run_bass_kernel_spmd(nc, [arrays], core_ids=[0])
    return r.results[0]["out_dram"]
```

```python
from contextlib import ExitStack

import concourse.bass as bass
from concourse import mybir

F32 = mybir.dt.float32
F32R = mybir.dt.float32r
BF16 = mybir.dt.bfloat16
ACT = mybir.ActivationFunctionType
ALU = mybir.AluOpType
AX_X = mybir.AxisListType.X

P = 128
BATCH, SEQ, HID = 4, 256, 256
KC = HID // P
NT = SEQ // P
HEADS, KV, HD = 16, 4, 128
UNITS = HEADS // 2
EXPERTS, INNER, SHARED, TOP_K = 16, 176, 704, 4
CHUNKS = -(-(EXPERTS * INNER + SHARED) // P)
GATES = EXPERTS + 1
GW = 32
EPS = 1e-5
MASKED = -3.0e38
SENTINEL = -5.0
HALF = BATCH * SEQ // 2
RAW = 4
FFN_RING = 4
EARLY = 4
SPLITS = 10
LOOKAHEAD = 3


def build(nc, x_d, wq_d, wk_d, wv_d, wo_d, gate_d, up_d, down_d, c_d, wmod_d,
          cos_d, sin_d, ident_d, causal_d, select_d, out_d):
    with ExitStack() as ctx:
        def sb(name, shape, dt):
            return ctx.enter_context(nc.sbuf_tensor(name, shape, dt))

        def sem(name):
            return ctx.enter_context(nc.semaphore(name))

        wq = sb("wq", [P, 2, KC, HEADS * HD], F32R)
        wk = sb("wk", [P, 2, KC, KV * HD], F32R)
        wv = sb("wv", [P, 2, KC, KV * HD], F32R)
        wo = sb("wo", [P, 2, HEADS, HID], F32R)
        hT = sb("hT", [P, 2, KC, BATCH * SEQ], F32R)
        xs = sb("xs", [P, BATCH, NT, HID], F32)
        gates = sb("gates", [P, BATCH, 2, HID], F32)
        raw = sb("raw", [P, RAW, 1024], F32)
        h_stat = sb("h_stat", [P, 2, KC, SEQ], F32R)
        v = sb("v", [P, 2, NT, KV * HD], F32R)
        qT = sb("qT", [P, 2, 2, 2, SEQ], F32R)
        kT = sb("kT", [P, 2, 2, SEQ], F32R)
        pT = sb("pT", [P, 2, 2 * SEQ + 2 * P], F32R)
        oT = sb("oT", [P, 2, 2, SEQ], F32R)
        work = sb("work", [P, 3584], F32)
        prob = work[:, 0:1536].rearrange("p (r n) -> p r n", r=2)
        rot = work[:, 1536:2560].rearrange("p (r h n) -> p r h n", r=2, h=2)
        qcos = work[:, 2560:3584].rearrange("p (r h n) -> p r h n", r=2, h=2)
        kwork = sb("kwork", [P, 512], F32)
        krot = kwork[:, 0:256]
        kcos = kwork[:, 256:512]
        z = sb("z", [P, NT, HID], F32)
        hbuf = sb("hbuf", [P, KC, SEQ], F32)
        ybuf = sb("ybuf", [P, NT, HID], F32)
        cosT = sb("cosT", [P, SEQ], F32)
        sinT = sb("sinT", [P, SEQ], F32)
        ident = sb("ident", [P, P], F32)
        ident_bf = sb("ident_bf", [P, P], BF16)
        causal = sb("causal", [P, 2, P], BF16)
        select = sb("select", [3 * GW, CHUNKS * P], BF16)
        coefT = sb("coefT", [3 * GW, BATCH * SEQ], BF16)
        gw = sb("gw", [P, 2, KC, GW], F32R)
        gw_raw = sb("gw_raw", [P, KC, GW], F32)
        wmod = [work[:, 0:KC * 2 * HID].rearrange("p (c n) -> p c n", c=KC),
                gates[:, :, :, :].rearrange("p b j n -> p (b j n)").rearrange("p (c n) -> p c n", c=KC)]
        cT = sb("cT", [P, KC, BATCH], F32)
        ce = sb("ce", [P, 3, KC, BATCH], F32)
        modc = sb("modc", [P, 4, KC, BATCH], F32)
        gate_cols = sb("gate_cols", [P, BATCH, 2, KC], F32)
        gate_sign = sb("gate_sign", [P, BATCH, 2, KC], F32)
        ones = sb("ones", [P, P], F32)
        stats = sb("stats", [P, NT, 6], F32)
        mv = sb("mv", [P, NT, 2], F32)
        ve = sb("ve", [P, NT], F32)
        neg_half = sb("neg_half", [P, NT], F32)
        rstd = sb("rstd", [P, NT], F32)
        nmax = sb("nmax", [P, 2, 2, 2], F32)
        sums = sb("sums", [P, 2, 2, 2], F32)
        rsum = sb("rsum", [P, 2, 2, 3], F32)
        lt = sb("lt", [P, SEQ], F32)
        rmax = sb("rmax", [P, NT], F32)
        rexp = sb("rexp", [P, NT, EXPERTS], F32)
        rtot = sb("rtot", [P, 2, NT], F32)
        sg = sb("sg", [P, 2, NT, 1], F32)
        probs20 = sb("probs20", [P, NT, EXPERTS + 4], F32)
        top8 = sb("top8", [P, NT, 8], F32)
        left20 = sb("left20", [P, NT, EXPERTS + 4], F32)
        coef = sb("coef", [P, NT, GATES], F32)
        rest = sb("rest", [P, 2, NT, GATES], F32)
        piece = sb("piece", [P, 2, NT, GATES], BF16)
        pieces = sb("pieces", [P, NT, 3, GW], F32)

        flat = wq[:, 0, :, :].rearrange("p c n -> p (c n)")
        flat2 = wq[:, 1, :, :].rearrange("p c n -> p (c n)")
        gu_at = [flat[:, 0:1024], flat[:, 1024:2048], flat2[:, 2048:3072], flat2[:, 3072:4096]]
        w_gu = [at.rearrange("p (s c g n) -> p s c g n", s=2, c=KC, g=2) for at in gu_at]
        w_dn = flat[:, 2048:4096].rearrange("p (r s n) -> p r s n", r=FFN_RING, s=2)
        actT = flat2[:, 0:2048].rearrange("p (r s n) -> p r s n", r=2, s=2)
        on_rope, on_prob = work[:, 1536:3072].rearrange("p (k n) -> p k n", k=3), work[:, 0:1536].rearrange("p (k n) -> p k n", k=3)
        silu = [at[:, 0, :] for at in (on_rope, on_prob)]
        prod = [at[:, 1, :] for at in (on_rope, on_prob)]
        scaled = [at[:, 2, :] for at in (on_rope, on_prob)]

        bank = [ctx.enter_context(nc.psum_tensor(f"bank{i}", [P, 512], F32)) for i in range(8)]
        q_ps = bank[0][:, :].rearrange("p (h n) -> p h n", h=2)
        misc = bank[1]
        s0_ps = bank[2][:, 0:256].rearrange("p (h n) -> p h n", h=2)
        s1_ps = bank[3][:, :].rearrange("p (h n) -> p h n", h=2)
        p0_ps = bank[4][:, :].rearrange("p (h n) -> p h n", h=2)
        p1_ps = bank[5][:, 0:256].rearrange("p (h n) -> p h n", h=2)
        o_ps = bank[6][:, :].rearrange("p (h n) -> p h n", h=2)
        y_ps = bank[7][:, :].rearrange("p (t n) -> p t n", t=NT)
        mod_ps = [bank[6][:, 0:16].rearrange("p (j k b) -> p j k b", j=2, k=KC),
                  bank[7][:, 0:32].rearrange("p (j k b) -> p j k b", j=4, k=KC)]
        y2_ps = [bank[4 + b][:, :].rearrange("p (t n) -> p t n", t=NT) for b in range(BATCH)]
        g_ps, u_ps, c_ps = bank[0], bank[2], bank[3]

        in_c, in_mod, in_mod_rest, in_x, in_x_rest, in_rope, in_ident, in_causal, in_select, in_gw = (sem(n) for n in (
            "in_c", "in_mod", "in_mod_rest", "in_x", "in_x_rest", "in_rope", "in_ident", "in_causal", "in_select", "in_gw"))
        raw_in = [sem(f"raw_in{i}") for i in range(RAW)]
        c_step, mod_cols, cols_out, gates_step, diag_ok, mod_rows, rows_out = (sem(n) for n in (
            "c_step", "mod_cols", "cols_out", "gates_step", "diag_ok", "mod_rows", "rows_out"))
        consts, half_ok = sem("consts"), sem("half_ok")
        hi_split, lo_even, lo_odd, gw_split = (sem(n) for n in ("hi_split", "lo_even", "lo_odd", "gw_split"))
        ln_step, rstd_ok, z_ok, zT_ok, h_ok, h_hi, h_lo, h_stat_ok = (sem(n) for n in (
            "ln_step", "rstd_ok", "z_ok", "zT_ok", "h_ok", "h_hi", "h_lo", "h_stat_ok"))
        q_ok, q_rot, q_cos, q_sin, q_add, q_hi, q_lo = (sem(n) for n in (
            "q_ok", "q_rot", "q_cos", "q_sin", "q_add", "q_hi", "q_lo"))
        k_ok, k_rot, k_cos, k_sin, k_add, k_hi, k_lo = (sem(n) for n in (
            "k_ok", "k_rot", "k_cos", "k_sin", "k_add", "k_hi", "k_lo"))
        v_ok, v_hi, v_lo = (sem(n) for n in ("v_ok", "v_hi", "v_lo"))
        s_ok, max_ok, exp_ok, rsum_ok, norm_ok = (sem(n) for n in ("s_ok", "max_ok", "exp_ok", "rsum_ok", "norm_ok"))
        pT_ok, pT_hi, pT_lo, o_ok, o_hi, o_lo = (sem(n) for n in ("pT_ok", "pT_hi", "pT_lo", "o_ok", "o_hi", "o_lo"))
        d_ok, y_read, x1_ok = (sem(n) for n in ("d_ok", "y_read", "x1_ok"))
        lt_ok, lt_out, l_ok, rmax_ok, rexp_ok, r_step, pieces_ok, cT_ok, coefs_ok = (sem(n) for n in (
            "lt_ok", "lt_out", "l_ok", "rmax_ok", "rexp_ok", "r_step", "pieces_ok", "cT_ok", "coefs_ok"))
        w_in = [sem(f"w_in{i}") for i in range(FFN_RING)]
        w_hi, w_lo = (sem(n) for n in ("w_hi", "w_lo"))
        g_ok, u_ok, c_ok, silu_ok, prod_ok, scaled_ok, a_hi, a_lo, down_ok = (sem(n) for n in (
            "g_ok", "u_ok", "c_ok", "silu_ok", "prod_ok", "scaled_ok", "a_hi", "a_lo", "down_ok"))
        yg_ok, x2_ok, out_ok = (sem(n) for n in ("yg_ok", "x2_ok", "out_ok"))

        wq_v = wq_d.rearrange("(c p) n -> p c n", p=P)
        wk_v = wk_d.rearrange("(c p) n -> p c n", p=P)
        wv_v = wv_d.rearrange("(c p) n -> p c n", p=P)
        wo_v = wo_d.rearrange("(h p) n -> p h n", p=P)
        x_v = x_d.rearrange("b (t p) n -> p b t n", p=P)
        out_v = out_d.rearrange("b (t p) n -> p b t n", p=P)

        def piece_of(w, w_v, cols):
            return w_v[:, :, cols], w[:, :, :, cols], KC

        q4 = [piece_of(wq, wq_v, slice(g * 512, (g + 1) * 512)) for g in range(KV)]
        all_k = slice(0, KV * HD)
        o4 = [(wo_v[:, 4 * r:4 * r + 4, :], wo[:, :, 4 * r:4 * r + 4, :], 4) for r in range(4)]
        splits = [piece_of(wk, wk_v, all_k), q4[0], q4[1], piece_of(wv, wv_v, all_k), q4[2], o4[0], q4[3], o4[1], o4[2], o4[3]]
        K_SPLIT, V_SPLIT = 0, 3
        Q_SPLIT = [1, 2, 4, 6]
        O_SPLIT = [5, 7, 8, 9]

        def raw_piece(i):
            return raw[:, i % RAW, :].rearrange("p (c n) -> p c n", c=splits[i][2])

        def norm1(b):
            return 0 if isinstance(b, int) and b == 0 else 2 * b - 1

        def norm2(b):
            return 2 * BATCH - 1 if isinstance(b, int) and b == BATCH - 1 else 2 * b + 2

        def s_ring(s, half):
            return s % 2 if isinstance(s, int) else half

        PASSES = ((1, 0), (0, 1), (0, 0))

        block = ctx.enter_context(nc.Block())

        @block.sync
        def _(sp):
            wmod_v = wmod_d.rearrange("(c p) n -> p c n", p=P)
            sp.dma_start(cT[:, :, :], c_d.rearrange("p (c b) -> p c b", c=KC)).then_inc(in_c, 16)
            sp.dma_start(wmod[0], wmod_v[:, :, 0:2 * HID]).then_inc(in_mod, 16)
            sp.dma_start(xs[:, 0], x_v[:, 0]).then_inc(in_x, 16)
            sp.dma_start(ident[:, :], ident_d).then_inc(in_ident, 16)
            for i in range(2):
                sp.dma_start(raw_piece(i), splits[i][0]).then_inc(raw_in[i], 16)
            sp.dma_start(cosT[:, :], cos_d).then_inc(in_rope, 16)
            sp.dma_start(sinT[:, :], sin_d).then_inc(in_rope, 16)
            sp.dma_start(wmod[1], wmod_v[:, :, 2 * HID:6 * HID]).then_inc(in_mod_rest, 16)
            for i in range(2, RAW):
                sp.dma_start(raw_piece(i), splits[i][0]).then_inc(raw_in[i], 16)
            sp.dma_start(causal[:, :, :], causal_d.rearrange("p (j n) -> p j n", j=2)).then_inc(in_causal, 16)
            sp.dma_start(xs[:, 1:BATCH], x_v[:, 1:BATCH]).then_inc(in_x_rest, 16)
            sp.dma_start(gw_raw[:, :, :], gate_d.rearrange("(c p) n -> p c n", p=P)).then_inc(in_gw, 16)
            sp.dma_start(select[:, :], select_d).then_inc(in_select, 16)
            for i in range(RAW, SPLITS):
                sp.wait_ge(hi_split, i - RAW + 1)
                if (i - RAW) % 2 == 0:
                    sp.wait_ge(lo_even, (i - RAW) // 2 + 1)
                else:
                    sp.wait_ge(lo_odd, (i - RAW) // 2 + 1)
                sp.dma_start(raw_piece(i), splits[i][0]).then_inc(raw_in[i % RAW], 16)

            def load_chunk(c, slot):
                sp.dma_start(raw[:, slot, 0:512], up_d[bass.ds(c, 1), :, :].rearrange("a p n -> p (a n)")).then_inc(w_in[slot], 16)
                sp.dma_start(raw[:, slot, 512:768], down_d[bass.ds(c, 1), :, :].rearrange("a p n -> p (a n)")).then_inc(w_in[slot], 16)

            sp.wait_ge(hi_split, SPLITS)
            sp.wait_ge(lo_even, SPLITS // 2)
            sp.wait_ge(lo_odd, SPLITS // 2)
            for c in range(FFN_RING):
                load_chunk(c, c)
            with sp.Fori(FFN_RING // 2, CHUNKS // 2) as i:
                for slot in range(2):
                    sp.wait_ge(w_hi, 2 * i - 1 + slot)
                    sp.wait_ge(w_lo, 2 * i - 1 + slot)
                    load_chunk(2 * i + slot, slot)
            for b in range(BATCH):
                sp.wait_ge(x2_ok, b + 1)
                sp.dma_start(out_v[:, b], xs[:, b]).then_inc(out_ok, 16)
            sp.wait_ge(out_ok, 16 * BATCH)

        @block.tensor
        def _(pe):
            def norm_transposes(l):
                pe.wait_ge(z_ok, l + 1)
                zT = misc[:, :].rearrange("p (c n) -> p c n", c=KC)
                for c in range(KC):
                    for t in range(NT):
                        last = nc.tensor.transpose(zT[:, c, t * P:(t + 1) * P], z[:, t, c * P:(c + 1) * P], ident[:, :])
                last.then_inc(zT_ok, 1)

            def project_q(b, p):
                u = UNITS * b + p
                if not (isinstance(b, int) and b == 0 and p == 0):
                    pe.wait_ge(q_cos, u)
                n = 0
                for j in range(2):
                    for c in range(KC):
                        for ws, xsel in PASSES:
                            mm = nc.tensor.matmul(q_ps[:, j, :], wq[:, ws, c, (2 * p + j) * HD:(2 * p + j + 1) * HD],
                                                  hT[:, xsel, c, bass.ds(b * SEQ, SEQ)],
                                                  start=(n == 0), stop=(n % (3 * KC) == 3 * KC - 1), skip_group_check=True)
                            n += 1
                mm.then_inc(q_ok, 1)

            def project_k(b, g):
                n = 0
                for c in range(KC):
                    for ws, xsel in PASSES:
                        mm = nc.tensor.matmul(misc[:, 0:SEQ], wk[:, ws, c, g * HD:(g + 1) * HD],
                                              hT[:, xsel, c, bass.ds(b * SEQ, SEQ)], start=(n == 0), stop=(n == 3 * KC - 1))
                        n += 1
                mm.then_inc(k_ok, 1)

            def project_v(b, t):
                at_start = isinstance(b, int) and b == 0
                if t == 0 and not at_start:
                    pe.wait_ge(h_stat_ok, b)
                n = 0
                for c in range(KC):
                    for hs, ws in PASSES:
                        h = hT if at_start else h_stat
                        mm = nc.tensor.matmul(misc[:, :], h[:, hs, c, t * P:(t + 1) * P], wv[:, ws, c, :],
                                              start=(n == 0), stop=(n == 3 * KC - 1))
                        n += 1
                mm.then_inc(v_ok, 1)

            def scores(b, p):
                u, g, r = UNITS * b + p, p // 2, p % 2
                pe.wait_ge(q_lo, u + 1)
                if p % 2 == 0:
                    pe.wait_ge(k_lo, KV * b + g + 1)
                if not (isinstance(b, int) and b == 0 and p == 0):
                    pe.wait_ge(exp_ok, u)
                nc.tensor.matmul(s0_ps[:, :, :], ident_bf[:, :], causal[:, :, :], start=True, stop=False, skip_group_check=True)
                for j in range(2):
                    for qs, ks in PASSES:
                        nc.tensor.matmul(s0_ps[:, j, :], qT[:, r, qs, j, 0:P], kT[:, g % 2, ks, 0:P],
                                         start=False, stop=(qs + ks == 0), skip_group_check=True)
                for j in range(2):
                    for n, (qs, ks) in enumerate(PASSES):
                        nc.tensor.matmul(s1_ps[:, j, :], qT[:, r, qs, j, P:SEQ], kT[:, g % 2, ks, :],
                                         start=(j == 0 and n == 0), stop=False, skip_group_check=True)
                nc.tensor.matmul(s1_ps[:, :, P:SEQ], ident_bf[:, :], causal[:, :, :], start=False, stop=True,
                                 skip_group_check=True).then_inc(s_ok, 1)

            def prob_transposes(b, p):
                u, r = UNITS * b + p, p % 2
                pe.wait_ge(norm_ok, u + 1)
                if not (isinstance(b, int) and b == 0 and p == 0):
                    pe.wait_ge(pT_lo, u)
                for j in range(2):
                    for n, dst in enumerate((p0_ps[:, j, 0:P], p0_ps[:, j, P:SEQ], p1_ps[:, j, :])):
                        at = (3 * j + n) * P
                        tr = nc.tensor.transpose(dst, prob[:, r, at:at + P], ident[:, :])
                tr.then_inc(pT_ok, 1)

            def times_v(b, p):
                u, g = UNITS * b + p, p // 2
                if p == 0:
                    pe.wait_ge(v_lo, NT * (b + 1))
                pe.wait_ge(pT_lo, u + 1)
                if isinstance(b, int) and b == 0 and p == 0:
                    pe.wait_ge(cols_out, 1)
                if not (isinstance(b, int) and b == 0 and p == 0):
                    pe.wait_ge(o_lo, u)
                cols = slice(g * HD, (g + 1) * HD)
                for n, (vs, ps) in enumerate(PASSES):
                    nc.tensor.matmul(o_ps[:, :, :], v[:, vs, 0, cols], pT[:, ps, 0:2 * SEQ], start=(n == 0), stop=False, skip_group_check=True)
                for n, (vs, ps) in enumerate(PASSES):
                    mm = nc.tensor.matmul(o_ps[:, :, P:SEQ], v[:, vs, 1, cols],
                                          pT[:, ps, 2 * SEQ:].rearrange("p (h n) -> p h n", h=2), start=False, stop=(n == 2), skip_group_check=True)
                mm.then_inc(o_ok, 1)

            def project_out(b, p):
                u = UNITS * b + p
                pe.wait_ge(o_lo, u + 1)
                if isinstance(b, int) and b == 0 and p == 0:
                    pe.wait_ge(cols_out, 2)
                if p == 0 and not (isinstance(b, int) and b == 0):
                    pe.wait_ge(y_read, b)
                if isinstance(b, int) and b == 0 and p % 2 == 0:
                    i = O_SPLIT[p // 2]
                    pe.wait_ge(hi_split, i + 1)
                    pe.wait_ge(lo_even if i % 2 == 0 else lo_odd, i // 2 + 1)
                for j in range(2):
                    for t in range(NT):
                        for n, (os, ws) in enumerate(PASSES):
                            mm = nc.tensor.matmul(y_ps[:, t, :], oT[:, os, j, t * P:(t + 1) * P], wo[:, ws, 2 * p + j, :],
                                                  start=(p == 0 and j == 0 and t == 0 and n == 0),
                                                  stop=(p == UNITS - 1 and j == 1 and n == 2), skip_group_check=True)
                mm.then_inc(d_ok, 1)

            def router_logits(b):
                pe.wait_ge(h_lo, norm2(b) + 1)
                n = 0
                for c in range(KC):
                    for ws, xsel in PASSES:
                        mm = nc.tensor.matmul(misc[0:GW, 0:SEQ], gw[:, ws, c, :], hT[:, xsel, c, bass.ds(b * SEQ, SEQ)],
                                              start=(n == 0), stop=(n == 3 * KC - 1))
                        n += 1
                mm.then_inc(lt_ok, 1)

            def logit_transposes(b):
                pe.wait_ge(lt_out, b + 1)
                for t in range(NT):
                    tr = nc.tensor.transpose(misc[:, t * P:(t + 1) * P], lt[:, t * P:(t + 1) * P], ident[:, :])
                tr.then_inc(l_ok, 1)

            def coef_transposes(b):
                pe.wait_ge(pieces_ok, b + 1)
                for t in range(NT):
                    tr = nc.tensor.transpose(misc[0:3 * GW, t * P:(t + 1) * P], pieces[:, t].rearrange("p a n -> p (a n)"), ident[:, :])
                tr.then_inc(cT_ok, 1)

            def gate_or_up(s, c, slot, half, i):
                ps, used, ready = ((g_ps, silu_ok, g_ok), (u_ps, prod_ok, u_ok))[i]
                if i == 0 and half == 0:
                    pe.wait_ge(w_hi, c + 1)
                    pe.wait_ge(w_lo, c + 1)
                if isinstance(s, int) and s == 0:
                    pe.wait_ge(*((q_cos, UNITS * BATCH) if i == 0 else (exp_ok, UNITS * BATCH)))
                else:
                    pe.wait_ge(used, s)
                n = 0
                for kc in range(KC):
                    for ws, xsel in PASSES:
                        mm = nc.tensor.matmul(ps[:, :], w_gu[slot][:, ws, kc, i, :], hT[:, xsel, kc, half * HALF:(half + 1) * HALF],
                                              start=(n == 0), stop=(n == 3 * KC - 1))
                        n += 1
                mm.then_inc(ready, 1)

            def coef_rows(s, c, half):
                if not (isinstance(s, int) and s == 0):
                    pe.wait_ge(scaled_ok, s)
                nc.tensor.matmul(c_ps[:, :], select[:, bass.ds(c * P, P)], coefT[:, half * HALF:(half + 1) * HALF],
                                 start=True, stop=True).then_inc(c_ok, 1)

            def down(s, slot, half, opening=False):
                pe.wait_ge(a_lo, s + 1)
                for t in range(4):
                    for n, (as_, ws) in enumerate(PASSES):
                        mm = nc.tensor.matmul(y2_ps[2 * half + t // 2][:, t % 2, :], actT[:, s_ring(s, half), as_, t * P:(t + 1) * P],
                                              w_dn[:, slot, ws, :], start=(opening and t % 2 == 0 and n == 0), stop=False, skip_group_check=True)
                mm.then_inc(down_ok, 1)

            def step(s, c, slot, half):
                gate_or_up(s, c, slot, half, 0)
                gate_or_up(s, c, slot, half, 1)
                coef_rows(s, c, half)

            def modulation(part, fields):
                for j, field in enumerate(fields):
                    for ko in range(KC):
                        at = (field - 2 * part) * HID + ko * P
                        for c in range(KC):
                            mm = nc.tensor.matmul(mod_ps[part][:, j, ko, :], wmod[part][:, c, at:at + P], ce[:, 2, c, :],
                                                  start=(c == 0), stop=(c == KC - 1))
                mm.then_inc(mod_cols, 1)

            def gate_rows(b):
                pe.wait_ge(diag_ok, b + 1)
                nc.tensor.matmul(misc[:, :], ones[:, :], ybuf[:, :, :].rearrange("p t n -> p (t n)"), start=True, stop=True).then_inc(mod_rows, 1)

            pe.wait_ge(in_mod, 16)
            pe.wait_ge(c_step, 4)
            modulation(0, (0, 1))
            pe.wait_ge(in_ident, 16)
            norm_transposes(0)
            pe.wait_ge(h_lo, 1)
            pe.wait_ge(hi_split, K_SPLIT + 1)
            pe.wait_ge(lo_even, 1)
            project_k(0, 0)
            pe.wait_ge(hi_split, Q_SPLIT[0] + 1)
            pe.wait_ge(lo_odd, 1)
            project_q(0, 0)
            pe.wait_ge(k_cos, 1)
            project_k(0, 1)
            pe.wait_ge(in_mod_rest, 16)
            modulation(1, (3, 4, 2, 5))
            project_q(0, 1)
            pe.wait_ge(consts, 2)
            pe.wait_ge(in_causal, 16)
            scores(0, 0)
            pe.wait_ge(hi_split, Q_SPLIT[1] + 1)
            pe.wait_ge(lo_even, 2)
            project_q(0, 2)

            def batch(b, first, last):
                for p in range(UNITS):
                    if p < UNITS - 1:
                        scores(b, p + 1)
                    elif not last:
                        scores(b + 1, 0)
                    if p == 0:
                        if first:
                            pe.wait_ge(hi_split, V_SPLIT + 1)
                            pe.wait_ge(lo_odd, V_SPLIT // 2 + 1)
                        pe.wait_ge(k_cos, KV * b + 2)
                        project_v(b, 0)
                    if last and p == UNITS - 1:
                        gate_or_up(0, 0, 0, 0, 1)
                        pe.wait_ge(in_select, 16)
                        pe.wait_ge(coefs_ok, BATCH - 1)
                        coef_rows(0, 0, 0)
                    prob_transposes(b, p)
                    if first and p in (2, 4, 6):
                        pe.wait_ge(k_cos, 2 + p // 2)
                        if p == 4:
                            norm_transposes(norm1(1))
                        else:
                            gate_rows({2: 0, 6: 2}[p])
                    if not first:
                        if p == 4 and not last:
                            pe.wait_ge(k_cos, KV * b + 4)
                            norm_transposes(norm1(b + 1))
                        if p == 5:
                            pe.wait_ge(lt_out, b)
                            logit_transposes(b - 1)
                        if p == 7:
                            pe.wait_ge(*((rexp_ok, b) if last else (k_cos, KV * b + 5)))
                            coef_transposes(b - 1)
                    if last and p == UNITS - 2:
                        gate_or_up(0, 0, 0, 0, 0)
                    if last and p == UNITS - 1:
                        break
                    if p in (5, 7):
                        project_out(b, p - 1)
                    ahead = p + LOOKAHEAD
                    if ahead < UNITS or not last:
                        if first and ahead < UNITS and ahead % 2 == 0:
                            i = Q_SPLIT[ahead // 2]
                            pe.wait_ge(hi_split, i + 1)
                            pe.wait_ge(lo_even if i % 2 == 0 else lo_odd, i // 2 + 1)
                        ab, ap = (b, ahead) if ahead < UNITS else (b + 1, ahead - UNITS)
                        if ap == 0:
                            pe.wait_ge(h_lo, norm1(b + 1) + 1)
                        if ap % 2 == 0:
                            if p == 1:
                                pe.wait_ge(v_lo, NT * b + 2)
                            elif first:
                                pe.wait_ge(rows_out, {3: 1, 5: 2, 7: 4}[p])
                            else:
                                pe.wait_ge(*{3: (h_ok, norm2(b - 1) + 1), 5: (rexp_ok, b), 7: (coefs_ok, b + 1)}[p])
                            project_k(ab, ap // 2)
                        project_q(ab, ap)
                    if p == 0:
                        pe.wait_ge(v_lo, NT * b + 1)
                        project_v(b, 1)
                    if p not in (0, 5, 7):
                        project_out(b, p - 1)
                    elif p == 0 and not first:
                        project_out(b - 1, UNITS - 1)
                    times_v(b, p)
                    if first:
                        if p == 4:
                            pe.wait_ge(h_ok, norm1(1) + 1)
                            gate_rows(1)
                        if p == 6:
                            pe.wait_ge(rows_out, 3)
                            gate_rows(3)
                    if not first:
                        if p == 2:
                            pe.wait_ge(k_cos, KV * b + 3)
                            norm_transposes(norm2(b - 1))
                        if p == 4:
                            if last:
                                pe.wait_ge(k_cos, KV * b + 4)
                            else:
                                pe.wait_ge(h_ok, norm1(b + 1) + 1)
                            router_logits(b - 1)

            batch(0, True, False)
            with pe.Fori(1, BATCH - 1) as b:
                batch(b, False, False)
            batch(BATCH - 1, False, True)

            b, p = BATCH - 1, UNITS - 1
            project_out(b, p - 1)
            gate_or_up(1, 1, 1, 0, 0)
            times_v(b, p)
            gate_or_up(1, 1, 1, 0, 1)
            coef_rows(1, 1, 0)
            project_out(b, p)
            down(0, 0, 0, True)
            gate_or_up(2, 2, 2, 0, 0)
            pe.wait_ge(coefs_ok, BATCH)
            norm_transposes(norm2(b))
            gate_or_up(2, 2, 2, 0, 1)
            coef_rows(2, 2, 0)
            pe.wait_ge(h_ok, norm2(b) + 1)
            router_logits(b)
            down(1, 1, 0)
            gate_or_up(3, 3, 3, 0, 0)
            gate_or_up(3, 3, 3, 0, 1)
            pe.wait_ge(lt_out, BATCH)
            logit_transposes(b)
            coef_rows(3, 3, 0)
            down(2, 2, 0)
            gate_or_up(4, 0, 0, 1, 0)
            gate_or_up(4, 0, 0, 1, 1)
            down(3, 3, 0)
            pe.wait_ge(rexp_ok, BATCH)
            coef_transposes(b)
            pe.wait_ge(coefs_ok, 1 + BATCH)
            coef_rows(4, 0, 1)
            pe.wait_ge(y_read, BATCH)
            for s in range(EARLY + 1, 2 * EARLY):
                step(s, s - EARLY, s - EARLY, 1)
                down(s - 1, s - 1 - EARLY, 1, s == EARLY + 1)

            def chunk_pair(i):
                for slot in range(2):
                    for half in range(2):
                        at = 2 * slot + half
                        step(4 * i + at, 2 * i + slot, slot, half)
                        if at > 0:
                            down(4 * i + at - 1, (at - 1) // 2, (at - 1) % 2)
                        else:
                            down(4 * i - 1, 1, 1)

            i = FFN_RING // 2
            for at in range(4):
                step(4 * i + at, 2 * i + at // 2, at // 2, at % 2)
                if at > 0:
                    down(4 * i + at - 1, (at - 1) // 2, (at - 1) % 2)
                else:
                    down(4 * i - 1, FFN_RING - 1, 1)
            with pe.Fori(FFN_RING // 2 + 1, CHUNKS // 2) as i:
                chunk_pair(i)
            down(2 * CHUNKS - 1, 1, 1)

        @block.scalar
        def _(act):
            nc.scalar.preload_act_table(ACT.Exp)

            def h_split(l, b):
                act.wait_ge(h_ok, l + 1)
                nc.scalar.activation(hT[:, 0, :, bass.ds(b * SEQ, SEQ)], hbuf[:, :, :], ACT.Copy).then_inc(h_hi, 1)

            def split_hi(i):
                act.wait_ge(raw_in[i % RAW], 16 * (i // RAW + 1))
                nc.scalar.activation(splits[i][1][:, 0], raw_piece(i), ACT.Copy).then_inc(hi_split, 1)

            def rotate_q(b, p):
                u, r = UNITS * b + p, p % 2
                act.wait_ge(q_ok, u + 1)
                if not (isinstance(b, int) and b == 0 and p < 2):
                    act.wait_ge(q_lo, u - 1)
                nc.scalar.activation(rot[0:64, r], q_ps[64:128, :, :], ACT.Copy)
                nc.scalar.activation(rot[64:128, r], q_ps[0:64, :, :], ACT.Copy).then_inc(q_rot, 1)

            def rotate_k(b, g):
                n = KV * b + g
                act.wait_ge(k_ok, n + 1)
                if not (isinstance(b, int) and b == 0 and g == 0):
                    act.wait_ge(k_lo, n)
                nc.scalar.activation(krot[0:64, :], misc[64:128, 0:SEQ], ACT.Copy)
                nc.scalar.activation(krot[64:128, :], misc[0:64, 0:SEQ], ACT.Copy).then_inc(k_rot, 1)

            def exps(b, p):
                u, r = UNITS * b + p, p % 2
                act.wait_ge(max_ok, u + 1)
                if not (isinstance(b, int) and b == 0 and p < 2):
                    act.wait_ge(pT_ok, u - 1)
                    act.wait_ge(rsum_ok, u - 1)
                for j in range(2):
                    at = 3 * j * P
                    nc.scalar.activation(prob[:, r, at:at + P], s0_ps[:, j, :], ACT.Exp, bias=nmax[:, r, 0, j:j + 1],
                                         accum_out=sums[:, r, j, 0:1])
                    e = nc.scalar.activation(prob[:, r, at + P:at + 3 * P], s1_ps[:, j, :], ACT.Exp, bias=nmax[:, r, 1, j:j + 1],
                                             accum_out=sums[:, r, j, 1:2])
                e.then_inc(exp_ok, 1)

            def pT_split(b, p):
                u = UNITS * b + p
                act.wait_ge(pT_ok, u + 1)
                if not (isinstance(b, int) and b == 0 and p == 0):
                    act.wait_ge(o_ok, u)
                nc.scalar.activation(pT[:, 0, 0:2 * SEQ], bank[4][:, :], ACT.Copy).then_inc(pT_hi, 1)
                nc.scalar.activation(pT[:, 0, 2 * SEQ:], bank[5][:, 0:2 * P], ACT.Copy).then_inc(pT_hi, 1)

            def o_split(b, p):
                u = UNITS * b + p
                act.wait_ge(o_ok, u + 1)
                if not (isinstance(b, int) and b == 0 and p == 0):
                    act.wait_ge(d_ok, u)
                nc.scalar.activation(oT[:, 0], o_ps[:, :, :], ACT.Copy).then_inc(o_hi, 1)

            def v_split(b, t):
                act.wait_ge(v_ok, NT * b + t + 1)
                if t == 0 and not (isinstance(b, int) and b == 0):
                    act.wait_ge(o_ok, UNITS * b)
                nc.scalar.activation(v[:, 0, t, :], misc[:, :], ACT.Copy).then_inc(v_hi, 1)

            def router_exps(b):
                act.wait_ge(rmax_ok, b + 1)
                lg = misc[:, 0:NT * P].rearrange("p (t n) -> p t n", t=NT)
                for t in range(NT):
                    nc.scalar.activation(rexp[:, t, :], lg[:, t, 0:EXPERTS], ACT.Exp, bias=rmax[:, t:t + 1], accum_out=rtot[:, 0, t:t + 1])
                nc.scalar.activation(sg[:, 0], lg[:, :, EXPERTS:GATES], ACT.Exp, scale=-1.0).then_inc(rexp_ok, 1)

            def rows_copy(b):
                act.wait_ge(mod_rows, b + 1)
                nc.scalar.activation(gates[:, b].rearrange("p j n -> p (j n)"), misc[:, :], ACT.Copy).then_inc(rows_out, 1)

            act.wait_ge(in_c, 16)
            nc.scalar.activation(ce[:, 0], cT[:, :, :], ACT.Exp, scale=-1.0).then_inc(c_step, 1)
            split_hi(0)
            split_hi(1)
            h_split(0, 0)
            split_hi(2)
            rotate_k(0, 0)
            rotate_q(0, 0)
            split_hi(3)
            rotate_q(0, 1)
            exps(0, 0)
            rotate_k(0, 1)
            rotate_q(0, 2)

            def batch(b, first, last):
                for p in range(UNITS):
                    if p == 0:
                        v_split(b, 0)
                    if not first and p == 3:
                        h_split(norm2(b - 1), b - 1)
                    if not first and p == 5:
                        router_exps(b - 1)
                    if last and p == UNITS - 1:
                        nc.scalar.preload_act_table(ACT.Silu)
                        silu_of(0, 0)
                    pT_split(b, p)
                    if first and p in (2, 6):
                        rows_copy({2: 0, 6: 2}[p])
                    if not last and p == 4:
                        h_split(norm1(b + 1), b + 1)
                    if last and p == 6:
                        for slot in range(2, FFN_RING):
                            weights_hi(0, slot, True)
                    if p < UNITS - 1:
                        exps(b, p + 1)
                    elif not last:
                        exps(b + 1, 0)
                    if p == 0:
                        v_split(b, 1)
                    ahead = p + LOOKAHEAD
                    if ahead < UNITS or not last:
                        ab, ap = (b, ahead) if ahead < UNITS else (b + 1, ahead - UNITS)
                        if ap % 2 == 0:
                            rotate_k(ab, ap // 2)
                        rotate_q(ab, ap)
                    elif p == UNITS - LOOKAHEAD:
                        for slot in range(2):
                            weights_hi(0, slot, True)
                    if last and p == UNITS - 1:
                        break
                    if first and p == 0:
                        split_hi(4)
                    if first and p == 1:
                        split_hi(6)
                    if first and p in (0, 1, 3, 4):
                        split_hi({0: 5, 1: 7, 3: 8, 4: 9}[p])
                    o_split(b, p)
                    if first and p in (4, 6):
                        rows_copy({4: 1, 6: 3}[p])

            def weights_hi(i, slot, first):
                if first:
                    act.wait_ge(w_in[slot], 32)
                    act.wait_ge(q_ok, UNITS * BATCH)
                else:
                    act.wait_ge(w_in[slot], 32 * i)
                    act.wait_ge(down_ok, 4 * i - 2 + 2 * slot)
                nc.scalar.activation(gu_at[slot][:, 0:512], raw[:, slot, 0:512], ACT.Copy)
                nc.scalar.activation(w_dn[:, slot, 0], raw[:, slot, 512:768], ACT.Copy).then_inc(w_hi, 1)

            def silu_of(s, half):
                act.wait_ge(g_ok, s + 1)
                if not (isinstance(s, int) and s < 2):
                    act.wait_ge(prod_ok, s - 1)
                nc.scalar.activation(silu[s_ring(s, half)], g_ps[:, :], ACT.Silu).then_inc(silu_ok, 1)

            def act_hi(s, half):
                act.wait_ge(scaled_ok, s + 1)
                if not (isinstance(s, int) and s < 2):
                    act.wait_ge(down_ok, s - 1)
                nc.scalar.activation(actT[:, s_ring(s, half), 0, :], scaled[s_ring(s, half)], ACT.Copy).then_inc(a_hi, 1)

            batch(0, True, False)
            with act.Fori(1, BATCH - 1) as b:
                batch(b, False, False)
            batch(BATCH - 1, False, True)

            b, p = BATCH - 1, UNITS - 1
            act_hi(0, 0)
            o_split(b, p)
            silu_of(1, 0)
            act_hi(1, 0)
            h_split(norm2(b), b)
            silu_of(2, 0)
            act_hi(2, 0)
            silu_of(3, 0)
            nc.scalar.preload_act_table(ACT.Exp)
            router_exps(b)
            nc.scalar.preload_act_table(ACT.Silu)
            act_hi(3, 0)
            for s in range(EARLY, 2 * EARLY):
                silu_of(s, 1)
                act_hi(s, 1)
                if s == 2 * EARLY - 2:
                    weights_hi(FFN_RING // 2, 0, False)

            def chunk_pair(i, last):
                for slot in range(2):
                    for half in range(2):
                        at = 2 * slot + half
                        silu_of(4 * i + at, half)
                        act_hi(4 * i + at, half)
                        if at == 2 and not last:
                            weights_hi(i + 1, 0, False)
                        if at == 0:
                            weights_hi(i, 1, False)

            with act.Fori(FFN_RING // 2, CHUNKS // 2 - 1) as i:
                chunk_pair(i, False)
            chunk_pair(CHUNKS // 2 - 1, True)

        @block.vector
        def _(dve):
            def norm_stats(l, b):
                for t in range(NT):
                    i = nc.vector.bn_stats(stats[:, t, :], xs[:, bass.ds(b, 1), t, :].rearrange("p a n -> p (a n)"))
                i.then_inc(ln_step, 1)
                dve.wait_ge(ln_step, 3 * l + 1)
                nc.vector.memset(ve[:, :], EPS)
                for t in range(NT):
                    i = nc.vector.bn_aggr(mv[:, t, :], stats[:, t, :])
                i.then_inc(ln_step, 1)
                dve.wait_ge(ln_step, 3 * l + 2)
                nc.vector.tensor_tensor(ve[:, :], mv[:, :, 1], ve[:, :], ALU.add).then_inc(ln_step, 1)

            def normalize(l, b):
                dve.wait_ge(rstd_ok, l + 1)
                if not (isinstance(l, int) and l == 0):
                    dve.wait_ge(zT_ok, l)
                for t in range(NT):
                    i = nc.vector.tensor_scalar(z[:, t, :], xs[:, bass.ds(b, 1), t, :].rearrange("p a n -> p (a n)"),
                                                mv[:, t, 0:1], rstd[:, t:t + 1], ALU.subtract, ALU.mult)
                i.then_inc(z_ok, 1)

            def modulate(l, b, shift):
                dve.wait_ge(zT_ok, l + 1)
                if not (isinstance(l, int) and l == 0):
                    dve.wait_ge(h_lo, l)
                zT = misc[:, :].rearrange("p (c n) -> p c n", c=KC)
                for c in range(KC):
                    i = nc.vector.tensor_scalar(hbuf[:, c, :], zT[:, c, :], modc[:, shift + 1, c, bass.ds(b, 1)],
                                                modc[:, shift, c, bass.ds(b, 1)], ALU.mult, ALU.add)
                i.then_inc(h_ok, 1)

            def h_rest(l, b):
                dve.wait_ge(h_hi, l + 1)
                at = bass.ds(b * SEQ, SEQ)
                nc.vector.tensor_tensor(hT[:, 1, :, at], hbuf[:, :, :], hT[:, 0, :, at].bitcast(F32), ALU.subtract).then_inc(h_lo, 1)

            def split_lo(i):
                dve.wait_ge(hi_split, i + 1)
                nc.vector.tensor_tensor(splits[i][1][:, 1], raw_piece(i), splits[i][1][:, 0].bitcast(F32), ALU.subtract).then_inc(lo_even, 1)

            def q_times_cos(b, p):
                u, r = UNITS * b + p, p % 2
                dve.wait_ge(q_rot, u + 1)
                if not (isinstance(b, int) and b == 0 and p < 2):
                    dve.wait_ge(q_add, u - 1)
                nc.vector.tensor_tensor(qcos[:, r], q_ps[:, :, :], cosT[:, :].unsqueeze(1).to_broadcast([P, 2, SEQ]), ALU.mult).then_inc(q_cos, 1)

            def k_times_cos(b, g):
                n = KV * b + g
                dve.wait_ge(k_rot, n + 1)
                if not (isinstance(b, int) and b == 0 and g == 0):
                    dve.wait_ge(k_lo, n)
                nc.vector.tensor_tensor(kcos, misc[:, 0:SEQ], cosT[:, :], ALU.mult).then_inc(k_cos, 1)

            def q_split(b, p):
                u, r = UNITS * b + p, p % 2
                dve.wait_ge(q_add, u + 1)
                if not (isinstance(b, int) and b == 0 and p < 2):
                    dve.wait_ge(s_ok, u - 1)
                nc.vector.tensor_copy(qT[:, r, 0], rot[:, r]).then_inc(q_hi, 1)
                dve.wait_ge(q_hi, u + 1)
                nc.vector.tensor_tensor(qT[:, r, 1], rot[:, r], qT[:, r, 0].bitcast(F32), ALU.subtract).then_inc(q_lo, 1)

            def k_split(b, g):
                n, r = KV * b + g, g % 2
                dve.wait_ge(k_add, n + 1)
                if not (isinstance(b, int) and b == 0 and g < 2):
                    dve.wait_ge(s_ok, 2 * n - 2)
                nc.vector.tensor_copy(kT[:, r, 0, :], krot).then_inc(k_hi, 1)
                dve.wait_ge(k_hi, n + 1)
                nc.vector.tensor_tensor(kT[:, r, 1, :], krot, kT[:, r, 0, :].bitcast(F32), ALU.subtract).then_inc(k_lo, 1)

            def maxima(b, p):
                u, r = UNITS * b + p, p % 2
                dve.wait_ge(s_ok, u + 1)
                if not (isinstance(b, int) and b == 0 and p < 2):
                    dve.wait_ge(exp_ok, u - 1)
                nc.vector.tensor_reduce(nmax[:, r, 0, :], s0_ps[:, :, :], AX_X, ALU.max, negate=True)
                nc.vector.tensor_reduce(nmax[:, r, 1, :], s1_ps[:, :, :], AX_X, ALU.max, negate=True).then_inc(max_ok, 1)

            def reciprocals(b, p):
                u, r = UNITS * b + p, p % 2
                dve.wait_ge(exp_ok, u + 1)
                if not (isinstance(b, int) and b == 0 and p < 2):
                    dve.wait_ge(norm_ok, u - 1)
                nc.vector.reciprocal(rsum[:, r, :, 0:1], sums[:, r, :, 0:1])
                nc.vector.reciprocal(rsum[:, r, :, 1:3], sums[:, r, :, 1:2].to_broadcast([P, 2, 2])).then_inc(rsum_ok, 1)

            def pT_rest(b, p):
                u = UNITS * b + p
                for n, (lo, hi, bk) in enumerate(((0, 2 * SEQ, 4), (2 * SEQ, 2 * SEQ + 2 * P, 5))):
                    dve.wait_ge(pT_hi, 2 * u + n + 1)
                    i = nc.vector.tensor_tensor(pT[:, 1, lo:hi], bank[bk][:, 0:hi - lo], pT[:, 0, lo:hi].bitcast(F32), ALU.subtract)
                i.then_inc(pT_lo, 1)

            def o_rest(b, p):
                u = UNITS * b + p
                dve.wait_ge(o_hi, u + 1)
                nc.vector.tensor_tensor(oT[:, 1], o_ps[:, :, :], oT[:, 0].bitcast(F32), ALU.subtract).then_inc(o_lo, 1)

            def v_rest(b, t):
                dve.wait_ge(v_hi, NT * b + t + 1)
                nc.vector.tensor_tensor(v[:, 1, t, :], misc[:, :], v[:, 0, t, :].bitcast(F32), ALU.subtract).then_inc(v_lo, 1)

            def clamp_gates():
                dve.wait_ge(mod_cols, 2)
                for j in range(2):
                    nc.vector.tensor_scalar(modc[:, 2 + j], mod_ps[1][:, j], float(j), None, ALU.add)
                nc.vector.tensor_copy(gate_cols[:, :, :, :], mod_ps[1][:, 2:4].rearrange("p j k b -> p b j k")).then_inc(cols_out, 1)
                g, sign = gate_cols[:, :, :, :], gate_sign[:, :, :, :]
                dve.wait_ge(cols_out, 2)
                nc.vector.tensor_scalar(sign, g, 0.0, 2.0, ALU.is_ge, ALU.mult).then_inc(gates_step, 1)
                dve.wait_ge(gates_step, 1)
                nc.vector.tensor_scalar(sign, sign, -1.0, None, ALU.add).then_inc(gates_step, 1)
                dve.wait_ge(gates_step, 2)
                nc.vector.tensor_tensor(g, g, sign, ALU.mult).then_inc(gates_step, 1)
                dve.wait_ge(gates_step, 3)
                nc.vector.scalar_tensor_tensor(g, g, 0.25, sign, ALU.max, ALU.mult).then_inc(gates_step, 1)

            def gate_y(b):
                dve.wait_ge(d_ok, UNITS * (b + 1))
                if not (isinstance(b, int) and b == 0):
                    dve.wait_ge(x1_ok, b)
                ga = gates[:, bass.ds(b, 1), 0, :].to_broadcast([P, NT, HID])
                nc.vector.tensor_tensor(ybuf[:, :, :], y_ps[:, :, :], ga, ALU.mult).then_inc(y_read, 1)

            def logits_out(b):
                dve.wait_ge(lt_ok, b + 1)
                if not (isinstance(b, int) and b == 0):
                    dve.wait_ge(l_ok, b)
                nc.vector.tensor_copy(lt[0:GW, :], misc[0:GW, 0:SEQ]).then_inc(lt_out, 1)

            def router_max(b):
                dve.wait_ge(l_ok, b + 1)
                lg = misc[:, 0:NT * P].rearrange("p (t n) -> p t n", t=NT)
                nc.vector.tensor_reduce(rmax[:, :], lg[:, :, 0:EXPERTS], AX_X, ALU.max, negate=True).then_inc(rmax_ok, 1)

            ROUTING_STEPS, PIECES_STEPS = 6, 5

            def counter(done):
                count = [0]

                def after_it(i):
                    i.then_inc(r_step, 1)
                    count[0] += 1
                    dve.wait_ge(r_step, done + count[0])
                return after_it

            def routing(b):
                after_it = counter((ROUTING_STEPS + PIECES_STEPS) * b)
                dve.wait_ge(rexp_ok, b + 1)
                after_it(nc.vector.reciprocal(rtot[:, 1, :], rtot[:, 0, :]))
                for t in range(NT):
                    i = nc.vector.tensor_scalar(probs20[:, t, 0:EXPERTS], rexp[:, t, :], rtot[:, 1, t:t + 1], None, ALU.mult)
                after_it(i)
                nc.vector.tensor_scalar(sg[:, 1], sg[:, 0], 1.0, None, ALU.add)
                for t in range(NT):
                    i = nc.vector.max(top8[:, t, :], probs20[:, t, 0:EXPERTS])
                after_it(i)
                after_it(nc.vector.memset(top8[:, :, TOP_K:8], SENTINEL))
                nc.vector.reciprocal(coef[:, :, EXPERTS:GATES], sg[:, 1])
                for t in range(NT):
                    i = nc.vector.match_replace(left20[:, t, :], top8[:, t, :], probs20[:, t, :], -1.0)
                after_it(i)
                after_it(nc.vector.scalar_tensor_tensor(coef[:, :, 0:EXPERTS], left20[:, :, 0:EXPERTS], 0.0, probs20[:, :, 0:EXPERTS],
                                                        ALU.is_lt, ALU.mult))

            def coef_pieces(b):
                after_it = counter((ROUTING_STEPS + PIECES_STEPS) * b + ROUTING_STEPS)
                after_it(nc.vector.tensor_copy(piece[:, 0], coef[:, :, :]))
                if not (isinstance(b, int) and b == 0):
                    dve.wait_ge(cT_ok, b)
                nc.vector.tensor_copy(pieces[:, :, 0, 0:GATES], piece[:, 0])
                after_it(nc.vector.tensor_tensor(rest[:, 0], coef[:, :, :], piece[:, 0], ALU.subtract))
                after_it(nc.vector.tensor_copy(piece[:, 1], rest[:, 0]))
                nc.vector.tensor_copy(pieces[:, :, 1, 0:GATES], piece[:, 1])
                after_it(nc.vector.tensor_tensor(rest[:, 1], rest[:, 0], piece[:, 1], ALU.subtract))
                after_it(nc.vector.tensor_copy(piece[:, 0], rest[:, 1]))
                nc.vector.tensor_copy(pieces[:, :, 2, 0:GATES], piece[:, 0]).then_inc(pieces_ok, 1)

            def coefs_out(b):
                dve.wait_ge(cT_ok, b + 1)
                nc.vector.tensor_copy(coefT[:, bass.ds(b * SEQ, SEQ)], misc[0:3 * GW, 0:SEQ]).then_inc(coefs_ok, 1)

            def product(s, half):
                r = s_ring(s, half)
                dve.wait_ge(silu_ok, s + 1)
                dve.wait_ge(u_ok, s + 1)
                if not (isinstance(s, int) and s < 2):
                    dve.wait_ge(scaled_ok, s - 1)
                nc.vector.tensor_tensor(prod[r], u_ps[:, :], silu[r], ALU.mult).then_inc(prod_ok, 1)

            def scale(s, half):
                r = s_ring(s, half)
                dve.wait_ge(prod_ok, s + 1)
                dve.wait_ge(c_ok, s + 1)
                if not (isinstance(s, int) and s < 2):
                    dve.wait_ge(a_lo, s - 1)
                nc.vector.tensor_tensor(scaled[r], c_ps[:, :], prod[r], ALU.mult).then_inc(scaled_ok, 1)

            def act_rest(s, half):
                r = s_ring(s, half)
                dve.wait_ge(a_hi, s + 1)
                nc.vector.tensor_tensor(actT[:, r, 1, :], scaled[r], actT[:, r, 0, :].bitcast(F32), ALU.subtract).then_inc(a_lo, 1)

            nc.vector.memset(ones[:, :], 1.0)
            nc.vector.memset(pieces[:, :, :, :], 0.0)
            nc.vector.memset(lt[:, :], 0.0)
            nc.vector.memset(probs20[:, :, EXPERTS:EXPERTS + 4], SENTINEL).then_inc(coefs_ok, 1)
            dve.wait_ge(c_step, 1)
            nc.vector.tensor_scalar(ce[:, 1], ce[:, 0], 1.0, None, ALU.add).then_inc(c_step, 1)
            dve.wait_ge(c_step, 2)
            nc.vector.reciprocal(ce[:, 0], ce[:, 1]).then_inc(c_step, 1)
            dve.wait_ge(c_step, 3)
            nc.vector.tensor_tensor(ce[:, 2], ce[:, 0], cT[:, :, :], ALU.mult).then_inc(c_step, 1)
            dve.wait_ge(in_x, 16)
            norm_stats(0, 0)
            normalize(0, 0)
            split_lo(0)
            dve.wait_ge(mod_cols, 1)
            for j in range(2):
                i = nc.vector.tensor_scalar(modc[:, j], mod_ps[0][:, j], float(j), None, ALU.add)
            i.then_inc(cols_out, 1)
            dve.wait_ge(cols_out, 1)
            modulate(0, 0, 0)
            h_rest(0, 0)
            dve.wait_ge(in_ident, 16)
            nc.vector.tensor_copy(ident_bf[:, :], ident[:, :]).then_inc(consts, 2)
            split_lo(2)
            dve.wait_ge(in_rope, 32)
            k_times_cos(0, 0)
            q_times_cos(0, 0)
            k_split(0, 0)
            q_split(0, 0)
            q_times_cos(0, 1)
            maxima(0, 0)
            k_times_cos(0, 1)
            q_split(0, 1)
            reciprocals(0, 0)
            k_split(0, 1)
            q_times_cos(0, 2)

            def batch(b, first, last):
                for p in range(UNITS):
                    if p > 0:
                        o_rest(b, p - 1)
                    elif not first:
                        o_rest(b - 1, UNITS - 1)
                    if not first and p == 3:
                        h_rest(norm2(b - 1), b - 1)
                    if not first and p == 5:
                        logits_out(b - 1)
                    if p < UNITS - 1:
                        maxima(b, p + 1)
                    elif not last:
                        maxima(b + 1, 0)
                    if p == 0:
                        v_rest(b, 0)
                    if not first and p == 5:
                        router_max(b - 1)
                    if last and p == UNITS - 1:
                        product(0, 0)
                    pT_rest(b, p)
                    if not first and p == 2:
                        normalize(norm2(b - 1), b - 1)
                    if not last and p == 3:
                        normalize(norm1(b + 1), b + 1)
                    if not last and p == 4:
                        modulate(norm1(b + 1), b + 1, 0)
                    if not first and p == 7:
                        coefs_out(b - 1)
                    ahead = p + LOOKAHEAD - 1
                    if ahead < UNITS or not last:
                        ab, ap = (b, ahead) if ahead < UNITS else (b + 1, ahead - UNITS)
                        if ap % 2 == 0 and not (first and p == 0):
                            k_split(ab, ap // 2)
                        q_split(ab, ap)
                    if not last and p == 4:
                        h_rest(norm1(b + 1), b + 1)
                    if last and p == UNITS - 1:
                        scale(0, 0)
                        break
                    if p < UNITS - 1:
                        reciprocals(b, p + 1)
                    else:
                        reciprocals(b + 1, 0)
                    if p == 0:
                        v_rest(b, 1)
                    ahead = p + LOOKAHEAD
                    if ahead < UNITS or not last:
                        ab, ap = (b, ahead) if ahead < UNITS else (b + 1, ahead - UNITS)
                        if ap % 2 == 0:
                            k_times_cos(ab, ap // 2)
                        q_times_cos(ab, ap)
                    if first and p in (0, 1, 3):
                        split_lo(4 + 2 * ((p + 1) // 2))
                    if first and p == 0:
                        clamp_gates()
                    if first and p == 1:
                        dve.wait_ge(in_gw, 16)
                        nc.vector.tensor_copy(gw[:, 0], gw_raw[:, :, :]).then_inc(gw_split, 1)
                        dve.wait_ge(gw_split, 1)
                        nc.vector.tensor_tensor(gw[:, 1], gw_raw[:, :, :], gw[:, 0].bitcast(F32), ALU.subtract)
                    if not first and p == 0:
                        gate_y(b - 1)
                    if not first and p == 1:
                        dve.wait_ge(x1_ok, b)
                        norm_stats(norm2(b - 1), b - 1)
                    if not first and p == 2:
                        modulate(norm2(b - 1), b - 1, 2)
                    if not last and p == 2:
                        if first:
                            dve.wait_ge(in_x_rest, 16)
                        norm_stats(norm1(b + 1), b + 1)
                    if not first and p == 5:
                        routing(b - 1)
                    if not first and p == 6:
                        coef_pieces(b - 1)

            batch(0, True, False)
            with dve.Fori(1, BATCH - 1) as b:
                batch(b, False, False)
            batch(BATCH - 1, False, True)

            def product(s, half):
                r = s_ring(s, half)
                dve.wait_ge(silu_ok, s + 1)
                dve.wait_ge(u_ok, s + 1)
                if not (isinstance(s, int) and s < 2):
                    dve.wait_ge(scaled_ok, s - 1)
                nc.vector.tensor_tensor(prod[r], u_ps[:, :], silu[r], ALU.mult).then_inc(prod_ok, 1)

            def scale(s, half):
                r = s_ring(s, half)
                dve.wait_ge(prod_ok, s + 1)
                dve.wait_ge(c_ok, s + 1)
                if not (isinstance(s, int) and s < 2):
                    dve.wait_ge(a_lo, s - 1)
                nc.vector.tensor_tensor(scaled[r], c_ps[:, :], prod[r], ALU.mult).then_inc(scaled_ok, 1)

            def act_rest(s, half):
                r = s_ring(s, half)
                dve.wait_ge(a_hi, s + 1)
                nc.vector.tensor_tensor(actT[:, r, 1, :], scaled[r], actT[:, r, 0, :].bitcast(F32), ALU.subtract).then_inc(a_lo, 1)

            b = BATCH - 1
            act_rest(0, 0)
            o_rest(b, UNITS - 1)
            gate_y(b)
            dve.wait_ge(x1_ok, BATCH)
            norm_stats(norm2(b), b)
            product(1, 0)
            normalize(norm2(b), b)
            scale(1, 0)
            act_rest(1, 0)
            modulate(norm2(b), b, 2)
            h_rest(norm2(b), b)
            product(2, 0)
            scale(2, 0)
            logits_out(b)
            act_rest(2, 0)
            product(3, 0)
            router_max(b)
            scale(3, 0)
            act_rest(3, 0)
            routing(b)
            coef_pieces(b)
            product(4, 1)
            coefs_out(b)
            scale(4, 1)
            act_rest(4, 1)
            for s in range(EARLY + 1, 2 * EARLY):
                product(s, 1)
                scale(s, 1)
                act_rest(s, 1)

            with dve.Fori(FFN_RING // 2, CHUNKS // 2) as i:
                for at in range(4):
                    product(4 * i + at, at % 2)
                    scale(4 * i + at, at % 2)
                    act_rest(4 * i + at, at % 2)
            for b in range(BATCH):
                dve.wait_ge(down_ok, 2 * CHUNKS - 1 + b // 2)
                nc.vector.tensor_tensor(z[:, :, :] if b % 2 else ybuf[:, :, :], y2_ps[b],
                                        gates[:, b, 1, :].unsqueeze(1).to_broadcast([P, NT, HID]), ALU.mult).then_inc(yg_ok, 1)
                dve.wait_ge(yg_ok, b + 1)
                nc.vector.tensor_tensor(xs[:, b], z[:, :, :] if b % 2 else ybuf[:, :, :], xs[:, b], ALU.add).then_inc(x2_ok, 1)

        @block.gpsimd
        def _(pool):
            def power(l):
                pool.wait_ge(ln_step, 3 * l + 3)
                if not (isinstance(l, int) and l == 0):
                    pool.wait_ge(z_ok, l)
                nc.gpsimd.tensor_tensor(rstd[:, :], ve[:, :], neg_half[:, :], ALU.pow).then_inc(rstd_ok, 1)

            def split_lo(i):
                pool.wait_ge(hi_split, i + 1)
                nc.gpsimd.tensor_tensor(splits[i][1][:, 1], raw_piece(i), splits[i][1][:, 0].bitcast(F32), ALU.subtract).then_inc(lo_odd, 1)

            def q_rope(b, p):
                u, r = UNITS * b + p, p % 2
                pool.wait_ge(q_rot, u + 1)
                nc.gpsimd.tensor_tensor(rot[:, r], rot[:, r], sinT[:, :].unsqueeze(1).to_broadcast([P, 2, SEQ]), ALU.mult).then_inc(q_sin, 1)
                pool.wait_ge(q_sin, u + 1)
                pool.wait_ge(q_cos, u + 1)
                nc.gpsimd.tensor_tensor(rot[:, r], rot[:, r], qcos[:, r], ALU.add).then_inc(q_add, 1)

            def k_rope(b, g):
                n = KV * b + g
                pool.wait_ge(k_rot, n + 1)
                nc.gpsimd.tensor_tensor(krot, krot, sinT[:, :], ALU.mult).then_inc(k_sin, 1)
                pool.wait_ge(k_sin, n + 1)
                pool.wait_ge(k_cos, n + 1)
                nc.gpsimd.tensor_tensor(krot, krot, kcos, ALU.add).then_inc(k_add, 1)

            def norm_probs(b, p):
                u, r = UNITS * b + p, p % 2
                pool.wait_ge(rsum_ok, u + 1)
                e = prob[:, r, :].rearrange("p (k n) -> p k n", k=6)
                by = rsum[:, r].rearrange("p h k -> p (h k)").unsqueeze(2).to_broadcast([P, 6, P])
                nc.gpsimd.tensor_tensor(e, e, by, ALU.mult).then_inc(norm_ok, 1)

            def add_x(b):
                pool.wait_ge(y_read, b + 1)
                at = xs[:, bass.ds(b, 1)].rearrange("p a t n -> p (a t) n")
                nc.gpsimd.tensor_tensor(at, at, ybuf[:, :, :], ALU.add).then_inc(x1_ok, 1)

            def h_copy(b):
                pool.wait_ge(h_lo, norm1(b) + 1)
                pool.wait_ge(v_ok, NT * b)
                for s in range(2):
                    i = nc.gpsimd.tensor_copy(h_stat[:, s], hT[:, s, :, bass.ds(b * SEQ, SEQ)])
                i.then_inc(h_stat_ok, 1)

            def gate_diagonals(b):
                if b == 0:
                    pool.wait_ge(gates_step, 4)
                else:
                    pool.wait_ge(mod_rows, b)
                nc.gpsimd.tensor_tensor(ybuf[:, :, :].rearrange("p t (c n) -> p (t c) n", c=KC), ident[:, :].unsqueeze(1).to_broadcast([P, 2 * KC, P]),
                                        gate_cols[:, b].rearrange("p j k -> p (j k)").unsqueeze(2).to_broadcast([P, 2 * KC, P]), ALU.mult).then_inc(diag_ok, 1)

            nc.gpsimd.memset(neg_half[:, :], -0.5).then_inc(half_ok, 1)
            pool.wait_ge(half_ok, 1)
            power(0)
            split_lo(1)
            pool.wait_ge(in_rope, 32)
            k_rope(0, 0)
            q_rope(0, 0)
            split_lo(3)
            q_rope(0, 1)
            norm_probs(0, 0)
            k_rope(0, 1)
            q_rope(0, 2)

            def batch(b, first, last):
                for p in range(UNITS):
                    if not first and p == 1:
                        add_x(b - 1)
                    if first and p in (2, 5):
                        split_lo(7 if p == 2 else 9)
                    if first and p in (1, 3, 5, 6):
                        gate_diagonals({1: 0, 3: 1, 5: 2, 6: 3}[p])
                    if not first and p == 2:
                        power(norm2(b - 1))
                    if not last and p == 3:
                        power(norm1(b + 1))
                    if p < UNITS - 1:
                        norm_probs(b, p + 1)
                    elif not last:
                        norm_probs(b + 1, 0)
                    ahead = p + LOOKAHEAD
                    if ahead < UNITS or not last:
                        ab, ap = (b, ahead) if ahead < UNITS else (b + 1, ahead - UNITS)
                        if ap % 2 == 0:
                            k_rope(ab, ap // 2)
                        q_rope(ab, ap)
                    else:
                        weights_lo(0, p - UNITS + LOOKAHEAD, True)
                    if first and p == 0:
                        split_lo(5)
                    if not last and p == 5:
                        h_copy(b + 1)

            def weights_lo(i, slot, first):
                pool.wait_ge(w_hi, 2 * i + slot + 1)
                nc.gpsimd.tensor_tensor(gu_at[slot][:, 512:1024], raw[:, slot, 0:512], gu_at[slot][:, 0:512].bitcast(F32), ALU.subtract)
                nc.gpsimd.tensor_tensor(w_dn[:, slot, 1], raw[:, slot, 512:768], w_dn[:, slot, 0].bitcast(F32), ALU.subtract).then_inc(w_lo, 1)

            batch(0, True, False)
            with pool.Fori(1, BATCH - 1) as b:
                batch(b, False, False)
            batch(BATCH - 1, False, True)
            add_x(BATCH - 1)
            power(norm2(BATCH - 1))
            weights_lo(0, 3, True)
            with pool.Fori(FFN_RING // 2, CHUNKS // 2) as i:
                for slot in range(2):
                    weights_lo(i, slot, False)


def _constants(np):
    f = np.float32
    inv = f(1.0) / np.power(f(10000.0), np.arange(0, HD, 2, dtype=f) / f(HD)).astype(f)
    ang = np.arange(SEQ, dtype=f)[None, :] * inv[:, None]
    root = f(HD ** -0.25)
    cos = np.concatenate([np.cos(ang), np.cos(ang)]) * root
    sin = np.concatenate([-np.sin(ang), np.sin(ang)]) * root
    causal = np.tile(np.where(np.arange(P)[None, :] > np.arange(P)[:, None], f(MASKED), f(0)), (1, 2))
    select = np.zeros((3 * GW, CHUNKS * P), f)
    for n in range(EXPERTS * INNER + SHARED):
        e = min(n // INNER, EXPERTS)
        select[[e, GW + e, 2 * GW + e], n] = 1
    return cos.astype(f), sin.astype(f), np.eye(P, dtype=f), causal.astype(f), select


def kernel(**inputs):
    import numpy as np
    import ml_dtypes
    import concourse.bacc as bacc
    from concourse.bass_utils import run_bass_kernel_spmd

    i = {k[3:]: np.asarray(a) for k, a in inputs.items()}
    pad = CHUNKS * P - EXPERTS * INNER - SHARED

    def features(w, shared):
        rows = [w.reshape(EXPERTS * INNER, HID), shared, np.zeros((pad, HID), w.dtype)]
        return np.concatenate(rows).reshape(CHUNKS, P, HID)

    def as_stationary(w):
        return w.reshape(CHUNKS, P, KC, P).transpose(0, 3, 2, 1)

    gate = features(i["ffn_w13"][:, :INNER], i["ffn_shared_gate_up_w"][:SHARED])
    up = features(i["ffn_w13"][:, INNER:], i["ffn_shared_gate_up_w"][SHARED:])
    gate_up = np.stack([as_stationary(gate), as_stationary(up)], 3).reshape(CHUNKS, P, 2 * KC * P)
    down = features(i["ffn_w2"].transpose(0, 2, 1), i["ffn_shared_down_w"].T)
    router = np.zeros((HID, GW), np.float32)
    router[:, :EXPERTS] = i["ffn_gate_w"].T
    router[:, EXPERTS] = i["ffn_sgate_w"][0]
    c = i["c"].T.reshape(KC, P, BATCH).transpose(1, 0, 2).reshape(P, KC * BATCH)
    cos, sin, ident, causal, select = _constants(np)
    arrays = {
        "x_dram": i["attn_x"], "wq_dram": i["attn_Wq"], "wk_dram": i["attn_Wk"], "wv_dram": i["attn_Wv"],
        "wo_dram": i["attn_Wo"], "router_dram": router, "gate_up_dram": gate_up, "down_dram": down,
        "c_dram": c, "wmod_dram": i["wmod"], "cos_dram": cos, "sin_dram": sin, "ident_dram": ident,
        "causal_dram": causal.astype(ml_dtypes.bfloat16), "select_dram": select.astype(ml_dtypes.bfloat16),
    }
    arrays = {k: np.ascontiguousarray(a) for k, a in arrays.items()}
    nc = bacc.Bacc("TRN2", target_bir_lowering=False, num_devices=1)
    args = [nc.dram_tensor(k, a.shape, mybir.dt.from_np(a.dtype), kind="ExternalInput").ap() for k, a in arrays.items()]
    out = nc.dram_tensor("out_dram", (BATCH, SEQ, HID), F32, kind="ExternalOutput").ap()
    build(nc, *args, out)
    r = run_bass_kernel_spmd(nc, [arrays], core_ids=[0])
    return r.results[0]["out_dram"]
```

```python
from contextlib import ExitStack

import concourse.bass as bass
from concourse import mybir

F32 = mybir.dt.float32
F32R = mybir.dt.float32r
BF16 = mybir.dt.bfloat16
ACT = mybir.ActivationFunctionType
ALU = mybir.AluOpType
AX_X = mybir.AxisListType.X

P = 128
BATCH, SEQ, HID = 4, 256, 256
KC = HID // P
NT = SEQ // P
HEADS, KV, HD = 16, 4, 128
UNITS = HEADS // 2
EXPERTS, INNER, SHARED, TOP_K = 16, 176, 704, 4
CHUNKS = -(-(EXPERTS * INNER + SHARED) // P)
EXPERT_CHUNKS = EXPERTS * INNER // P
REST = (EXPERTS * INNER + SHARED) % P
HALF_CHUNK = CHUNKS - 2
assert EXPERTS * INNER % P == 0 and EXPERT_CHUNKS % 2 == 0 and CHUNKS % 2 == 0 and REST == P // 2
GATES = EXPERTS + 1
GW = 32
EPS = 1e-5
MASKED = -3.0e38
SENTINEL = -5.0
HALF = BATCH * SEQ // 2
RAW = 4
FFN_RING = 4
EARLY = 4
SPLITS = 10
LOOKAHEAD = 3


def build(nc, x_d, wq_d, wk_d, wv_d, wo_d, gate_d, up_d, down_d, c_d, wmod_d,
          cos_d, sin_d, ident_d, causal_d, select_d, out_d):
    with ExitStack() as ctx:
        def sb(name, shape, dt):
            return ctx.enter_context(nc.sbuf_tensor(name, shape, dt))

        def sem(name):
            return ctx.enter_context(nc.semaphore(name))

        wq = sb("wq", [P, 2, KC, HEADS * HD], F32R)
        wk = sb("wk", [P, 2, KC, KV * HD], F32R)
        wv = sb("wv", [P, 2, KC, KV * HD], F32R)
        wo = sb("wo", [P, 2, HEADS, HID], F32R)
        hT = sb("hT", [P, 2, KC, BATCH * SEQ], F32R)
        xs = sb("xs", [P, BATCH, NT, HID], F32)
        gates = sb("gates", [P, BATCH, 2, HID], F32)
        raw = sb("raw", [P, RAW, 1024], F32)
        h_stat = sb("h_stat", [P, 2, KC, SEQ], F32R)
        v = sb("v", [P, 2, NT, KV * HD], F32R)
        qT = sb("qT", [P, 2, 2, 2, SEQ], F32R)
        kT = sb("kT", [P, 2, 2, SEQ], F32R)
        pT = sb("pT", [P, 2, 2 * SEQ + 2 * P], F32R)
        oT = sb("oT", [P, 2, 2, SEQ], F32R)
        work = sb("work", [P, 3584], F32)
        prob = work[:, 0:1536].rearrange("p (r n) -> p r n", r=2)
        rot = work[:, 1536:2560].rearrange("p (r h n) -> p r h n", r=2, h=2)
        qcos = work[:, 2560:3584].rearrange("p (r h n) -> p r h n", r=2, h=2)
        kwork = sb("kwork", [P, 512], F32)
        krot = kwork[:, 0:256]
        kcos = kwork[:, 256:512]
        z = sb("z", [P, NT, HID], F32)
        hbuf = sb("hbuf", [P, KC, SEQ], F32)
        ybuf = sb("ybuf", [P, NT, HID], F32)
        cosT = sb("cosT", [P, SEQ], F32)
        sinT = sb("sinT", [P, SEQ], F32)
        ident = sb("ident", [P, P], F32)
        ident_bf = sb("ident_bf", [P, P], BF16)
        causal = sb("causal", [P, 2, P], BF16)
        select = sb("select", [3 * GW, (EXPERT_CHUNKS + 1) * P], BF16)
        coefT = sb("coefT", [3 * GW, BATCH * SEQ], BF16)
        gw = sb("gw", [P, 2, KC, GW], F32R)
        gw_raw = sb("gw_raw", [P, KC, GW], F32)
        wmod = [work[:, 0:KC * 2 * HID].rearrange("p (c n) -> p c n", c=KC),
                gates[:, :, :, :].rearrange("p b j n -> p (b j n)").rearrange("p (c n) -> p c n", c=KC)]
        cT = sb("cT", [P, KC, BATCH], F32)
        ce = sb("ce", [P, 3, KC, BATCH], F32)
        modc = sb("modc", [P, 4, KC, BATCH], F32)
        gate_cols = sb("gate_cols", [P, BATCH, 2, KC], F32)
        gate_sign = sb("gate_sign", [P, BATCH, 2, KC], F32)
        ones = sb("ones", [P, P], F32)
        stats = sb("stats", [P, BATCH + 1, NT, 6], F32)
        mv = sb("mv", [P, BATCH + 1, NT, 2], F32)
        ve = sb("ve", [P, BATCH + 1, NT], F32)
        rstd = sb("rstd", [P, BATCH + 1, NT], F32)
        neg_half = sb("neg_half", [P, BATCH + 1, NT], F32)
        nmax = sb("nmax", [P, 2, 2, 2], F32)
        sums = sb("sums", [P, 2, 2, 2], F32)
        rsum = sb("rsum", [P, 2, 2, 3], F32)
        lt = sb("lt", [P, SEQ], F32)
        rmax = sb("rmax", [P, NT], F32)
        rexp = sb("rexp", [P, NT, EXPERTS], F32)
        rtot = sb("rtot", [P, 2, NT], F32)
        sg = sb("sg", [P, 2, NT, 1], F32)
        probs20 = sb("probs20", [P, NT, EXPERTS + 4], F32)
        top8 = sb("top8", [P, NT, 8], F32)
        left20 = sb("left20", [P, NT, EXPERTS + 4], F32)
        coef = sb("coef", [P, NT, GATES], F32)
        rest = sb("rest", [P, 2, NT, GATES], F32)
        piece = sb("piece", [P, 2, NT, GATES], BF16)
        pieces = sb("pieces", [P, NT, 3, GW], F32)

        flat = wq[:, 0, :, :].rearrange("p c n -> p (c n)")
        flat2 = wq[:, 1, :, :].rearrange("p c n -> p (c n)")
        gu_at = [flat[:, 0:1024], flat[:, 1024:2048], flat2[:, 2048:3072], flat2[:, 3072:4096]]
        w_gu = [at.rearrange("p (s c g n) -> p s c g n", s=2, c=KC, g=2) for at in gu_at]
        w_dn = flat[:, 2048:4096].rearrange("p (r s n) -> p r s n", r=FFN_RING, s=2)
        actT = flat2[:, 0:2048].rearrange("p (r s n) -> p r s n", r=2, s=2)
        on_rope, on_prob = work[:, 1536:3072].rearrange("p (k n) -> p k n", k=3), work[:, 0:1536].rearrange("p (k n) -> p k n", k=3)
        silu = [at[:, 0, :] for at in (on_rope, on_prob)]
        prod = [at[:, 1, :] for at in (on_rope, on_prob)]
        scaled = [at[:, 2, :] for at in (on_rope, on_prob)]

        bank = [ctx.enter_context(nc.psum_tensor(f"bank{i}", [P, 512], F32)) for i in range(8)]
        q_ps = bank[0][:, :].rearrange("p (h n) -> p h n", h=2)
        misc = bank[1]
        s0_ps = bank[2][:, 0:256].rearrange("p (h n) -> p h n", h=2)
        s1_ps = bank[3][:, :].rearrange("p (h n) -> p h n", h=2)
        p0_ps = bank[4][:, :].rearrange("p (h n) -> p h n", h=2)
        p1_ps = bank[5][:, 0:256].rearrange("p (h n) -> p h n", h=2)
        o_ps = bank[6][:, :].rearrange("p (h n) -> p h n", h=2)
        y_ps = bank[7][:, :].rearrange("p (t n) -> p t n", t=NT)
        mod_ps = [bank[6][:, 0:16].rearrange("p (j k b) -> p j k b", j=2, k=KC),
                  bank[7][:, 0:32].rearrange("p (j k b) -> p j k b", j=4, k=KC)]
        y2_ps = [bank[4 + b][:, :].rearrange("p (t n) -> p t n", t=NT) for b in range(BATCH)]
        g_ps, u_ps = bank[0], bank[2]
        c_ps = [bank[3], misc]

        in_c, in_mod, in_mod_rest, in_x, in_x_rest, in_rope, in_ident, in_causal, in_select, in_gw = (sem(n) for n in (
            "in_c", "in_mod", "in_mod_rest", "in_x", "in_x_rest", "in_rope", "in_ident", "in_causal", "in_select", "in_gw"))
        raw_in = [sem(f"raw_in{i}") for i in range(RAW)]
        c_step, mod_cols, cols_out, gates_step, diag_ok, mod_rows, rows_out = (sem(n) for n in (
            "c_step", "mod_cols", "cols_out", "gates_step", "diag_ok", "mod_rows", "rows_out"))
        consts, half_ok = sem("consts"), sem("half_ok")
        hi_split, dve_lo, pool_lo, gw_split = (sem(n) for n in ("hi_split", "dve_lo", "pool_lo", "gw_split"))
        ln_step, rstd_ok, z_ok, zT_ok, h_ok, h_hi, h_lo, h_stat_ok = (sem(n) for n in (
            "ln_step", "rstd_ok", "z_ok", "zT_ok", "h_ok", "h_hi", "h_lo", "h_stat_ok"))
        q_ok, q_rot, q_cos, q_sin, q_add, q_hi, q_lo = (sem(n) for n in (
            "q_ok", "q_rot", "q_cos", "q_sin", "q_add", "q_hi", "q_lo"))
        k_ok, k_rot, k_cos, k_sin, k_add, k_hi, k_lo = (sem(n) for n in (
            "k_ok", "k_rot", "k_cos", "k_sin", "k_add", "k_hi", "k_lo"))
        v_ok, v_hi, v_lo = (sem(n) for n in ("v_ok", "v_hi", "v_lo"))
        s_ok, max_ok, exp_ok, rsum_ok, norm_ok = (sem(n) for n in ("s_ok", "max_ok", "exp_ok", "rsum_ok", "norm_ok"))
        pT_ok, pT_hi, pT_lo, o_ok, o_hi, o_lo = (sem(n) for n in ("pT_ok", "pT_hi", "pT_lo", "o_ok", "o_hi", "o_lo"))
        d_ok, y_read, x1_ok = (sem(n) for n in ("d_ok", "y_read", "x1_ok"))
        lt_ok, lt_out, l_ok, rmax_ok, rexp_ok, r_step, pieces_ok, cT_ok, coefs_ok = (sem(n) for n in (
            "lt_ok", "lt_out", "l_ok", "rmax_ok", "rexp_ok", "r_step", "pieces_ok", "cT_ok", "coefs_ok"))
        w_in = [sem(f"w_in{i}") for i in range(FFN_RING)]
        w_hi, w_lo = (sem(n) for n in ("w_hi", "w_lo"))
        g_ok, u_ok, c_ok, silu_ok, prod_ok, scaled_ok, a_hi, a_lo, down_ok = (sem(n) for n in (
            "g_ok", "u_ok", "c_ok", "silu_ok", "prod_ok", "scaled_ok", "a_hi", "a_lo", "down_ok"))
        end_prod, end_scaled, end_hi, end_lo, end_down = (sem(n) for n in (
            "end_prod", "end_scaled", "end_hi", "end_lo", "end_down"))
        yg_ok, x2_ok, y0_out, y0_gb, x2_of_0, out_ok = (sem(n) for n in ("yg_ok", "x2_ok", "y0_out", "y0_gb", "x2_of_0", "out_ok"))

        wq_v = wq_d.rearrange("(c p) n -> p c n", p=P)
        wk_v = wk_d.rearrange("(c p) n -> p c n", p=P)
        wv_v = wv_d.rearrange("(c p) n -> p c n", p=P)
        wo_v = wo_d.rearrange("(h p) n -> p h n", p=P)
        x_v = x_d.rearrange("b (t p) n -> p b t n", p=P)
        out_v = out_d.rearrange("b (t p) n -> p b t n", p=P)

        def piece_of(w, w_v, cols):
            return w_v[:, :, cols], w[:, :, :, cols], KC

        q4 = [piece_of(wq, wq_v, slice(g * 512, (g + 1) * 512)) for g in range(KV)]
        all_k = slice(0, KV * HD)
        o4 = [(wo_v[:, 4 * r:4 * r + 4, :], wo[:, :, 4 * r:4 * r + 4, :], 4) for r in range(4)]
        splits = [piece_of(wk, wk_v, all_k), q4[0], q4[1], piece_of(wv, wv_v, all_k), q4[2], o4[0], q4[3], o4[1], o4[2], o4[3]]
        K_SPLIT, V_SPLIT = 0, 3
        Q_SPLIT = [1, 2, 4, 6]
        O_SPLIT = [5, 7, 8, 9]
        BY_POOL = (1, 5, 9)

        def wait_split(engine, i):
            engine.wait_ge(hi_split, i + 1)
            if i in BY_POOL:
                engine.wait_ge(pool_lo, len([j for j in BY_POOL if j <= i]))
            else:
                engine.wait_ge(dve_lo, i + 1 - len([j for j in BY_POOL if j <= i]))

        def raw_piece(i):
            return raw[:, i % RAW, :].rearrange("p (c n) -> p c n", c=splits[i][2])

        def norm1(b):
            return 0 if isinstance(b, int) and b == 0 else 2 * b - 1

        def norm2(b):
            return 2 * BATCH - 1 if isinstance(b, int) and b == BATCH - 1 else 2 * b + 2

        def s_ring(s, half):
            return s % 2 if isinstance(s, int) else half

        def stats2(b):
            return 2 + b

        OF_NORM2 = slice(BATCH, BATCH + 1)

        LAST = 2 * CHUNKS - 1
        PART = HALF // 2
        LAST_SLOT = 2
        HALF_STEPS = (2 * HALF_CHUNK, 2 * HALF_CHUNK + 1)

        SHARED_STEPS = (2 * EXPERT_CHUNKS, 2 * EXPERT_CHUNKS + 1)

        def ups(s):
            return s - 1 if isinstance(s, int) and s > HALF_STEPS[1] else s + 1

        def rows_of(s):
            return slice(0, REST if isinstance(s, int) and s in HALF_STEPS else P)

        PASSES = ((1, 0), (0, 1), (0, 0))

        block = ctx.enter_context(nc.Block())

        @block.sync
        def _(sp):
            wmod_v = wmod_d.rearrange("(c p) n -> p c n", p=P)
            sp.dma_start(cT[:, :, :], c_d.rearrange("p (c b) -> p c b", c=KC)).then_inc(in_c, 16)
            sp.dma_start(wmod[0], wmod_v[:, :, 0:2 * HID]).then_inc(in_mod, 16)
            sp.dma_start(xs[:, 0], x_v[:, 0]).then_inc(in_x, 16)
            sp.dma_start(ident[:, :], ident_d).then_inc(in_ident, 16)
            for i in range(2):
                sp.dma_start(raw_piece(i), splits[i][0]).then_inc(raw_in[i], 16)
            sp.dma_start(cosT[:, :], cos_d).then_inc(in_rope, 16)
            sp.dma_start(sinT[:, :], sin_d).then_inc(in_rope, 16)
            sp.dma_start(xs[:, 1:BATCH], x_v[:, 1:BATCH]).then_inc(in_x_rest, 16)
            for i in range(2, RAW):
                sp.dma_start(raw_piece(i), splits[i][0]).then_inc(raw_in[i], 16)
            sp.dma_start(causal[:, :, :], causal_d.rearrange("p (j n) -> p j n", j=2)).then_inc(in_causal, 16)
            sp.dma_start(wmod[1], wmod_v[:, :, 2 * HID:6 * HID]).then_inc(in_mod_rest, 16)
            sp.dma_start(gw_raw[:, :, :], gate_d.rearrange("(c p) n -> p c n", p=P)).then_inc(in_gw, 16)
            sp.dma_start(select[:, :], select_d).then_inc(in_select, 16)
            for i in range(RAW, SPLITS):
                wait_split(sp, i - RAW)
                sp.dma_start(raw_piece(i), splits[i][0]).then_inc(raw_in[i % RAW], 16)

            def load_chunk(c, slot):
                sp.dma_start(raw[:, slot, 0:512], up_d[bass.ds(c, 1), :, :].rearrange("a p n -> p (a n)")).then_inc(w_in[slot], 16)
                sp.dma_start(raw[:, slot, 512:768], down_d[bass.ds(c, 1), :, :].rearrange("a p n -> p (a n)")).then_inc(w_in[slot], 16)

            sp.wait_ge(hi_split, SPLITS)
            sp.wait_ge(dve_lo, SPLITS - len(BY_POOL))
            sp.wait_ge(pool_lo, len(BY_POOL))
            for c in range(FFN_RING):
                load_chunk(c, c)

            def next_chunk(i, slot):
                sp.wait_ge(w_hi, 2 * i - 1 + slot)
                sp.wait_ge(w_lo, 2 * i - 1 + slot)
                load_chunk(2 * i + slot, slot)

            with sp.Fori(FFN_RING // 2, CHUNKS // 2 - 1) as i:
                for slot in range(2):
                    next_chunk(i, slot)
            load_chunk(CHUNKS - 1, LAST_SLOT)
            next_chunk(CHUNKS // 2 - 1, 0)
            for b in (1, 2, 0, 3):
                if b == 0:
                    sp.wait_ge(x2_of_0, 1)
                else:
                    sp.wait_ge(x2_ok, b)
                sp.dma_start(out_v[:, b], xs[:, b]).then_inc(out_ok, 16)
            sp.wait_ge(out_ok, 16 * BATCH)

        @block.tensor
        def _(pe):
            def norm_transposes(l):
                pe.wait_ge(z_ok, l + 1)
                zT = misc[:, :].rearrange("p (c n) -> p c n", c=KC)
                for c in range(KC):
                    for t in range(NT):
                        last = nc.tensor.transpose(zT[:, c, t * P:(t + 1) * P], z[:, t, c * P:(c + 1) * P], ident[:, :])
                last.then_inc(zT_ok, 1)

            def project_q(b, p):
                u = UNITS * b + p
                if not (isinstance(b, int) and b == 0 and p == 0):
                    pe.wait_ge(q_cos, u)
                n = 0
                for j in range(2):
                    for c in range(KC):
                        for ws, xsel in PASSES:
                            mm = nc.tensor.matmul(q_ps[:, j, :], wq[:, ws, c, (2 * p + j) * HD:(2 * p + j + 1) * HD],
                                                  hT[:, xsel, c, bass.ds(b * SEQ, SEQ)],
                                                  start=(n == 0), stop=(n % (3 * KC) == 3 * KC - 1), skip_group_check=True)
                            n += 1
                mm.then_inc(q_ok, 1)

            def project_k(b, g):
                n = 0
                for c in range(KC):
                    for ws, xsel in PASSES:
                        mm = nc.tensor.matmul(misc[:, 0:SEQ], wk[:, ws, c, g * HD:(g + 1) * HD],
                                              hT[:, xsel, c, bass.ds(b * SEQ, SEQ)], start=(n == 0), stop=(n == 3 * KC - 1))
                        n += 1
                mm.then_inc(k_ok, 1)

            def project_v(b, t):
                at_start = isinstance(b, int) and b == 0
                if t == 0 and not at_start:
                    pe.wait_ge(h_stat_ok, b)
                n = 0
                for c in range(KC):
                    for hs, ws in PASSES:
                        h = hT if at_start else h_stat
                        mm = nc.tensor.matmul(misc[:, :], h[:, hs, c, t * P:(t + 1) * P], wv[:, ws, c, :],
                                              start=(n == 0), stop=(n == 3 * KC - 1))
                        n += 1
                mm.then_inc(v_ok, 1)

            def scores(b, p):
                u, g, r = UNITS * b + p, p // 2, p % 2
                pe.wait_ge(q_lo, u + 1)
                if p % 2 == 0:
                    pe.wait_ge(k_lo, KV * b + g + 1)
                if not (isinstance(b, int) and b == 0 and p == 0):
                    pe.wait_ge(exp_ok, u)
                nc.tensor.matmul(s0_ps[:, :, :], ident_bf[:, :], causal[:, :, :], start=True, stop=False, skip_group_check=True)
                for j in range(2):
                    for qs, ks in PASSES:
                        nc.tensor.matmul(s0_ps[:, j, :], qT[:, r, qs, j, 0:P], kT[:, g % 2, ks, 0:P],
                                         start=False, stop=(qs + ks == 0), skip_group_check=True)
                for j in range(2):
                    for n, (qs, ks) in enumerate(PASSES):
                        nc.tensor.matmul(s1_ps[:, j, :], qT[:, r, qs, j, P:SEQ], kT[:, g % 2, ks, :],
                                         start=(j == 0 and n == 0), stop=False, skip_group_check=True)
                nc.tensor.matmul(s1_ps[:, :, P:SEQ], ident_bf[:, :], causal[:, :, :], start=False, stop=True,
                                 skip_group_check=True).then_inc(s_ok, 1)

            def prob_transposes(b, p):
                u, r = UNITS * b + p, p % 2
                pe.wait_ge(norm_ok, u + 1)
                if not (isinstance(b, int) and b == 0 and p == 0):
                    pe.wait_ge(pT_lo, u)
                for j in range(2):
                    for n, dst in enumerate((p0_ps[:, j, 0:P], p0_ps[:, j, P:SEQ], p1_ps[:, j, :])):
                        at = (3 * j + n) * P
                        tr = nc.tensor.transpose(dst, prob[:, r, at:at + P], ident[:, :])
                tr.then_inc(pT_ok, 1)

            def times_v(b, p):
                u, g = UNITS * b + p, p // 2
                if p == 0:
                    pe.wait_ge(v_lo, NT * (b + 1))
                pe.wait_ge(pT_lo, u + 1)
                if isinstance(b, int) and b == 0 and p == 0:
                    pe.wait_ge(cols_out, 1)
                if not (isinstance(b, int) and b == 0 and p == 0):
                    pe.wait_ge(o_lo, u)
                cols = slice(g * HD, (g + 1) * HD)
                for n, (vs, ps) in enumerate(PASSES):
                    nc.tensor.matmul(o_ps[:, :, :], v[:, vs, 0, cols], pT[:, ps, 0:2 * SEQ], start=(n == 0), stop=False, skip_group_check=True)
                for n, (vs, ps) in enumerate(PASSES):
                    mm = nc.tensor.matmul(o_ps[:, :, P:SEQ], v[:, vs, 1, cols],
                                          pT[:, ps, 2 * SEQ:].rearrange("p (h n) -> p h n", h=2), start=False, stop=(n == 2), skip_group_check=True)
                mm.then_inc(o_ok, 1)

            def project_out(b, p):
                u = UNITS * b + p
                pe.wait_ge(o_lo, u + 1)
                if isinstance(b, int) and b == 0 and p == 0:
                    pe.wait_ge(cols_out, 2)
                if p == 0 and not (isinstance(b, int) and b == 0):
                    pe.wait_ge(y_read, b)
                if isinstance(b, int) and b == 0 and p % 2 == 0:
                    wait_split(pe, O_SPLIT[p // 2])
                for j in range(2):
                    for t in range(NT):
                        for n, (os, ws) in enumerate(PASSES):
                            mm = nc.tensor.matmul(y_ps[:, t, :], oT[:, os, j, t * P:(t + 1) * P], wo[:, ws, 2 * p + j, :],
                                                  start=(p == 0 and j == 0 and t == 0 and n == 0),
                                                  stop=(p == UNITS - 1 and j == 1 and n == 2), skip_group_check=True)
                mm.then_inc(d_ok, 1)

            def router_logits(b):
                pe.wait_ge(h_lo, norm2(b) + 1)
                n = 0
                for c in range(KC):
                    for ws, xsel in PASSES:
                        mm = nc.tensor.matmul(misc[0:GW, 0:SEQ], gw[:, ws, c, :], hT[:, xsel, c, bass.ds(b * SEQ, SEQ)],
                                              start=(n == 0), stop=(n == 3 * KC - 1))
                        n += 1
                mm.then_inc(lt_ok, 1)

            def logit_transposes(b):
                pe.wait_ge(lt_out, b + 1)
                for t in range(NT):
                    tr = nc.tensor.transpose(misc[:, t * P:(t + 1) * P], lt[:, t * P:(t + 1) * P], ident[:, :])
                tr.then_inc(l_ok, 1)

            def coef_transposes(b):
                pe.wait_ge(pieces_ok, b + 1)
                for t in range(NT):
                    tr = nc.tensor.transpose(misc[0:3 * GW, t * P:(t + 1) * P], pieces[:, t].rearrange("p a n -> p (a n)"), ident[:, :])
                tr.then_inc(cT_ok, 1)

            def gate_or_up(s, c, slot, half, i):
                ps, used, ready = ((g_ps, silu_ok, g_ok), (u_ps, prod_ok, u_ok))[i]
                if half == 0 and (i == 0 or slot == LAST_SLOT):
                    pe.wait_ge(w_hi, c + 1)
                    pe.wait_ge(w_lo, c + 1)
                if isinstance(s, int) and s == 0:
                    pe.wait_ge(*((q_cos, UNITS * BATCH) if i == 0 else (exp_ok, UNITS * BATCH)))
                elif i == 1 and isinstance(s, int) and s == HALF_STEPS[1] + 1:
                    pe.wait_ge(used, s - 2)
                else:
                    pe.wait_ge(used, s)
                n = 0
                for kc in range(KC):
                    for ws, xsel in PASSES:
                        mm = nc.tensor.matmul(ps[:, :], w_gu[slot][:, ws, kc, i, :], hT[:, xsel, kc, half * HALF:(half + 1) * HALF],
                                              start=(n == 0), stop=(n == 3 * KC - 1))
                        n += 1
                mm.then_inc(ready, 1)

            def coef_rows(s, c, half):
                if not (isinstance(s, int) and s < 2 * EARLY):
                    pe.wait_ge(scaled_ok, s - 1)
                elif s > 0:
                    pe.wait_ge(scaled_ok, s)
                nc.tensor.matmul(c_ps[half][:, :], select[:, bass.ds(c * P, P)], coefT[:, half * HALF:(half + 1) * HALF],
                                 start=True, stop=True).then_inc(c_ok, 1)

            def down(s, slot, half, opening=False):
                pe.wait_ge(a_lo, s + 1)
                rows = rows_of(s)
                for t in range(4):
                    for n, (as_, ws) in enumerate(PASSES):
                        mm = nc.tensor.matmul(y2_ps[2 * half + t // 2][:, t % 2, :], actT[rows, s_ring(s, half), as_, t * P:(t + 1) * P],
                                              w_dn[rows, slot, ws, :], start=(opening and t % 2 == 0 and n == 0), stop=False, skip_group_check=True)
                mm.then_inc(down_ok, 1)

            def step(s, c, slot, half):
                gate_or_up(s, c, slot, half, 0)
                gate_or_up(s, c, slot, half, 1)
                if not (isinstance(c, int) and c > EXPERT_CHUNKS):
                    coef_rows(s, c, half)

            def modulation(part, fields, at_row):
                for j, field in enumerate(fields, at_row):
                    for ko in range(KC):
                        at = (field - 2 * part) * HID + ko * P
                        for c in range(KC):
                            mm = nc.tensor.matmul(mod_ps[part][:, j, ko, :], wmod[part][:, c, at:at + P], ce[:, 2, c, :],
                                                  start=(c == 0), stop=(c == KC - 1))
                mm.then_inc(mod_cols, 1)

            def gate_rows(b):
                pe.wait_ge(diag_ok, b + 1)
                nc.tensor.matmul(misc[:, :], ones[:, :], ybuf[:, :, :].rearrange("p t n -> p (t n)"), start=True, stop=True).then_inc(mod_rows, 1)

            pe.wait_ge(in_mod, 16)
            pe.wait_ge(c_step, 4)
            modulation(0, (0, 1), 0)
            pe.wait_ge(in_ident, 16)
            norm_transposes(0)
            pe.wait_ge(h_lo, 1)
            wait_split(pe, K_SPLIT)
            project_k(0, 0)
            wait_split(pe, Q_SPLIT[0])
            project_q(0, 0)
            pe.wait_ge(k_cos, 1)
            project_k(0, 1)
            project_q(0, 1)
            pe.wait_ge(in_mod_rest, 16)
            modulation(1, (3, 4), 0)
            pe.wait_ge(consts, 2)
            pe.wait_ge(in_causal, 16)
            scores(0, 0)
            wait_split(pe, Q_SPLIT[1])
            project_q(0, 2)
            modulation(1, (2, 5), 2)

            def batch(b, first, last):
                for p in range(UNITS):
                    if p < UNITS - 1:
                        scores(b, p + 1)
                    elif not last:
                        scores(b + 1, 0)
                    if p == 0:
                        if first:
                            wait_split(pe, V_SPLIT)
                        pe.wait_ge(k_cos, KV * b + 2)
                        project_v(b, 0)
                    if last and p == UNITS - 1:
                        gate_or_up(0, 0, 0, 0, 1)
                        pe.wait_ge(in_select, 16)
                        pe.wait_ge(coefs_ok, BATCH - 1)
                        coef_rows(0, 0, 0)
                    prob_transposes(b, p)
                    if first and p in (2, 4, 6):
                        pe.wait_ge(k_cos, 2 + p // 2)
                        if p == 4:
                            norm_transposes(norm1(1))
                        else:
                            gate_rows({2: 0, 6: 2}[p])
                    if not first:
                        if p == 4 and not last:
                            pe.wait_ge(k_cos, KV * b + 4)
                            norm_transposes(norm1(b + 1))
                        if p == 5:
                            pe.wait_ge(lt_out, b)
                            logit_transposes(b - 1)
                        if p == 7:
                            pe.wait_ge(*((rexp_ok, b) if last else (k_cos, KV * b + 5)))
                            coef_transposes(b - 1)
                    if last and p == UNITS - 2:
                        gate_or_up(0, 0, 0, 0, 0)
                    if last and p == UNITS - 1:
                        break
                    if p in (5, 7):
                        project_out(b, p - 1)
                    ahead = p + LOOKAHEAD
                    if ahead < UNITS or not last:
                        if first and ahead < UNITS and ahead % 2 == 0:
                            wait_split(pe, Q_SPLIT[ahead // 2])
                        ab, ap = (b, ahead) if ahead < UNITS else (b + 1, ahead - UNITS)
                        if ap == 0:
                            pe.wait_ge(h_lo, norm1(b + 1) + 1)
                        if ap % 2 == 0:
                            if p == 1:
                                pe.wait_ge(v_lo, NT * b + 2)
                            elif first:
                                pe.wait_ge(rows_out, {3: 1, 5: 2, 7: 4}[p])
                            else:
                                pe.wait_ge(*{3: (h_ok, norm2(b - 1) + 1), 5: (rexp_ok, b), 7: (coefs_ok, b + 1)}[p])
                            project_k(ab, ap // 2)
                        project_q(ab, ap)
                    if p == 0:
                        pe.wait_ge(v_lo, NT * b + 1)
                        project_v(b, 1)
                    if p not in (0, 5, 7):
                        project_out(b, p - 1)
                    elif p == 0 and not first:
                        project_out(b - 1, UNITS - 1)
                    times_v(b, p)
                    if first:
                        if p == 4:
                            pe.wait_ge(h_ok, norm1(1) + 1)
                            gate_rows(1)
                        if p == 6:
                            pe.wait_ge(rows_out, 3)
                            gate_rows(3)
                    if not first:
                        if p == 2:
                            pe.wait_ge(k_cos, KV * b + 3)
                            norm_transposes(norm2(b - 1))
                        if p == 4:
                            if last:
                                pe.wait_ge(k_cos, KV * b + 4)
                            else:
                                pe.wait_ge(h_ok, norm1(b + 1) + 1)
                            router_logits(b - 1)

            batch(0, True, False)
            with pe.Fori(1, BATCH - 1) as b:
                batch(b, False, False)
            batch(BATCH - 1, False, True)

            b, p = BATCH - 1, UNITS - 1
            project_out(b, p - 1)
            gate_or_up(1, 1, 1, 0, 0)
            times_v(b, p)
            gate_or_up(1, 1, 1, 0, 1)
            coef_rows(1, 1, 0)
            project_out(b, p)
            down(0, 0, 0, True)
            gate_or_up(2, 2, 2, 0, 0)
            gate_or_up(2, 2, 2, 0, 1)
            pe.wait_ge(coefs_ok, BATCH)
            norm_transposes(norm2(b))
            coef_rows(2, 2, 0)
            down(1, 1, 0)
            pe.wait_ge(h_ok, norm2(b) + 1)
            router_logits(b)
            gate_or_up(3, 3, 3, 0, 0)
            pe.wait_ge(lt_out, BATCH)
            logit_transposes(b)
            gate_or_up(3, 3, 3, 0, 1)
            coef_rows(3, 3, 0)
            down(2, 2, 0)
            gate_or_up(4, 0, 0, 1, 0)
            gate_or_up(4, 0, 0, 1, 1)
            down(3, 3, 0)
            gate_or_up(5, 1, 1, 1, 0)
            pe.wait_ge(rexp_ok, BATCH)
            coef_transposes(b)
            pe.wait_ge(coefs_ok, 1 + BATCH)
            coef_rows(4, 0, 1)
            pe.wait_ge(y_read, BATCH)
            for s in range(EARLY + 1, 2 * EARLY):
                if s > EARLY + 1:
                    gate_or_up(s, s - EARLY, s - EARLY, 1, 0)
                gate_or_up(s, s - EARLY, s - EARLY, 1, 1)
                coef_rows(s, s - EARLY, 1)
                down(s - 1, s - 1 - EARLY, 1, s == EARLY + 1)

            def chunk_pair(i):
                for slot in range(2):
                    for half in range(2):
                        at = 2 * slot + half
                        step(4 * i + at, 2 * i + slot, slot, half)
                        if at > 0:
                            down(4 * i + at - 1, (at - 1) // 2, (at - 1) % 2)
                        else:
                            down(4 * i - 1, 1, 1)

            i = FFN_RING // 2
            for at in range(4):
                step(4 * i + at, 2 * i + at // 2, at // 2, at % 2)
                if at > 0:
                    down(4 * i + at - 1, (at - 1) // 2, (at - 1) % 2)
                else:
                    down(4 * i - 1, FFN_RING - 1, 1)
            with pe.Fori(FFN_RING // 2 + 1, EXPERT_CHUNKS // 2) as i:
                chunk_pair(i)
            for i in range(EXPERT_CHUNKS // 2, CHUNKS // 2 - 1):
                chunk_pair(i)
            s = 2 * HALF_CHUNK
            gate_or_up(s, HALF_CHUNK, 0, 0, 0)
            down(s - 1, 1, 1)
            gate_or_up(s + 1, HALF_CHUNK, 0, 1, 0)
            gate_or_up(s + 2, CHUNKS - 1, LAST_SLOT, 0, 1)
            down(s, 0, 0)
            gate_or_up(s + 2, CHUNKS - 1, LAST_SLOT, 0, 0)
            down(s + 1, 0, 1)
            gate_or_up(s + 3, CHUNKS - 1, LAST_SLOT, 1, 0)
            gate_or_up(s + 3, CHUNKS - 1, LAST_SLOT, 1, 1)
            down(s + 2, LAST_SLOT, 0)
            for part in range(2):
                pe.wait_ge(end_lo, part + 1)
                for t in range(NT):
                    at = (NT * part + t) * P
                    for n, (as_, ws) in enumerate(PASSES):
                        mm = nc.tensor.matmul(y2_ps[2 + part][:, t, :], actT[:, 1, as_, at:at + P], w_dn[:, LAST_SLOT, ws, :],
                                              start=False, stop=False, skip_group_check=True)
                mm.then_inc(end_down, 1)

        @block.scalar
        def _(act):
            nc.scalar.preload_act_table(ACT.Exp)

            def h_split(l, b):
                act.wait_ge(h_ok, l + 1)
                nc.scalar.activation(hT[:, 0, :, bass.ds(b * SEQ, SEQ)], hbuf[:, :, :], ACT.Copy).then_inc(h_hi, 1)

            def h_copy(b):
                for s in range(2):
                    i = nc.scalar.activation(h_stat[:, s], hT[:, s, :, bass.ds(b * SEQ, SEQ)], ACT.Copy)
                i.then_inc(h_stat_ok, 1)

            def split_hi(i):
                act.wait_ge(raw_in[i % RAW], 16 * (i // RAW + 1))
                nc.scalar.activation(splits[i][1][:, 0], raw_piece(i), ACT.Copy).then_inc(hi_split, 1)

            def rotate_q(b, p):
                u, r = UNITS * b + p, p % 2
                act.wait_ge(q_ok, u + 1)
                if not (isinstance(b, int) and b == 0 and p < 2):
                    act.wait_ge(q_lo, u - 1)
                nc.scalar.activation(rot[0:64, r], q_ps[64:128, :, :], ACT.Copy)
                nc.scalar.activation(rot[64:128, r], q_ps[0:64, :, :], ACT.Copy).then_inc(q_rot, 1)

            def rotate_k(b, g):
                n = KV * b + g
                act.wait_ge(k_ok, n + 1)
                if not (isinstance(b, int) and b == 0 and g == 0):
                    act.wait_ge(k_lo, n)
                nc.scalar.activation(krot[0:64, :], misc[64:128, 0:SEQ], ACT.Copy)
                nc.scalar.activation(krot[64:128, :], misc[0:64, 0:SEQ], ACT.Copy).then_inc(k_rot, 1)

            def exps(b, p):
                u, r = UNITS * b + p, p % 2
                act.wait_ge(max_ok, u + 1)
                if not (isinstance(b, int) and b == 0 and p < 2):
                    act.wait_ge(pT_ok, u - 1)
                    act.wait_ge(rsum_ok, u - 1)
                for j in range(2):
                    at = 3 * j * P
                    nc.scalar.activation(prob[:, r, at:at + P], s0_ps[:, j, :], ACT.Exp, bias=nmax[:, r, 0, j:j + 1],
                                         accum_out=sums[:, r, j, 0:1])
                    e = nc.scalar.activation(prob[:, r, at + P:at + 3 * P], s1_ps[:, j, :], ACT.Exp, bias=nmax[:, r, 1, j:j + 1],
                                             accum_out=sums[:, r, j, 1:2])
                e.then_inc(exp_ok, 1)

            def pT_split(b, p):
                u = UNITS * b + p
                act.wait_ge(pT_ok, u + 1)
                if not (isinstance(b, int) and b == 0 and p == 0):
                    act.wait_ge(o_ok, u)
                nc.scalar.activation(pT[:, 0, 0:2 * SEQ], bank[4][:, :], ACT.Copy).then_inc(pT_hi, 1)
                nc.scalar.activation(pT[:, 0, 2 * SEQ:], bank[5][:, 0:2 * P], ACT.Copy).then_inc(pT_hi, 1)

            def o_split(b, p):
                u = UNITS * b + p
                act.wait_ge(o_ok, u + 1)
                if not (isinstance(b, int) and b == 0 and p == 0):
                    act.wait_ge(d_ok, u)
                nc.scalar.activation(oT[:, 0], o_ps[:, :, :], ACT.Copy).then_inc(o_hi, 1)

            def v_split(b, t):
                act.wait_ge(v_ok, NT * b + t + 1)
                if t == 0 and not (isinstance(b, int) and b == 0):
                    act.wait_ge(o_ok, UNITS * b)
                nc.scalar.activation(v[:, 0, t, :], misc[:, :], ACT.Copy).then_inc(v_hi, 1)

            def router_exps(b):
                act.wait_ge(rmax_ok, b + 1)
                lg = misc[:, 0:NT * P].rearrange("p (t n) -> p t n", t=NT)
                for t in range(NT):
                    nc.scalar.activation(rexp[:, t, :], lg[:, t, 0:EXPERTS], ACT.Exp, bias=rmax[:, t:t + 1], accum_out=rtot[:, 0, t:t + 1])
                nc.scalar.activation(sg[:, 0], lg[:, :, EXPERTS:GATES], ACT.Exp, scale=-1.0).then_inc(rexp_ok, 1)

            def rows_copy(b):
                act.wait_ge(mod_rows, b + 1)
                nc.scalar.activation(gates[:, b].rearrange("p j n -> p (j n)"), misc[:, :], ACT.Copy).then_inc(rows_out, 1)

            act.wait_ge(in_c, 16)
            nc.scalar.activation(ce[:, 0], cT[:, :, :], ACT.Exp, scale=-1.0).then_inc(c_step, 1)
            split_hi(0)
            split_hi(1)
            h_split(0, 0)
            split_hi(2)
            rotate_k(0, 0)
            rotate_q(0, 0)
            split_hi(3)
            rotate_q(0, 1)
            rotate_k(0, 1)
            exps(0, 0)
            rotate_q(0, 2)

            def batch(b, first, last):
                for p in range(UNITS):
                    if p == 0:
                        v_split(b, 0)
                    if not first and p == 3:
                        h_split(norm2(b - 1), b - 1)
                    if last and p == UNITS - 1:
                        nc.scalar.preload_act_table(ACT.Silu)
                        silu_of(0, 0)
                    pT_split(b, p)
                    if not first and p == 5:
                        router_exps(b - 1)
                    if first and p in (2, 6):
                        rows_copy({2: 0, 6: 2}[p])
                    if not last and p == 4:
                        h_split(norm1(b + 1), b + 1)
                    if p < UNITS - 1:
                        exps(b, p + 1)
                    elif not last:
                        exps(b + 1, 0)
                    if p == 0:
                        v_split(b, 1)
                    ahead = p + LOOKAHEAD
                    if ahead < UNITS or not last:
                        ab, ap = (b, ahead) if ahead < UNITS else (b + 1, ahead - UNITS)
                        if ap % 2 == 0:
                            rotate_k(ab, ap // 2)
                        rotate_q(ab, ap)
                    if last and p == UNITS - 1:
                        break
                    if first and p == 0:
                        split_hi(4)
                    if first and p == 1:
                        split_hi(6)
                    if first and p in (0, 1, 3, 4):
                        split_hi({0: 5, 1: 7, 3: 8, 4: 9}[p])
                    if not last and p == 6:
                        h_copy(b + 1)
                    if last and p in (4, 5):
                        for slot in range(2 * p - 8, 2 * p - 6):
                            weights_hi(0, slot, True)
                    o_split(b, p)
                    if first and p in (4, 6):
                        rows_copy({4: 1, 6: 3}[p])

            def weights_hi(i, slot, first):
                if first:
                    act.wait_ge(w_in[slot], 32)
                    act.wait_ge(q_ok, UNITS * BATCH)
                elif slot == LAST_SLOT:
                    act.wait_ge(w_in[slot], 2 * 32)
                    act.wait_ge(down_ok, 2 * EARLY)
                else:
                    act.wait_ge(w_in[slot], 32 * i)
                    act.wait_ge(down_ok, 4 * i - 2 + 2 * slot)
                nc.scalar.activation(gu_at[slot][:, 0:512], raw[:, slot, 0:512], ACT.Copy)
                nc.scalar.activation(w_dn[:, slot, 0], raw[:, slot, 512:768], ACT.Copy).then_inc(w_hi, 1)

            def silu_of(s, half):
                act.wait_ge(g_ok, s + 1)
                if not (isinstance(s, int) and s < 2):
                    act.wait_ge(prod_ok, s - 1)
                r, rows = s_ring(s, half), rows_of(s)
                if isinstance(s, int) and s in HALF_STEPS:
                    act.wait_ge(scaled_ok, s - 1)
                    nc.scalar.activation(prod[r][rows], g_ps[REST:2 * REST, :], ACT.Copy)
                nc.scalar.activation(silu[r][rows], g_ps[rows, :], ACT.Silu).then_inc(silu_ok, 1)

            def act_hi(s, half):
                act.wait_ge(scaled_ok, s + 1)
                if not (isinstance(s, int) and s < 2):
                    act.wait_ge(down_ok, s - 1)
                r, rows = s_ring(s, half), rows_of(s)
                nc.scalar.activation(actT[rows, r, 0, :], scaled[r][rows], ACT.Copy).then_inc(a_hi, 1)

            batch(0, True, False)
            with act.Fori(1, BATCH - 1) as b:
                batch(b, False, False)
            batch(BATCH - 1, False, True)

            b, p = BATCH - 1, UNITS - 1
            act_hi(0, 0)
            o_split(b, p)
            silu_of(1, 0)
            act_hi(1, 0)
            h_split(norm2(b), b)
            silu_of(2, 0)
            act_hi(2, 0)
            silu_of(3, 0)
            nc.scalar.preload_act_table(ACT.Exp)
            router_exps(b)
            nc.scalar.preload_act_table(ACT.Silu)
            act_hi(3, 0)
            for s in range(EARLY, 2 * EARLY):
                silu_of(s, 1)
                act_hi(s, 1)
                if s == 2 * EARLY - 2:
                    weights_hi(FFN_RING // 2, 0, False)

            def chunk_pair(i, last):
                for slot in range(2):
                    for half in range(2):
                        at = 2 * slot + half
                        silu_of(4 * i + at, half)
                        if last and at == 3:
                            break
                        act_hi(4 * i + at, half)
                        if at == 2 and not last:
                            weights_hi(i + 1, 0, False)
                        if at == 0 and not last:
                            weights_hi(i, 1, False)
                        if at == 3 and isinstance(i, int):
                            weights_hi(i + 1, LAST_SLOT, False)

            with act.Fori(FFN_RING // 2, CHUNKS // 2 - 2) as i:
                chunk_pair(i, False)
            chunk_pair(CHUNKS // 2 - 2, False)
            chunk_pair(CHUNKS // 2 - 1, True)
            act.wait_ge(down_ok, LAST - 1)
            for part in range(2):
                at = slice(part * PART, (part + 1) * PART)
                act.wait_ge(end_scaled, part + 1)
                nc.scalar.activation(actT[:, 1, 0, at], scaled[1][:, at], ACT.Copy).then_inc(end_hi, 1)
            act.wait_ge(down_ok, LAST)
            nc.scalar.activation(ybuf[:, :, :], y2_ps[0], ACT.Copy).then_inc(y0_out, 1)

        @block.vector
        def _(dve):
            def norm_stats(n, at, rows):
                for k, x in enumerate(rows):
                    for t in range(NT):
                        i = nc.vector.bn_stats(stats[:, at.start + k, t, :], x[:, t, :])
                i.then_inc(ln_step, 1)
                dve.wait_ge(ln_step, 3 * n + 1)
                nc.vector.memset(ve[:, at], EPS)
                for k in range(len(rows)):
                    for t in range(NT):
                        i = nc.vector.bn_aggr(mv[:, at.start + k, t, :], stats[:, at.start + k, t, :])
                i.then_inc(ln_step, 1)
                dve.wait_ge(ln_step, 3 * n + 2)
                nc.vector.tensor_tensor(ve[:, at], mv[:, at, :, 1], ve[:, at], ALU.add).then_inc(ln_step, 1)

            def x_of(b):
                return xs[:, bass.ds(b, 1)].rearrange("p a t n -> p (a t) n")

            def normalize(l, n, at, b):
                dve.wait_ge(rstd_ok, n + 1)
                if not (isinstance(l, int) and l == 0):
                    dve.wait_ge(zT_ok, l)
                for t in range(NT):
                    i = nc.vector.tensor_scalar(z[:, t, :], x_of(b)[:, t, :], mv[:, bass.ds(at, 1), t, 0],
                                                rstd[:, bass.ds(at, 1), t], ALU.subtract, ALU.mult)
                i.then_inc(z_ok, 1)

            def modulate(l, b, shift):
                dve.wait_ge(zT_ok, l + 1)
                if not (isinstance(l, int) and l == 0):
                    dve.wait_ge(h_lo, l)
                zT = misc[:, :].rearrange("p (c n) -> p c n", c=KC)
                for c in range(KC):
                    i = nc.vector.tensor_scalar(hbuf[:, c, :], zT[:, c, :], modc[:, shift + 1, c, bass.ds(b, 1)],
                                                modc[:, shift, c, bass.ds(b, 1)], ALU.mult, ALU.add)
                i.then_inc(h_ok, 1)

            def h_rest(l, b):
                dve.wait_ge(h_hi, l + 1)
                at = bass.ds(b * SEQ, SEQ)
                nc.vector.tensor_tensor(hT[:, 1, :, at], hbuf[:, :, :], hT[:, 0, :, at].bitcast(F32), ALU.subtract).then_inc(h_lo, 1)

            def split_lo(i):
                dve.wait_ge(hi_split, i + 1)
                nc.vector.tensor_tensor(splits[i][1][:, 1], raw_piece(i), splits[i][1][:, 0].bitcast(F32), ALU.subtract).then_inc(dve_lo, 1)

            def q_times_cos(b, p):
                u, r = UNITS * b + p, p % 2
                dve.wait_ge(q_rot, u + 1)
                if not (isinstance(b, int) and b == 0 and p < 2):
                    dve.wait_ge(q_add, u - 1)
                nc.vector.tensor_tensor(qcos[:, r], q_ps[:, :, :], cosT[:, :].unsqueeze(1).to_broadcast([P, 2, SEQ]), ALU.mult).then_inc(q_cos, 1)

            def k_times_cos(b, g):
                n = KV * b + g
                dve.wait_ge(k_rot, n + 1)
                if not (isinstance(b, int) and b == 0 and g == 0):
                    dve.wait_ge(k_lo, n)
                nc.vector.tensor_tensor(kcos, misc[:, 0:SEQ], cosT[:, :], ALU.mult).then_inc(k_cos, 1)

            def q_split(b, p):
                u, r = UNITS * b + p, p % 2
                dve.wait_ge(q_add, u + 1)
                if not (isinstance(b, int) and b == 0 and p < 2):
                    dve.wait_ge(s_ok, u - 1)
                nc.vector.tensor_copy(qT[:, r, 0], rot[:, r]).then_inc(q_hi, 1)
                dve.wait_ge(q_hi, u + 1)
                nc.vector.tensor_tensor(qT[:, r, 1], rot[:, r], qT[:, r, 0].bitcast(F32), ALU.subtract).then_inc(q_lo, 1)

            def k_split(b, g):
                n, r = KV * b + g, g % 2
                dve.wait_ge(k_add, n + 1)
                if not (isinstance(b, int) and b == 0 and g < 2):
                    dve.wait_ge(s_ok, 2 * n - 2)
                nc.vector.tensor_copy(kT[:, r, 0, :], krot).then_inc(k_hi, 1)
                dve.wait_ge(k_hi, n + 1)
                nc.vector.tensor_tensor(kT[:, r, 1, :], krot, kT[:, r, 0, :].bitcast(F32), ALU.subtract).then_inc(k_lo, 1)

            def maxima(b, p):
                u, r = UNITS * b + p, p % 2
                dve.wait_ge(s_ok, u + 1)
                if not (isinstance(b, int) and b == 0 and p < 2):
                    dve.wait_ge(exp_ok, u - 1)
                nc.vector.tensor_reduce(nmax[:, r, 0, :], s0_ps[:, :, :], AX_X, ALU.max, negate=True)
                nc.vector.tensor_reduce(nmax[:, r, 1, :], s1_ps[:, :, :], AX_X, ALU.max, negate=True).then_inc(max_ok, 1)

            def reciprocals(b, p):
                u, r = UNITS * b + p, p % 2
                dve.wait_ge(exp_ok, u + 1)
                if not (isinstance(b, int) and b == 0 and p < 2):
                    dve.wait_ge(norm_ok, u - 1)
                nc.vector.reciprocal(rsum[:, r, :, 0:1], sums[:, r, :, 0:1])
                nc.vector.reciprocal(rsum[:, r, :, 1:3], sums[:, r, :, 1:2].to_broadcast([P, 2, 2])).then_inc(rsum_ok, 1)

            def pT_rest(b, p):
                u = UNITS * b + p
                for n, (lo, hi, bk) in enumerate(((0, 2 * SEQ, 4), (2 * SEQ, 2 * SEQ + 2 * P, 5))):
                    dve.wait_ge(pT_hi, 2 * u + n + 1)
                    i = nc.vector.tensor_tensor(pT[:, 1, lo:hi], bank[bk][:, 0:hi - lo], pT[:, 0, lo:hi].bitcast(F32), ALU.subtract)
                i.then_inc(pT_lo, 1)

            def o_rest(b, p):
                u = UNITS * b + p
                dve.wait_ge(o_hi, u + 1)
                nc.vector.tensor_tensor(oT[:, 1], o_ps[:, :, :], oT[:, 0].bitcast(F32), ALU.subtract).then_inc(o_lo, 1)

            def v_rest(b, t):
                dve.wait_ge(v_hi, NT * b + t + 1)
                nc.vector.tensor_tensor(v[:, 1, t, :], misc[:, :], v[:, 0, t, :].bitcast(F32), ALU.subtract).then_inc(v_lo, 1)

            def clamp_gates():
                dve.wait_ge(mod_cols, 3)
                for j in range(2):
                    nc.vector.tensor_scalar(modc[:, 2 + j], mod_ps[1][:, j], float(j), None, ALU.add)
                nc.vector.tensor_copy(gate_cols[:, :, :, :], mod_ps[1][:, 2:4].rearrange("p j k b -> p b j k")).then_inc(cols_out, 1)
                g, sign = gate_cols[:, :, :, :], gate_sign[:, :, :, :]
                dve.wait_ge(cols_out, 2)
                nc.vector.tensor_scalar(sign, g, 0.0, 2.0, ALU.is_ge, ALU.mult).then_inc(gates_step, 1)
                dve.wait_ge(gates_step, 1)
                nc.vector.tensor_scalar(sign, sign, -1.0, None, ALU.add).then_inc(gates_step, 1)
                dve.wait_ge(gates_step, 2)
                nc.vector.tensor_tensor(g, g, sign, ALU.mult).then_inc(gates_step, 1)
                dve.wait_ge(gates_step, 3)
                nc.vector.scalar_tensor_tensor(g, g, 0.25, sign, ALU.max, ALU.mult).then_inc(gates_step, 1)

            def gate_y(b):
                dve.wait_ge(d_ok, UNITS * (b + 1))
                if not (isinstance(b, int) and b == 0):
                    dve.wait_ge(x1_ok, b)
                ga = gates[:, bass.ds(b, 1), 0, :].to_broadcast([P, NT, HID])
                nc.vector.tensor_tensor(ybuf[:, :, :], y_ps[:, :, :], ga, ALU.mult).then_inc(y_read, 1)

            def logits_out(b):
                dve.wait_ge(lt_ok, b + 1)
                if not (isinstance(b, int) and b == 0):
                    dve.wait_ge(l_ok, b)
                nc.vector.tensor_copy(lt[0:GW, :], misc[0:GW, 0:SEQ]).then_inc(lt_out, 1)

            def router_max(b):
                dve.wait_ge(l_ok, b + 1)
                lg = misc[:, 0:NT * P].rearrange("p (t n) -> p t n", t=NT)
                nc.vector.tensor_reduce(rmax[:, :], lg[:, :, 0:EXPERTS], AX_X, ALU.max, negate=True).then_inc(rmax_ok, 1)

            ROUTING_STEPS, PIECES_STEPS = 6, 5

            def counter(done):
                count = [0]

                def after_it(i):
                    i.then_inc(r_step, 1)
                    count[0] += 1
                    dve.wait_ge(r_step, done + count[0])
                return after_it

            def routing(b):
                after_it = counter((ROUTING_STEPS + PIECES_STEPS) * b)
                dve.wait_ge(rexp_ok, b + 1)
                after_it(nc.vector.reciprocal(rtot[:, 1, :], rtot[:, 0, :]))
                for t in range(NT):
                    i = nc.vector.tensor_scalar(probs20[:, t, 0:EXPERTS], rexp[:, t, :], rtot[:, 1, t:t + 1], None, ALU.mult)
                after_it(i)
                nc.vector.tensor_scalar(sg[:, 1], sg[:, 0], 1.0, None, ALU.add)
                for t in range(NT):
                    i = nc.vector.max(top8[:, t, :], probs20[:, t, 0:EXPERTS])
                after_it(i)
                after_it(nc.vector.memset(top8[:, :, TOP_K:8], SENTINEL))
                nc.vector.reciprocal(coef[:, :, EXPERTS:GATES], sg[:, 1])
                for t in range(NT):
                    i = nc.vector.match_replace(left20[:, t, :], top8[:, t, :], probs20[:, t, :], -1.0)
                after_it(i)
                after_it(nc.vector.scalar_tensor_tensor(coef[:, :, 0:EXPERTS], left20[:, :, 0:EXPERTS], 0.0, probs20[:, :, 0:EXPERTS],
                                                        ALU.is_lt, ALU.mult))

            def coef_pieces(b):
                after_it = counter((ROUTING_STEPS + PIECES_STEPS) * b + ROUTING_STEPS)
                after_it(nc.vector.tensor_copy(piece[:, 0], coef[:, :, :]))
                if not (isinstance(b, int) and b == 0):
                    dve.wait_ge(cT_ok, b)
                nc.vector.tensor_copy(pieces[:, :, 0, 0:GATES], piece[:, 0])
                after_it(nc.vector.tensor_tensor(rest[:, 0], coef[:, :, :], piece[:, 0], ALU.subtract))
                after_it(nc.vector.tensor_copy(piece[:, 1], rest[:, 0]))
                nc.vector.tensor_copy(pieces[:, :, 1, 0:GATES], piece[:, 1])
                after_it(nc.vector.tensor_tensor(rest[:, 1], rest[:, 0], piece[:, 1], ALU.subtract))
                after_it(nc.vector.tensor_copy(piece[:, 0], rest[:, 1]))
                nc.vector.tensor_copy(pieces[:, :, 2, 0:GATES], piece[:, 0]).then_inc(pieces_ok, 1)

            def coefs_out(b):
                dve.wait_ge(cT_ok, b + 1)
                nc.vector.tensor_copy(coefT[:, bass.ds(b * SEQ, SEQ)], misc[0:3 * GW, 0:SEQ]).then_inc(coefs_ok, 1)

            def product(s, half):
                r, rows = s_ring(s, half), rows_of(s)
                dve.wait_ge(silu_ok, s + 1)
                if isinstance(s, int) and s in HALF_STEPS:
                    up = prod[r][rows]
                else:
                    up = u_ps[:, :]
                    dve.wait_ge(u_ok, ups(s))
                    if not (isinstance(s, int) and s < 2):
                        dve.wait_ge(scaled_ok, s - 1)
                nc.vector.tensor_tensor(prod[r][rows], up, silu[r][rows], ALU.mult).then_inc(prod_ok, 1)

            def scale(s, half):
                r, rows = s_ring(s, half), rows_of(s)
                dve.wait_ge(prod_ok, s + 1)
                if not (isinstance(s, int) and s > SHARED_STEPS[1]):
                    dve.wait_ge(c_ok, s + 1)
                if not (isinstance(s, int) and s < 2):
                    dve.wait_ge(a_lo, s - 1)
                nc.vector.tensor_tensor(scaled[r][rows], c_ps[half][rows, :], prod[r][rows], ALU.mult).then_inc(scaled_ok, 1)

            def act_rest(s, half):
                r, rows = s_ring(s, half), rows_of(s)
                dve.wait_ge(a_hi, s + 1)
                nc.vector.tensor_tensor(actT[rows, r, 1, :], scaled[r][rows], actT[rows, r, 0, :].bitcast(F32), ALU.subtract).then_inc(a_lo, 1)

            nc.vector.memset(ones[:, :], 1.0)
            nc.vector.memset(pieces[:, :, :, :], 0.0)
            nc.vector.memset(lt[:, :], 0.0)
            nc.vector.memset(probs20[:, :, EXPERTS:EXPERTS + 4], SENTINEL).then_inc(coefs_ok, 1)
            dve.wait_ge(c_step, 1)
            nc.vector.tensor_scalar(ce[:, 1], ce[:, 0], 1.0, None, ALU.add).then_inc(c_step, 1)
            dve.wait_ge(c_step, 2)
            nc.vector.reciprocal(ce[:, 0], ce[:, 1]).then_inc(c_step, 1)
            dve.wait_ge(c_step, 3)
            nc.vector.tensor_tensor(ce[:, 2], ce[:, 0], cT[:, :, :], ALU.mult).then_inc(c_step, 1)
            dve.wait_ge(in_x, 16)
            norm_stats(0, slice(0, 1), [x_of(0)])
            normalize(0, 0, 0, 0)
            split_lo(0)
            dve.wait_ge(mod_cols, 1)
            for j in range(2):
                i = nc.vector.tensor_scalar(modc[:, j], mod_ps[0][:, j], float(j), None, ALU.add)
            i.then_inc(cols_out, 1)
            dve.wait_ge(cols_out, 1)
            modulate(0, 0, 0)
            h_rest(0, 0)
            dve.wait_ge(in_ident, 16)
            nc.vector.tensor_copy(ident_bf[:, :], ident[:, :]).then_inc(consts, 2)
            dve.wait_ge(in_x_rest, 16)
            norm_stats(1, slice(1, BATCH), [x_of(n) for n in range(1, BATCH)])
            split_lo(2)
            dve.wait_ge(in_rope, 32)
            k_times_cos(0, 0)
            q_times_cos(0, 0)
            k_split(0, 0)
            split_lo(3)
            q_split(0, 0)
            q_times_cos(0, 1)
            maxima(0, 0)
            k_times_cos(0, 1)
            q_split(0, 1)
            reciprocals(0, 0)
            k_split(0, 1)
            q_times_cos(0, 2)

            def batch(b, first, last):
                for p in range(UNITS):
                    if p > 0:
                        o_rest(b, p - 1)
                    elif not first:
                        o_rest(b - 1, UNITS - 1)
                    if not first and p == 3:
                        h_rest(norm2(b - 1), b - 1)
                    if not first and p == 5:
                        logits_out(b - 1)
                    if p < UNITS - 1:
                        maxima(b, p + 1)
                    elif not last:
                        maxima(b + 1, 0)
                    if p == 0:
                        v_rest(b, 0)
                    if not first and p == 5:
                        router_max(b - 1)
                    if last and p == UNITS - 1:
                        product(0, 0)
                    if not first and p == 7:
                        coefs_out(b - 1)
                    pT_rest(b, p)
                    if not first and p == 2:
                        normalize(norm2(b - 1), stats2(b - 1), BATCH, b - 1)
                    if not last and p == 3:
                        normalize(norm1(b + 1), 1, b + 1, b + 1)
                    if not last and p == 4:
                        modulate(norm1(b + 1), b + 1, 0)
                    ahead = p + LOOKAHEAD - 1
                    if ahead < UNITS or not last:
                        ab, ap = (b, ahead) if ahead < UNITS else (b + 1, ahead - UNITS)
                        if ap % 2 == 0 and not (first and p == 0):
                            k_split(ab, ap // 2)
                        q_split(ab, ap)
                    if not last and p == 4:
                        h_rest(norm1(b + 1), b + 1)
                    if last and p == UNITS - 1:
                        scale(0, 0)
                        break
                    if p == 0:
                        v_rest(b, 1)
                    if p < UNITS - 1:
                        reciprocals(b, p + 1)
                    else:
                        reciprocals(b + 1, 0)
                    ahead = p + LOOKAHEAD
                    if ahead < UNITS or not last:
                        ab, ap = (b, ahead) if ahead < UNITS else (b + 1, ahead - UNITS)
                        if ap % 2 == 0:
                            k_times_cos(ab, ap // 2)
                        q_times_cos(ab, ap)
                    if first and p < 4:
                        split_lo((4, 6, 7, 8)[p])
                    if first and p == 0:
                        clamp_gates()
                    if first and p == 1:
                        dve.wait_ge(in_gw, 16)
                        nc.vector.tensor_copy(gw[:, 0], gw_raw[:, :, :]).then_inc(gw_split, 1)
                        dve.wait_ge(gw_split, 1)
                        nc.vector.tensor_tensor(gw[:, 1], gw_raw[:, :, :], gw[:, 0].bitcast(F32), ALU.subtract)
                    if not first and p == 0:
                        gate_y(b - 1)
                    if not first and p == 1:
                        dve.wait_ge(x1_ok, b)
                        norm_stats(stats2(b - 1), OF_NORM2, [x_of(b - 1)])
                    if not first and p == 2:
                        modulate(norm2(b - 1), b - 1, 2)
                    if not first and p == 5:
                        routing(b - 1)
                    if not first and p == 6:
                        coef_pieces(b - 1)

            batch(0, True, False)
            with dve.Fori(1, BATCH - 1) as b:
                batch(b, False, False)
            batch(BATCH - 1, False, True)

            b = BATCH - 1
            act_rest(0, 0)
            o_rest(b, UNITS - 1)
            product(1, 0)
            gate_y(b)
            scale(1, 0)
            dve.wait_ge(x1_ok, BATCH)
            norm_stats(stats2(b), OF_NORM2, [x_of(b)])
            act_rest(1, 0)
            normalize(norm2(b), stats2(b), BATCH, b)
            modulate(norm2(b), b, 2)
            h_rest(norm2(b), b)
            product(2, 0)
            scale(2, 0)
            logits_out(b)
            act_rest(2, 0)
            router_max(b)
            product(3, 0)
            scale(3, 0)
            act_rest(3, 0)
            routing(b)
            coef_pieces(b)
            product(4, 1)
            coefs_out(b)
            scale(4, 1)
            act_rest(4, 1)
            for s in range(EARLY + 1, 2 * EARLY):
                product(s, 1)
                scale(s, 1)
                act_rest(s, 1)

            def chunk_pair(i, steps=4):
                for at in range(steps):
                    product(4 * i + at, at % 2)
                    scale(4 * i + at, at % 2)
                    act_rest(4 * i + at, at % 2)

            with dve.Fori(FFN_RING // 2, EXPERT_CHUNKS // 2) as i:
                chunk_pair(i)
            for i in range(EXPERT_CHUNKS // 2, CHUNKS // 2 - 1):
                chunk_pair(i)
            chunk_pair(CHUNKS // 2 - 1, 3)
            dve.wait_ge(silu_ok, LAST + 1)
            dve.wait_ge(u_ok, ups(LAST))
            parts = [slice(part * PART, (part + 1) * PART) for part in range(2)]
            for part, at in enumerate(parts):
                nc.vector.tensor_tensor(prod[1][:, at], u_ps[:, at], silu[1][:, at], ALU.mult).then_inc(end_prod, 1)
                dve.wait_ge(end_prod, part + 1)
                nc.vector.tensor_tensor(scaled[1][:, at], c_ps[1][:, at], prod[1][:, at], ALU.mult).then_inc(end_scaled, 1)
            for part, at in enumerate(parts):
                dve.wait_ge(end_hi, part + 1)
                nc.vector.tensor_tensor(actT[:, 1, 1, at], scaled[1][:, at], actT[:, 1, 0, at].bitcast(F32), ALU.subtract).then_inc(end_lo, 1)
            yg = [None, z[:, :, :], hbuf[:, :, :], prod[0].rearrange("p (t n) -> p t n", t=NT)]

            def y_times_gb(b):
                nc.vector.tensor_tensor(yg[b], y2_ps[b], gates[:, b, 1, :].unsqueeze(1).to_broadcast([P, NT, HID]), ALU.mult).then_inc(yg_ok, 1)

            def plus_x(b):
                dve.wait_ge(yg_ok, b)
                nc.vector.tensor_tensor(xs[:, b], yg[b], xs[:, b], ALU.add).then_inc(x2_ok, 1)

            dve.wait_ge(down_ok, LAST)
            y_times_gb(1)
            dve.wait_ge(end_down, 1)
            y_times_gb(2)
            plus_x(1)
            dve.wait_ge(end_down, 2)
            y_times_gb(3)
            plus_x(2)
            plus_x(3)

        @block.gpsimd
        def _(pool):
            def power(n, at):
                pool.wait_ge(ln_step, 3 * n + 3)
                if not (isinstance(n, int) and n <= stats2(0)):
                    pool.wait_ge(z_ok, norm2(n - 3) + 1)
                nc.gpsimd.tensor_tensor(rstd[:, at], ve[:, at], neg_half[:, at], ALU.pow).then_inc(rstd_ok, 1)

            def split_lo(i):
                pool.wait_ge(hi_split, i + 1)
                nc.gpsimd.tensor_tensor(splits[i][1][:, 1], raw_piece(i), splits[i][1][:, 0].bitcast(F32), ALU.subtract).then_inc(pool_lo, 1)

            def q_rope(b, p):
                u, r = UNITS * b + p, p % 2
                pool.wait_ge(q_rot, u + 1)
                nc.gpsimd.tensor_tensor(rot[:, r], rot[:, r], sinT[:, :].unsqueeze(1).to_broadcast([P, 2, SEQ]), ALU.mult).then_inc(q_sin, 1)
                pool.wait_ge(q_sin, u + 1)
                pool.wait_ge(q_cos, u + 1)
                nc.gpsimd.tensor_tensor(rot[:, r], rot[:, r], qcos[:, r], ALU.add).then_inc(q_add, 1)

            def k_rope(b, g):
                n = KV * b + g
                pool.wait_ge(k_rot, n + 1)
                nc.gpsimd.tensor_tensor(krot, krot, sinT[:, :], ALU.mult).then_inc(k_sin, 1)
                pool.wait_ge(k_sin, n + 1)
                pool.wait_ge(k_cos, n + 1)
                nc.gpsimd.tensor_tensor(krot, krot, kcos, ALU.add).then_inc(k_add, 1)

            def norm_probs(b, p):
                u, r = UNITS * b + p, p % 2
                pool.wait_ge(rsum_ok, u + 1)
                e = prob[:, r, :].rearrange("p (k n) -> p k n", k=6)
                by = rsum[:, r].rearrange("p h k -> p (h k)").unsqueeze(2).to_broadcast([P, 6, P])
                nc.gpsimd.tensor_tensor(e, e, by, ALU.mult).then_inc(norm_ok, 1)

            def add_x(b):
                pool.wait_ge(y_read, b + 1)
                at = xs[:, bass.ds(b, 1)].rearrange("p a t n -> p (a t) n")
                nc.gpsimd.tensor_tensor(at, at, ybuf[:, :, :], ALU.add).then_inc(x1_ok, 1)

            def gate_diagonals(b):
                if b == 0:
                    pool.wait_ge(gates_step, 4)
                else:
                    pool.wait_ge(mod_rows, b)
                nc.gpsimd.tensor_tensor(ybuf[:, :, :].rearrange("p t (c n) -> p (t c) n", c=KC), ident[:, :].unsqueeze(1).to_broadcast([P, 2 * KC, P]),
                                        gate_cols[:, b].rearrange("p j k -> p (j k)").unsqueeze(2).to_broadcast([P, 2 * KC, P]), ALU.mult).then_inc(diag_ok, 1)

            nc.gpsimd.memset(neg_half[:, :, :], -0.5).then_inc(half_ok, 1)
            pool.wait_ge(half_ok, 1)
            power(0, slice(0, 1))
            split_lo(1)
            pool.wait_ge(in_rope, 32)
            k_rope(0, 0)
            q_rope(0, 0)
            power(1, slice(1, BATCH))
            q_rope(0, 1)
            k_rope(0, 1)
            norm_probs(0, 0)
            q_rope(0, 2)

            def batch(b, first, last):
                for p in range(UNITS):
                    if not first and p == 1:
                        add_x(b - 1)
                    if first and p == 5:
                        split_lo(9)
                    if first and p in (1, 3, 5, 6):
                        gate_diagonals({1: 0, 3: 1, 5: 2, 6: 3}[p])
                    if p < UNITS - 1:
                        norm_probs(b, p + 1)
                    elif not last:
                        norm_probs(b + 1, 0)
                    ahead = p + LOOKAHEAD
                    if ahead < UNITS or not last:
                        ab, ap = (b, ahead) if ahead < UNITS else (b + 1, ahead - UNITS)
                        if ap % 2 == 0:
                            k_rope(ab, ap // 2)
                        if not first and p == 1:
                            power(stats2(b - 1), OF_NORM2)
                        q_rope(ab, ap)
                    if last and p >= UNITS - EARLY:
                        weights_lo(0, p - UNITS + EARLY)
                    if first and p == 0:
                        split_lo(5)

            def weights_lo(i, k, slot=None):
                slot = k if slot is None else slot
                pool.wait_ge(w_hi, 2 * i + k + 1)
                nc.gpsimd.tensor_tensor(gu_at[slot][:, 512:1024], raw[:, slot, 0:512], gu_at[slot][:, 0:512].bitcast(F32), ALU.subtract)
                nc.gpsimd.tensor_tensor(w_dn[:, slot, 1], raw[:, slot, 512:768], w_dn[:, slot, 0].bitcast(F32), ALU.subtract).then_inc(w_lo, 1)

            batch(0, True, False)
            with pool.Fori(1, BATCH - 1) as b:
                batch(b, False, False)
            batch(BATCH - 1, False, True)
            add_x(BATCH - 1)
            power(stats2(BATCH - 1), OF_NORM2)
            with pool.Fori(FFN_RING // 2, CHUNKS // 2 - 1) as i:
                for slot in range(2):
                    weights_lo(i, slot)
            weights_lo(CHUNKS // 2 - 1, 0)
            weights_lo(CHUNKS // 2 - 1, 1, LAST_SLOT)
            pool.wait_ge(y0_out, 1)
            nc.gpsimd.tensor_tensor(ybuf[:, :, :], ybuf[:, :, :], gates[:, 0, 1, :].unsqueeze(1).to_broadcast([P, NT, HID]), ALU.mult).then_inc(y0_gb, 1)
            pool.wait_ge(y0_gb, 1)
            nc.gpsimd.tensor_tensor(xs[:, 0], ybuf[:, :, :], xs[:, 0], ALU.add).then_inc(x2_of_0, 1)


def _constants(np):
    f = np.float32
    inv = f(1.0) / np.power(f(10000.0), np.arange(0, HD, 2, dtype=f) / f(HD)).astype(f)
    ang = np.arange(SEQ, dtype=f)[None, :] * inv[:, None]
    root = f(HD ** -0.25)
    cos = np.concatenate([np.cos(ang), np.cos(ang)]) * root
    sin = np.concatenate([-np.sin(ang), np.sin(ang)]) * root
    causal = np.tile(np.where(np.arange(P)[None, :] > np.arange(P)[:, None], f(MASKED), f(0)), (1, 2))
    select = np.zeros((3 * GW, (EXPERT_CHUNKS + 1) * P), f)
    for n in range((EXPERT_CHUNKS + 1) * P):
        e = min(n // INNER, EXPERTS)
        select[[e, GW + e, 2 * GW + e], n] = 1
    return cos.astype(f), sin.astype(f), np.eye(P, dtype=f), causal.astype(f), select


def kernel(**inputs):
    import numpy as np
    import ml_dtypes
    import concourse.bacc as bacc
    from concourse.bass_utils import run_bass_kernel_spmd

    i = {k[3:]: np.asarray(a) for k, a in inputs.items()}
    def features(w, shared):
        full = HALF_CHUNK * P + REST - EXPERTS * INNER
        rows = [w.reshape(EXPERTS * INNER, HID), shared[:full], np.zeros((P - REST, HID), w.dtype), shared[full:]]
        return np.concatenate(rows).reshape(CHUNKS, P, HID)

    def as_stationary(w):
        return w.reshape(CHUNKS, P, KC, P).transpose(0, 3, 2, 1)

    gate = features(i["ffn_w13"][:, :INNER], i["ffn_shared_gate_up_w"][:SHARED])
    up = features(i["ffn_w13"][:, INNER:], i["ffn_shared_gate_up_w"][SHARED:])
    gate_up = np.stack([as_stationary(gate), as_stationary(up)], 3)
    gate_up[HALF_CHUNK, :, :, 0, REST:] = gate_up[HALF_CHUNK, :, :, 1, :REST]
    gate_up = gate_up.reshape(CHUNKS, P, 2 * KC * P)
    down = features(i["ffn_w2"].transpose(0, 2, 1), i["ffn_shared_down_w"].T)
    router = np.zeros((HID, GW), np.float32)
    router[:, :EXPERTS] = i["ffn_gate_w"].T
    router[:, EXPERTS] = i["ffn_sgate_w"][0]
    c = i["c"].T.reshape(KC, P, BATCH).transpose(1, 0, 2).reshape(P, KC * BATCH)
    cos, sin, ident, causal, select = _constants(np)
    arrays = {
        "x_dram": i["attn_x"], "wq_dram": i["attn_Wq"], "wk_dram": i["attn_Wk"], "wv_dram": i["attn_Wv"],
        "wo_dram": i["attn_Wo"], "router_dram": router, "gate_up_dram": gate_up, "down_dram": down,
        "c_dram": c, "wmod_dram": i["wmod"], "cos_dram": cos, "sin_dram": sin, "ident_dram": ident,
        "causal_dram": causal.astype(ml_dtypes.bfloat16), "select_dram": select.astype(ml_dtypes.bfloat16),
    }
    arrays = {k: np.ascontiguousarray(a) for k, a in arrays.items()}
    nc = bacc.Bacc("TRN2", target_bir_lowering=False, num_devices=1)
    args = [nc.dram_tensor(k, a.shape, mybir.dt.from_np(a.dtype), kind="ExternalInput").ap() for k, a in arrays.items()]
    out = nc.dram_tensor("out_dram", (BATCH, SEQ, HID), F32, kind="ExternalOutput").ap()
    build(nc, *args, out)
    r = run_bass_kernel_spmd(nc, [arrays], core_ids=[0])
    return r.results[0]["out_dram"]
```
